# Optimizing a Trainium2 kernel written in Bass

```python
import numpy as np
import jax
import jax.numpy as jnp

def _softmax(x, axis=-1):
    return jax.nn.softmax(x, axis=axis)

def _gelu(x):
    return jax.nn.gelu(x, approximate=True)

def _silu(x):
    return jax.nn.silu(x)

def _sigmoid(x):
    return jax.nn.sigmoid(x)

def _layernorm(x, axis=-1, eps=1e-05):
    m = jnp.mean(x, axis=axis, keepdims=True)
    v = jnp.var(x, axis=axis, keepdims=True)
    return (x - m) / jnp.sqrt(v + eps)

def _scatter_add(tgt, idx, src, axis=0):
    return tgt.at[idx].add(src)

def _segment_sum(src, seg, n):
    return jax.ops.segment_sum(src, seg, n)
kernel_name = 'mk_gnn_ffn_d2_gnn_r8_040431'

def setup_inputs(seed: int=0):
    np.random.seed(seed)
    _w = jnp.asarray

    def _rec_inputs():
        import jax
        import jax.numpy as jnp
        _gk = jax.random.key(seed)
        x = -0.0003713 + 1 * jax.random.normal(jax.random.fold_in(_gk, 1), (12500, 256), jnp.float32)
        src = jax.random.randint(jax.random.fold_in(_gk, 2), (200000,), 0, 12500, jnp.int32)
        dst = jnp.minimum((12500 * jax.random.uniform(jax.random.fold_in(_gk, 3), (200000,)) ** 2.0).astype(jnp.int32), 99999)
        _o = jnp.argsort(dst, stable=True)
        src = src[_o]
        dst = dst[_o]
        return (x, src, dst)
    x, src, dst = _rec_inputs()

    def _L0_gnn_setup():
        import jax, jax.numpy as jnp
        import numpy as np
        N, IN, H, C, OUT = (6250, 256, 4, 32, 256)
        E = 100000
        NEG_SLOPE = 0.2

        def _gat_project(x, edge_index, W, att_src, att_dst, bias, Wp, bp):
            n = x.shape[0]
            h_, c_ = att_src.shape
            loops = jnp.arange(n, dtype=edge_index.dtype)
            src = jnp.concatenate([edge_index[0], loops])
            dst = jnp.concatenate([edge_index[1], loops])
            h = (x @ W).reshape(n, h_, c_)
            a_src = jnp.einsum('nhc,hc->nh', h, att_src)
            a_dst = jnp.einsum('nhc,hc->nh', h, att_dst)
            e = jax.nn.leaky_relu(a_src[src] + a_dst[dst], NEG_SLOPE)
            m = jax.ops.segment_max(e, dst, num_segments=n)
            e = jnp.exp(e - m[dst])
            denom = jax.ops.segment_sum(e, dst, num_segments=n)
            alpha = e / (denom[dst] + 1e-16)
            msg = h[src] * alpha[:, :, None]
            out = jax.ops.segment_sum(msg, dst, num_segments=n)
            out = out.reshape(n, h_ * c_) + bias
            return out @ Wp + bp
        key = jax.random.key(seed)
        ks = jax.random.split(key, 8)
        x = jax.random.normal(ks[0], (N, IN), dtype=jnp.float32)
        edge_index = jax.random.randint(ks[1], (2, E), 0, N, dtype=jnp.int64)
        s = 1.0 / np.sqrt(IN)
        W = jax.random.uniform(ks[2], (IN, H * C), minval=-s, maxval=s, dtype=jnp.float32)
        att_src = jax.random.normal(ks[3], (H, C), dtype=jnp.float32) * s
        att_dst = jax.random.normal(ks[4], (H, C), dtype=jnp.float32) * s
        bias = jnp.zeros((H * C,), dtype=jnp.float32)
        sp = 1.0 / np.sqrt(H * C)
        Wp = jax.random.uniform(ks[5], (H * C, OUT), minval=-sp, maxval=sp, dtype=jnp.float32)
        bp = jax.random.uniform(ks[6], (OUT,), minval=-sp, maxval=sp, dtype=jnp.float32)
        return {'x': x, 'edge_index': edge_index, 'W': W, 'att_src': att_src, 'att_dst': att_dst, 'bias': bias, 'Wp': Wp, 'bp': bp}
    _L0_gnn_all = _L0_gnn_setup()
    _L0_gnn_in = {k: v for k, v in _L0_gnn_all.items() if k in ('W', 'att_src', 'att_dst', 'bias', 'Wp', 'bp')}
    del _L0_gnn_all

    def _L0_ffn_setup():
        import jax, jax.numpy as jnp
        import numpy as np
        DIM = 256
        H = 8
        D = 64
        G = 64
        INNER = H * D
        SCALE = D ** (-0.5)
        key = jax.random.key(seed)
        ks = jax.random.split(key, 12)
        B, N = (4, 2048)
        x = jax.random.normal(ks[0], (B, N, DIM), dtype=jnp.float32)
        s = lambda fan_in: 1.0 / np.sqrt(fan_in)
        W_fx = jax.random.normal(ks[1], (DIM, INNER), dtype=jnp.float32) * s(DIM)
        b_fx = jnp.zeros((INNER,), dtype=jnp.float32)
        W_x = jax.random.normal(ks[2], (DIM, INNER), dtype=jnp.float32) * s(DIM)
        b_x = jnp.zeros((INNER,), dtype=jnp.float32)
        A = jax.random.normal(ks[3], (G, D), dtype=jnp.float32)
        Q, _ = jnp.linalg.qr(A.T)
        W_slice = Q[:, :G].astype(jnp.float32)
        b_slice = jnp.zeros((G,), dtype=jnp.float32)
        W_q = jax.random.normal(ks[4], (D, D), dtype=jnp.float32) * s(D)
        W_k = jax.random.normal(ks[5], (D, D), dtype=jnp.float32) * s(D)
        W_v = jax.random.normal(ks[6], (D, D), dtype=jnp.float32) * s(D)
        W_out = jax.random.normal(ks[7], (INNER, DIM), dtype=jnp.float32) * s(INNER)
        b_out = jnp.zeros((DIM,), dtype=jnp.float32)
        temperature = jnp.ones((1, H, 1, 1), dtype=jnp.float32) * 0.5
        return {'x': x, 'W_fx': W_fx, 'b_fx': b_fx, 'W_x': W_x, 'b_x': b_x, 'W_slice': W_slice, 'b_slice': b_slice, 'W_q': W_q, 'W_k': W_k, 'W_v': W_v, 'W_out': W_out, 'b_out': b_out, 'temperature': temperature}
    _L0_ffn_all = _L0_ffn_setup()
    _L0_ffn_in = {k: v for k, v in _L0_ffn_all.items() if k in ('W_fx', 'b_fx', 'W_x', 'b_x', 'W_slice', 'b_slice', 'W_q', 'W_k', 'W_v', 'W_out', 'b_out', 'temperature')}
    del _L0_ffn_all

    def _L1_gnn_setup():
        import jax, jax.numpy as jnp
        import numpy as np
        N_NODES = 1250
        N_EDGES = 40000
        D_IN = 256
        D_OUT = 256
        MAX_NORM = 0.95

        def _expmap0(u):
            un = jnp.linalg.norm(u, axis=-1, keepdims=True)
            un_c = jnp.maximum(un, 1e-15)
            return jnp.tanh(un_c) * u / un_c
        key = jax.random.key(seed)
        ks = jax.random.split(key, 7)
        x = jax.random.normal(ks[0], (N_NODES, D_IN), dtype=jnp.float32)
        edge_index = jax.random.randint(ks[1], (2, N_EDGES), 0, N_NODES, dtype=jnp.int64)
        W = jax.random.normal(ks[2], (D_OUT, D_IN), dtype=jnp.float32) * (1.0 / np.sqrt(D_IN))
        b = jax.random.normal(ks[3], (D_OUT,), dtype=jnp.float32) * 0.02
        mag_w = jax.random.normal(ks[4], (1, D_IN), dtype=jnp.float32) * 0.02
        mag_b = jax.random.normal(ks[5], (1,), dtype=jnp.float32) * 0.02
        attn_w = jax.random.normal(ks[6], (1, 2 * D_OUT), dtype=jnp.float32) * (1.0 / np.sqrt(2 * D_OUT))
        return {'x': x, 'edge_index': edge_index, 'W': W, 'b': b, 'mag_w': mag_w, 'mag_b': mag_b, 'attn_w': attn_w}
    _L1_gnn_all = _L1_gnn_setup()
    _L1_gnn_in = {k: v for k, v in _L1_gnn_all.items() if k in ('W', 'b', 'mag_w', 'mag_b', 'attn_w')}
    del _L1_gnn_all

    def _L1_ffn_setup():
        import jax, jax.numpy as jnp
        import numpy as np
        D_MODEL = 256
        EXPERT_DIM = 512
        NUM_EXPERTS = 8
        TOP_K = 2
        SEQ_LEN = 256
        BATCH = 2
        key = jax.random.key(seed)
        ks = jax.random.split(key, 8)
        s = 0.02
        x = jax.random.normal(ks[0], (SEQ_LEN, BATCH, D_MODEL), dtype=jnp.float32)
        Wg = jax.random.normal(ks[1], (D_MODEL, NUM_EXPERTS), dtype=jnp.float32) * s
        bg = jax.random.normal(ks[2], (NUM_EXPERTS,), dtype=jnp.float32) * s
        bias = jnp.zeros((NUM_EXPERTS,), dtype=jnp.float32)
        W1 = jax.random.normal(ks[3], (NUM_EXPERTS, D_MODEL, EXPERT_DIM), dtype=jnp.float32) * s
        b1 = jax.random.normal(ks[4], (NUM_EXPERTS, EXPERT_DIM), dtype=jnp.float32) * s
        W2 = jax.random.normal(ks[5], (NUM_EXPERTS, EXPERT_DIM, D_MODEL), dtype=jnp.float32) * s
        b2 = jax.random.normal(ks[6], (NUM_EXPERTS, D_MODEL), dtype=jnp.float32) * s
        return {'x': x, 'Wg': Wg, 'bg': bg, 'bias': bias, 'W1': W1, 'b1': b1, 'W2': W2, 'b2': b2}
    _L1_ffn_all = _L1_ffn_setup()
    _L1_ffn_in = {k: v for k, v in _L1_ffn_all.items() if k in ('Wg', 'bg', 'bias', 'W1', 'b1', 'W2', 'b2')}
    del _L1_ffn_all
    return {'x': x, 'src': src, 'dst': dst, 'L0_gnn_W': _L0_gnn_in['W'], 'L0_gnn_att_src': _L0_gnn_in['att_src'], 'L0_gnn_att_dst': _L0_gnn_in['att_dst'], 'L0_gnn_bias': _L0_gnn_in['bias'], 'L0_gnn_Wp': _L0_gnn_in['Wp'], 'L0_gnn_bp': _L0_gnn_in['bp'], 'L0_ffn_W_fx': _L0_ffn_in['W_fx'], 'L0_ffn_b_fx': _L0_ffn_in['b_fx'], 'L0_ffn_W_x': _L0_ffn_in['W_x'], 'L0_ffn_b_x': _L0_ffn_in['b_x'], 'L0_ffn_W_slice': _L0_ffn_in['W_slice'], 'L0_ffn_b_slice': _L0_ffn_in['b_slice'], 'L0_ffn_W_q': _L0_ffn_in['W_q'], 'L0_ffn_W_k': _L0_ffn_in['W_k'], 'L0_ffn_W_v': _L0_ffn_in['W_v'], 'L0_ffn_W_out': _L0_ffn_in['W_out'], 'L0_ffn_b_out': _L0_ffn_in['b_out'], 'L0_ffn_temperature': _L0_ffn_in['temperature'], 'L1_gnn_W': _L1_gnn_in['W'], 'L1_gnn_b': _L1_gnn_in['b'], 'L1_gnn_mag_w': _L1_gnn_in['mag_w'], 'L1_gnn_mag_b': _L1_gnn_in['mag_b'], 'L1_gnn_attn_w': _L1_gnn_in['attn_w'], 'L1_ffn_Wg': _L1_ffn_in['Wg'], 'L1_ffn_bg': _L1_ffn_in['bg'], 'L1_ffn_bias': _L1_ffn_in['bias'], 'L1_ffn_W1': _L1_ffn_in['W1'], 'L1_ffn_b1': _L1_ffn_in['b1'], 'L1_ffn_W2': _L1_ffn_in['W2'], 'L1_ffn_b2': _L1_ffn_in['b2']}

def reference(x, src, dst, L0_gnn_W, L0_gnn_att_src, L0_gnn_att_dst, L0_gnn_bias, L0_gnn_Wp, L0_gnn_bp, L0_ffn_W_fx, L0_ffn_b_fx, L0_ffn_W_x, L0_ffn_b_x, L0_ffn_W_slice, L0_ffn_b_slice, L0_ffn_W_q, L0_ffn_W_k, L0_ffn_W_v, L0_ffn_W_out, L0_ffn_b_out, L0_ffn_temperature, L1_gnn_W, L1_gnn_b, L1_gnn_mag_w, L1_gnn_mag_b, L1_gnn_attn_w, L1_ffn_Wg, L1_ffn_bg, L1_ffn_bias, L1_ffn_W1, L1_ffn_b1, L1_ffn_W2, L1_ffn_b2):
    import jax
    import jax.numpy as jnp

    def _L0_gnn_ref(x, edge_index, W, att_src, att_dst, bias, Wp, bp):
        import jax, jax.numpy as jnp
        import numpy as np
        N, IN, H, C, OUT = (6250, 256, 4, 32, 256)
        E = 100000
        NEG_SLOPE = 0.2

        def _gat_project(x, edge_index, W, att_src, att_dst, bias, Wp, bp):
            n = x.shape[0]
            h_, c_ = att_src.shape
            loops = jnp.arange(n, dtype=edge_index.dtype)
            src = jnp.concatenate([edge_index[0], loops])
            dst = jnp.concatenate([edge_index[1], loops])
            h = (x @ W).reshape(n, h_, c_)
            a_src = jnp.einsum('nhc,hc->nh', h, att_src)
            a_dst = jnp.einsum('nhc,hc->nh', h, att_dst)
            e = jax.nn.leaky_relu(a_src[src] + a_dst[dst], NEG_SLOPE)
            m = jax.ops.segment_max(e, dst, num_segments=n)
            e = jnp.exp(e - m[dst])
            denom = jax.ops.segment_sum(e, dst, num_segments=n)
            alpha = e / (denom[dst] + 1e-16)
            msg = h[src] * alpha[:, :, None]
            out = jax.ops.segment_sum(msg, dst, num_segments=n)
            out = out.reshape(n, h_ * c_) + bias
            return out @ Wp + bp
        return _gat_project(x, edge_index, W, att_src, att_dst, bias, Wp, bp)

    def _L0_ffn_ref(x, W_fx, b_fx, W_x, b_x, W_slice, b_slice, W_q, W_k, W_v, W_out, b_out, temperature):
        import jax, jax.numpy as jnp
        import numpy as np
        DIM = 256
        H = 8
        D = 64
        G = 64
        INNER = H * D
        SCALE = D ** (-0.5)
        B, N, _ = x.shape
        fx_mid = (x @ W_fx + b_fx).reshape(B, N, H, D).transpose(0, 2, 1, 3)
        x_mid = (x @ W_x + b_x).reshape(B, N, H, D).transpose(0, 2, 1, 3)
        temp = jnp.clip(temperature, 0.1, 5.0)
        slice_weights = jax.nn.softmax((x_mid @ W_slice + b_slice) / temp, axis=-1)
        slice_norm = slice_weights.sum(axis=2)
        slice_token = jnp.einsum('bhnc,bhng->bhgc', fx_mid, slice_weights)
        slice_token = slice_token / (slice_norm[..., None] + 1e-05)
        q = slice_token @ W_q
        k = slice_token @ W_k
        v = slice_token @ W_v
        attn = jax.nn.softmax(jnp.einsum('bhgc,bhkc->bhgk', q, k) * SCALE, axis=-1)
        out_slice = jnp.einsum('bhgk,bhkc->bhgc', attn, v)
        out_x = jnp.einsum('bhgc,bhng->bhnc', out_slice, slice_weights)
        out_x = out_x.transpose(0, 2, 1, 3).reshape(B, N, INNER)
        return out_x @ W_out + b_out

    def _L1_gnn_ref(x, edge_index, W, b, mag_w, mag_b, attn_w):
        import jax, jax.numpy as jnp
        import numpy as np
        N_NODES = 1250
        N_EDGES = 40000
        D_IN = 256
        D_OUT = 256
        MAX_NORM = 0.95

        def _expmap0(u):
            un = jnp.linalg.norm(u, axis=-1, keepdims=True)
            un_c = jnp.maximum(un, 1e-15)
            return jnp.tanh(un_c) * u / un_c
        N = x.shape[0]
        F_out = W.shape[0]
        h_raw = x @ W.T + b
        h_dir = h_raw / jnp.maximum(jnp.linalg.norm(h_raw, axis=-1, keepdims=True), 1e-12)
        h_mag = jax.nn.sigmoid(x @ mag_w.T + mag_b) * 1.5
        h = h_dir * h_mag
        src, tgt = (edge_index[0], edge_index[1])
        h_src = h[src]
        h_tgt = h[tgt]
        a_s, a_t = (attn_w[0, :F_out], attn_w[0, F_out:])
        scores = h_src @ a_s + h_tgt @ a_t
        mx = jnp.maximum(jax.ops.segment_max(scores, tgt, num_segments=N), -1000000000.0)
        ex = jnp.exp(scores - mx[tgt])
        se = jax.ops.segment_sum(ex, tgt, num_segments=N)
        attn_weights = ex / (se[tgt] + 1e-10)
        agg = jax.ops.segment_sum(h_src * attn_weights[:, None], tgt, num_segments=N)
        h_combined = h + agg
        h_poincare = _expmap0(h_combined)
        norms = jnp.linalg.norm(h_poincare, axis=1, keepdims=True)
        return jnp.where(norms > MAX_NORM, h_poincare * (MAX_NORM / (norms + 1e-08)), h_poincare)

    def _L1_ffn_ref(x, Wg, bg, bias, W1, b1, W2, b2):
        import jax, jax.numpy as jnp
        import numpy as np
        D_MODEL = 256
        EXPERT_DIM = 512
        NUM_EXPERTS = 8
        TOP_K = 2
        SEQ_LEN = 256
        BATCH = 2
        x_flat = x.reshape(-1, D_MODEL)
        gate_logits = x_flat @ Wg + bg + bias
        topk_vals, topk_idx = jax.lax.top_k(gate_logits, TOP_K)
        topk_w = jax.nn.softmax(topk_vals, axis=-1)
        combine = (jax.nn.one_hot(topk_idx, NUM_EXPERTS, dtype=x.dtype) * topk_w[..., None]).sum(axis=1)
        h = jax.nn.relu(jnp.einsum('td,edh->teh', x_flat, W1) + b1)
        y = jnp.einsum('teh,ehd->ted', h, W2) + b2
        out = jnp.einsum('ted,te->td', y, combine)
        return out.reshape(x.shape)
    edge_index = jnp.stack([src, dst])
    x = x + _L0_gnn_ref(_layernorm(x, axis=-1), edge_index, L0_gnn_W, L0_gnn_att_src, L0_gnn_att_dst, L0_gnn_bias, L0_gnn_Wp, L0_gnn_bp)
    x = x + _L0_ffn_ref(_layernorm(x, axis=-1)[None], L0_ffn_W_fx, L0_ffn_b_fx, L0_ffn_W_x, L0_ffn_b_x, L0_ffn_W_slice, L0_ffn_b_slice, L0_ffn_W_q, L0_ffn_W_k, L0_ffn_W_v, L0_ffn_W_out, L0_ffn_b_out, L0_ffn_temperature)[0]
    x = x + _L1_gnn_ref(_layernorm(x, axis=-1), edge_index, L1_gnn_W, L1_gnn_b, L1_gnn_mag_w, L1_gnn_mag_b, L1_gnn_attn_w)
    x = x + _L1_ffn_ref(_layernorm(x, axis=-1)[None], L1_ffn_Wg, L1_ffn_bg, L1_ffn_bias, L1_ffn_W1, L1_ffn_b1, L1_ffn_W2, L1_ffn_b2)[0]
    return x

_drawn_inputs = setup_inputs


def setup_inputs(seed=0):
    import zlib

    import numpy as np

    out = dict(_drawn_inputs(seed))
    spreads = {'L0_gnn_bias': (0.0, 0.1),
     'L0_ffn_b_fx': (0.0, 0.1),
     'L0_ffn_b_x': (0.0, 0.8),
     'L0_ffn_b_slice': (0.0, 2.0),
     'L0_ffn_b_out': (0.0, 0.1),
     'L0_ffn_temperature': (0.5, 0.6),
     'L1_ffn_bias': (0.0, 0.1)}
    factors = {'L0_gnn_att_src': 2.808,
     'L0_gnn_att_dst': 8.0,
     'L0_ffn_W_x': 8.0,
     'L0_ffn_W_slice': 8.0,
     'L0_ffn_W_q': 8.0,
     'L0_ffn_W_k': 8.0,
     'L1_gnn_b': 36.98,
     'L1_gnn_mag_w': 8.0,
     'L1_gnn_attn_w': 55.355,
     'L1_ffn_bg': 4.277,
     'L1_ffn_b1': 8.0,
     'L1_ffn_b2': 3.992}
    for name, (base, spread) in spreads.items():
        noise = np.random.default_rng([zlib.crc32(name.encode()), seed]).standard_normal(out[name].shape)
        drawn = base * np.exp(spread * noise) if base else spread * noise
        out[name] = jnp.asarray(drawn.astype(out[name].dtype))
    for name, factor in factors.items():
        out[name] = (out[name] * factor).astype(out[name].dtype)
    return out
```

```python
from contextlib import ExitStack

import numpy as np
import concourse.bass as bass
from concourse import mybir

F32 = mybir.dt.float32
BF16 = mybir.dt.bfloat16
I32 = mybir.dt.int32
ALU = mybir.AluOpType
ACT = mybir.ActivationFunctionType
AX = mybir.AxisListType

P = 128
N = 12500
D = 256
E = 200000
NT = -(-N // P)
NPAD = NT * P
ET = -(-E // P)
G = 32
NG = 2 * (-(-(ET + NT - 1) // (2 * G)))
K = NG * G
KC = K // P
EPAD = K * P
T = 7
NB = NT // T
assert NB * T == NT and NB % 2 == 0 and KC * P == K
BIG = float(2 ** 100)
EPS = 1e-5
HEADS, HC = 4, 32
A_ROW = HEADS * HC + HEADS
A_ACC = A_ROW + HEADS
B_ROW = D + 2
B_ACC = D + 1
FH, FG = 8, 64
INNER = FH * FG
NX, FF = 8, 512


class Core:
    pass


def batches(eng):
    return eng.Fori(0, NB // 2)


def groups(eng):
    return eng.Fori(0, NG // 2)


def prime(eng, *events):
    for event in events:
        eng.sem_inc(event, 1)


def make_constants(nc, c, sb, sem):
    c.ident = sb("ident", [P, P])
    c.ramp_row = sb("ramp_row", [P, P])
    c.ramp_col = sb("ramp_col", [P, 1])
    c.minus_ramp = sb("minus_ramp", [P, 1])
    c.ones = sb("ones", [P, P])
    c.ones_bf = sb("ones_bf", [P, P], BF16)
    c.valid = sb("valid", [P, NT])
    c.eps = sb("eps", [P, 1])
    ints = sb("ramp_ints", [P, P + 1 + NT], I32)
    ramps_made, ramps_copied, constants_made = sem("ramps_made"), sem("ramps_copied"), sem("constants_made")
    with nc.Block() as block:
        @block.gpsimd
        def _(pool):
            nc.gpsimd.iota(ints[:, 0:P], [[1, P]], base=0, channel_multiplier=0)
            nc.gpsimd.iota(ints[:, P:P + 1], [[1, 1]], base=0, channel_multiplier=1)
            nc.gpsimd.iota(ints[:, P + 1:], [[P, NT]], base=0, channel_multiplier=1).then_inc(ramps_made, 1)

        @block.vector
        def _(dve):
            nc.vector.memset(c.ones[:, :], 1.0)
            nc.vector.memset(c.eps[:, :], EPS)
            nc.vector.memset(c.ones_bf[:, :], 1.0)
            dve.wait_ge(ramps_made, 1)
            nc.vector.tensor_copy(c.ramp_row[:, :], ints[:, 0:P])
            nc.vector.tensor_copy(c.ramp_col[:, :], ints[:, P:P + 1])
            nc.vector.tensor_copy(c.valid[:, :], ints[:, P + 1:]).then_inc(ramps_copied, 1)
            dve.wait_ge(ramps_copied, 1)
            nc.vector.tensor_scalar(c.minus_ramp[:, :], c.ramp_col[:, :], -1.0, None, ALU.mult)
            nc.vector.tensor_scalar(c.ident[:, :], c.ramp_row[:, :], c.ramp_col[:, 0:1], None, ALU.is_equal)
            nc.vector.tensor_scalar(c.valid[:, :], c.valid[:, :], float(N), None, ALU.is_lt).then_inc(constants_made, 1)
            dve.wait_ge(constants_made, 1)


def make_schedule(nc, c, src, dst, dram):
    flat = dram("dst_flat", [1, EPAD + 2], F32)
    c.keep_prev = dram("keep_prev", [K, P], F32)
    c.keep_next = dram("keep_next", [K, P], F32)
    c.local_rows = dram("local_rows", [1, EPAD], BF16)
    c.step_rows = dram("step_rows", [4, K], F32)
    c.step_tiles = dram("step_tiles", [1, K], I32)
    c.edge_src = dram("edge_src", [NG, P, G], I32)
    c.edge_place = dram("edge_place", [NG, P, G], F32)
    small, tiles = c.step_rows, c.step_tiles
    with ExitStack() as ctx:
        def sb(name, shape, dt=F32):
            return ctx.enter_context(nc.sbuf_tensor(name, shape, dt))

        def sem(name):
            return nc.alloc_semaphore(name)

        dst_in = sb("dst_in", [P, KC, P], I32)
        last = sb("last", [P, KC], I32)
        key = sb("key", [P, KC])
        step = sb("step", [P, KC])
        step_i = sb("step_i", [P, KC], I32)
        diag = sb("diag", [P, KC, P])
        keys = sb("keys", [P, K])
        below = sb("below", [P, K])
        t_f = sb("t_f", [P, KC])
        t_i = sb("t_i", [P, KC], I32)
        n_f = sb("n_f", [P, KC])
        n_i = sb("n_i", [P, KC], I32)
        n_p = sb("n_p", [P, KC])
        rows_i = sb("rows_i", [P, 2, KC, P], I32)
        dst_f = sb("dst_f", [P, KC, P])
        src_f = sb("src_f", [P, KC, P])
        local = sb("local", [P, KC, P])
        local_bf = sb("local_bf", [P, KC, P], BF16)
        near = sb("near", [P, 2, KC, P])
        one_seg = sb("one_seg", [P, KC])
        four = sb("four", [P, 4, KC])
        turned_src = sb("turned_src", [P, K], I32)
        turned_place = sb("turned_place", [P, K])
        margin = sb("margin", [1, 2])
        dst_loaded, ramp, told, dv = sem("dst_loaded"), sem("step_ramp"), sem("step_told"), sem("schedule_vector")
        keys_spread, rows_found, flat_stored, near_loaded = sem("keys_spread"), sem("rows_found"), sem("flat_stored"), sem("near_loaded")
        turned, all_stored, by_edge_stored = sem("turned"), sem("all_stored"), sem("by_edge_stored")
        with nc.Block() as block:
            @block.sync
            def _(sp):
                sp.dma_start(dst_in[:, :, :], dst.rearrange("(j p) e -> p j e", p=P)).then_inc(dst_loaded, 16)
                sp.wait_ge(dv, 7)
                sp.dma_start(flat[0, 1:1 + EPAD].rearrange("(j p e) -> p j e", p=P, e=P), dst_f[:, :, :]).then_inc(flat_stored, 16)
                sp.dma_start(flat[0:1, 0:1], margin[:, 0:1]).then_inc(flat_stored, 16)
                sp.dma_start(flat[0:1, EPAD + 1:EPAD + 2], margin[:, 1:2]).then_inc(flat_stored, 16)
                sp.wait_ge(flat_stored, 48)
                sp.dma_start(near[:, 0, :, :], flat[0, 0:EPAD].rearrange("(j p e) -> p j e", p=P, e=P)).then_inc(near_loaded, 16)
                sp.dma_start(near[:, 1, :, :], flat[0, 2:2 + EPAD].rearrange("(j p e) -> p j e", p=P, e=P)).then_inc(near_loaded, 16)
                sp.wait_ge(dv, 12)
                sp.dma_start(c.keep_prev.rearrange("(j p) e -> p j e", p=P), near[:, 0, :, :]).then_inc(all_stored, 16)
                sp.dma_start(c.keep_next.rearrange("(j p) e -> p j e", p=P), near[:, 1, :, :]).then_inc(all_stored, 16)
                sp.dma_start(c.local_rows[0, :].rearrange("(j p e) -> p j e", p=P, e=P), local_bf[:, :, :]).then_inc(all_stored, 16)
                sp.dma_start(tiles[0, :].rearrange("(j p one) -> p j one", p=P, one=1), n_i[:, :].rearrange("p (j one) -> p j one", one=1), allow_slow_non_contiguous=True).then_inc(all_stored, 16)
                for r in range(4):
                    sp.dma_start(small[r, :].rearrange("(j p one) -> p j one", p=P, one=1), four[:, r, :].rearrange("p (j one) -> p j one", one=1), allow_slow_non_contiguous=True).then_inc(all_stored, 16)
                sp.wait_ge(all_stored, 16 * 8)
                sp.wait_ge(dv, 13)
                sp.dma_start(c.edge_src.rearrange("g p s -> p g s"), turned_src[:, :].rearrange("p (g s) -> p g s", s=G)).then_inc(by_edge_stored, 16)
                sp.dma_start(c.edge_place.rearrange("g p s -> p g s"), turned_place[:, :].rearrange("p (g s) -> p g s", s=G)).then_inc(by_edge_stored, 16)
                sp.wait_ge(by_edge_stored, 32)

            @block.gpsimd
            def _(pool):
                nc.gpsimd.iota(step_i[:, :], [[P, KC]], base=0, channel_multiplier=1).then_inc(ramp, 1)
                pool.wait_ge(dv, 5)
                for j in range(KC):
                    for which, rows in ((0, src), (1, dst)):
                        nc.gpsimd.indirect_dma_start(rows_i[:, which, j, :], None, rows,
                                                     bass.IndirectOffsetOnAxis(ap=t_i[:, j:j + 1], axis=0)).then_inc(rows_found, 16)

            @block.tensor
            def _(pe):
                pe.wait_ge(dv, 3)
                for j in range(KC):
                    last_mm = nc.tensor.matmul(c.bank[j // 4][:, (j % 4) * P:(j % 4 + 1) * P], c.ones[:, :], diag[:, j, :], start=True, stop=True)
                last_mm.then_inc(keys_spread, 1)
                pe.wait_ge(dv, 9)
                for j in range(KC):
                    nc.tensor.transpose(c.bank[j // 4][:, (j % 4) * P:(j % 4 + 1) * P], local[:, j, :], c.ident[:, :])
                    last_mm = nc.tensor.transpose(c.bank[4 + j // 4][:, (j % 4) * P:(j % 4 + 1) * P], src_f[:, j, :], c.ident[:, :])
                last_mm.then_inc(turned, 1)

            @block.vector
            def _(dve):
                v = nc.vector
                v.memset(margin[:, 0:1], -5.0)
                v.memset(margin[:, 1:2], -7.0)
                dve.wait_ge(ramp, 1)
                v.tensor_copy(step[:, :], step_i[:, :])
                dve.wait_ge(dst_loaded, 16)
                v.tensor_scalar(last[:, :], dst_in[:, :, P - 1], 7, None, ALU.arith_shift_right).then_inc(dv, 1)
                dve.wait_ge(dv, 1)
                v.tensor_tensor(key[:, :], last[:, :], step[:, :], ALU.add).then_inc(dv, 1)
                dve.wait_ge(dv, 2)
                for j in range(KC):
                    op = v.tensor_scalar(diag[:, j, :], c.ident[:, :], key[:, j:j + 1], None, ALU.mult)
                op.then_inc(dv, 1)
                dve.wait_ge(keys_spread, 1)
                for b in range(-(-KC // 4)):
                    w = min(512, K - b * 512)
                    op = v.tensor_copy(keys[:, b * 512:b * 512 + w], c.bank[b][:, 0:w])
                op.then_inc(dv, 1)
                dve.wait_ge(dv, 4)
                for j in range(KC):
                    v.tensor_scalar(below[:, :], keys[:, :], step[:, j:j + 1], 0.0, ALU.is_lt, ALU.add, accum_out=t_f[:, j:j + 1]).then_inc(told, 1)
                    dve.wait_ge(told, j + 1)
                v.tensor_copy(t_i[:, :], t_f[:, :]).then_inc(dv, 1)
                v.tensor_tensor(n_f[:, :], step[:, :], t_f[:, :], ALU.subtract).then_inc(dv, 1)
                dve.wait_ge(dv, 6)
                v.tensor_copy(n_i[:, :], n_f[:, :])
                v.tensor_scalar(n_p[:, :], n_f[:, :], float(P), None, ALU.mult)
                dve.wait_ge(rows_found, 32 * KC)
                v.tensor_copy(dst_f[:, :, :], rows_i[:, 1, :, :]).then_inc(dv, 1)
                v.tensor_copy(src_f[:, :, :], rows_i[:, 0, :, :])
                dve.wait_ge(dv, 7)
                for j in range(KC):
                    op = v.tensor_scalar(local[:, j, :], dst_f[:, j, :], n_p[:, j:j + 1], -1.0, ALU.subtract, ALU.max)
                op.then_inc(dv, 1)
                dve.wait_ge(dv, 8)
                v.tensor_scalar(local[:, :, :], local[:, :, :], float(P), None, ALU.min).then_inc(dv, 1)
                dve.wait_ge(dv, 9)
                v.tensor_copy(local_bf[:, :, :], local[:, :, :])
                v.tensor_tensor(one_seg[:, :], dst_f[:, :, 0], dst_f[:, :, P - 1], ALU.is_equal)
                v.tensor_copy(four[:, 3, :], local[:, :, 0])
                dve.wait_ge(near_loaded, 32)
                for w in range(2):
                    op = v.tensor_tensor(near[:, w, :, :], near[:, w, :, :], dst_f[:, :, :], ALU.is_equal)
                op.then_inc(dv, 1)
                dve.wait_ge(dv, 10)
                v.tensor_copy(four[:, 2, :], near[:, 0, :, 0])
                v.tensor_tensor(four[:, 0, :], near[:, 0, :, 0], one_seg[:, :], ALU.mult)
                v.tensor_tensor(four[:, 1, :], near[:, 1, :, P - 1], one_seg[:, :], ALU.mult).then_inc(dv, 1)
                dve.wait_ge(dv, 11)
                v.tensor_scalar(near[:, :, :, :], near[:, :, :, :], 1.0, BIG, ALU.subtract, ALU.mult)
                v.tensor_scalar(four[:, 0:2, :], four[:, 0:2, :], 1.0, BIG, ALU.subtract, ALU.mult).then_inc(dv, 1)
                dve.wait_ge(turned, 1)
                for b in range(-(-KC // 4)):
                    w = min(512, K - b * 512)
                    v.tensor_copy(turned_place[:, b * 512:b * 512 + w], c.bank[b][:, 0:w])
                    op = v.tensor_copy(turned_src[:, b * 512:b * 512 + w], c.bank[4 + b][:, 0:w])
                op.then_inc(dv, 1)
                dve.wait_ge(dv, 13)


class Front:

    def __init__(self, nc, ctx, tag):
        def sb(name, shape, dt=F32):
            return ctx.enter_context(nc.sbuf_tensor(f"{name}_{tag}", shape, dt))

        def sem(name):
            return nc.alloc_semaphore(f"{name}_{tag}")

        self.x = sb("x", [P, 2, T, D])
        self.stats = sb("stats", [P, 2, T, 6])
        self.mv = sb("mv", [P, 2, T, 2])
        self.sd = sb("sd", [P, 2, T])
        self.rstd = sb("rstd", [P, 2, T])
        self.shift = sb("shift", [P, 2, T])
        self.xn = sb("xn", [P, T, D + 1])
        self.xt = sb("xt", [P, T, 2, P])
        self.loaded = [sem("x_loaded0"), sem("x_loaded1")]
        self.passed = sem("passed")
        self.stats_made, self.mv_made, self.sd_made = sem("stats_made"), sem("mv_made"), sem("sd_made")
        self.rstd_made, self.shift_made, self.xn_made = sem("rstd_made"), sem("shift_made"), sem("xn_made")
        self.turned, self.xt_made = sem("turned"), sem("xt_made")

    def load(self, sp, nc, x_dram, b, p):
        nc.sync.dma_start(self.x[:, p, :, :], x_dram.rearrange("(n p) d -> p n d", p=P)[:, bass.ds(b * T, T), :]).then_inc(self.loaded[p], 16)

    def sync(self, sp, nc, x_dram, used, store):
        for p in range(2):
            self.load(sp, nc, x_dram, p, p)
        with sp.Fori(0, NB // 2 - 1) as pair:
            for p in range(2):
                sp.wait_ge(used, 1 + (pair * 2 + p + 1) * T)
                sp.sem_inc(self.passed, 1)
                self.load(sp, nc, x_dram, pair * 2 + p + 2, p)
                store(pair * 2 + p, p)
        for p in range(2):
            store(NB - 2 + p, p)

    def vector(self, dve, nc, b, pair, p, update=None):
        dve.wait_ge(self.loaded[p], 16 * pair + 16)
        if update:
            update()
        for i in range(T):
            op = nc.vector.bn_stats(self.stats[:, p, i, :], self.x[:, p, i, :])
        op.then_inc(self.stats_made, 1)
        dve.wait_ge(self.stats_made, b + 1)
        dve.sem_inc(self.passed, 1)
        for i in range(T):
            op = nc.vector.bn_aggr(self.mv[:, p, i, :], self.stats[:, p, i, :])
        op.then_inc(self.mv_made, 1)
        dve.wait_ge(self.sd_made, b + 1)
        nc.vector.reciprocal(self.rstd[:, p, :], self.sd[:, p, :]).then_inc(self.rstd_made, 1)
        dve.wait_ge(self.rstd_made, b + 1)
        nc.vector.scalar_tensor_tensor(self.shift[:, p, :], self.mv[:, p, :, 0], -1.0, self.rstd[:, p, :], ALU.mult, ALU.mult).then_inc(self.shift_made, 1)

    def scalar(self, act, nc, c, b, p, used, also=None, more=0):
        act.wait_ge(self.mv_made, b + 1)
        nc.scalar.activation(self.sd[:, p, :], self.mv[:, p, :, 1], ACT.Sqrt, bias=c.eps[:, 0:1]).then_inc(self.sd_made, 1)
        act.wait_ge(self.shift_made, b + 1)
        act.wait_ge(used, 1 + b * T)
        for i in range(T + 1 + more):
            if i < T:
                nc.scalar.activation(self.xn[:, i, 0:D], self.x[:, p, i, :], ACT.Identity,
                                     bias=self.shift[:, p, i:i + 1], scale=self.rstd[:, p, i:i + 1]).then_inc(self.xn_made, 1)
            if 1 <= i <= T:
                act.wait_ge(self.turned, b * T + i)
                nc.scalar.copy(self.xt[:, i - 1, :, :].rearrange("p c n -> p (c n)"), c.bank[(i - 1) % 2][:, 0:D]).then_inc(self.xt_made, 1)
            if also:
                also(i)

    def tensor(self, pe, nc, c, b, i):
        pe.wait_ge(self.xn_made, b * T + i + 1)
        pe.wait_ge(self.xt_made, 1 + b * T + max(i - 1, 0))
        for h in range(2):
            op = nc.tensor.transpose(c.bank[i % 2][:, h * P:(h + 1) * P], self.xn[:, i, h * P:(h + 1) * P], c.ident[:, :])
        op.then_inc(self.turned, 1)


def gat_project(nc, c, w):
    with ExitStack() as ctx:
        def sb(name, shape, dt=F32):
            return ctx.enter_context(nc.sbuf_tensor(name, shape, dt))

        def sem(name):
            return nc.alloc_semaphore(name)

        HW = HEADS * HC
        w_ext = sb("w_ext", [P, 2, HW + 2 * HEADS])
        w_t = sb("w_t", [P, 2, P])
        att = sb("att", [P, 2])
        att_block = sb("att_block", [P, 2 * HEADS])
        head_of = sb("head_of", [P, HEADS])
        head_lo = sb("head_lo", [P, HEADS])
        rows = sb("rows", [P, 2, T, A_ROW])
        w_loaded, w_turned, block_made, w_copied, w_folded, w_ready = (sem(s) for s in ("gp_w_loaded", "gp_w_turned", "gp_block_made", "gp_w_copied", "gp_w_folded", "gp_w_ready"))
        projected, rows_copied, rows_stored0, rows_stored1 = sem("gp_projected"), sem("gp_rows_copied"), sem("gp_rows_stored0"), sem("gp_rows_stored1")
        rows_stored = [rows_stored0, rows_stored1]
        f = Front(nc, ctx, "gp")
        with nc.Block() as block:
            @block.sync
            def _(sp):
                sp.dma_start(w_ext[:, :, 0:HW], w["L0_gnn_W"].rearrange("(c p) n -> p c n", p=P)).then_inc(w_loaded, 16)
                sp.dma_start(att[:, 0:1], w["L0_gnn_att_src"].rearrange("h (c one) -> (h c) one", one=1)).then_inc(w_loaded, 16)
                sp.dma_start(att[:, 1:2], w["L0_gnn_att_dst"].rearrange("h (c one) -> (h c) one", one=1)).then_inc(w_loaded, 16)
                for p in range(2):
                    sp.sem_inc(rows_stored[p], 16)

                def store(b, p):
                    sp.wait_ge(rows_copied, 1 + (b + 1) * T)
                    sp.sem_inc(f.passed, 1)
                    nc.sync.dma_start(c.a_table.rearrange("(n p) d -> p n d", p=P)[:, bass.ds(b * T, T), :], rows[:, p, :, :]).then_inc(rows_stored[p], 16)

                f.sync(sp, nc, c.x_in, projected, store)
                for p in range(2):
                    sp.wait_ge(rows_stored[p], 16 + 16 * (NB // 2))

            @block.vector
            def _(dve):
                prime(dve, rows_copied)
                v = nc.vector
                v.tensor_scalar(head_of[:, :], c.ramp_row[:, 0:HEADS], float(HC), None, ALU.mult).then_inc(block_made, 1)
                dve.wait_ge(block_made, 1)
                v.tensor_scalar(head_lo[:, :], head_of[:, :], c.ramp_col[:, 0:1], None, ALU.is_le)
                v.tensor_scalar(head_of[:, :], head_of[:, :], float(HC), c.ramp_col[:, 0:1], ALU.add, ALU.is_gt).then_inc(block_made, 1)
                dve.wait_ge(block_made, 2)
                v.tensor_tensor(head_of[:, :], head_of[:, :], head_lo[:, :], ALU.mult).then_inc(block_made, 1)
                dve.wait_ge(block_made, 3)
                dve.wait_ge(w_loaded, 48)
                for s in range(2):
                    op = v.tensor_scalar(att_block[:, s * HEADS:(s + 1) * HEADS], head_of[:, :], att[:, s:s + 1], None, ALU.mult)
                op.then_inc(block_made, 1)
                dve.wait_ge(w_turned, 1)
                v.tensor_copy(w_t[:, :, :].rearrange("p c n -> p (c n)"), c.bank[2][:, 0:2 * P]).then_inc(w_copied, 1)
                dve.wait_ge(w_folded, 1)
                v.tensor_copy(w_ext[:, :, HW:], c.bank[3][:, 0:4 * HEADS].rearrange("p (c n) -> p c n", c=2)).then_inc(w_ready, 1)
                with batches(dve) as pair:
                    for p in range(2):
                        b = pair * 2 + p
                        f.vector(dve, nc, b, pair, p)
                        dve.wait_ge(rows_stored[p], 16 * pair + 16)
                        for i in range(T):
                            dve.wait_ge(projected, 1 + b * T + i + 1)
                            v.tensor_copy(rows[:, p, i, :], c.bank[2 + i % 2][:, 0:A_ROW])
                            op = v.tensor_copy(c.dst_score[:, bass.ds((b * T + i) * HEADS, HEADS)], c.bank[2 + i % 2][:, A_ROW:A_ROW + HEADS])
                            op.then_inc(rows_copied, 1)

            @block.scalar
            def _(act):
                prime(act, f.xt_made)
                with batches(act) as pair:
                    for p in range(2):
                        b = pair * 2 + p
                        f.scalar(act, nc, c, b, p, projected)

            @block.tensor
            def _(pe):
                prime(pe, projected)
                pe.wait_ge(w_loaded, 48)
                for ch in range(2):
                    op = nc.tensor.transpose(c.bank[2][:, ch * P:(ch + 1) * P], w_ext[:, ch, 0:HW], c.ident[:, :])
                op.then_inc(w_turned, 1)
                pe.wait_ge(w_copied, 1)
                pe.wait_ge(block_made, 4)
                for ch in range(2):
                    op = nc.tensor.matmul(c.bank[3][:, ch * 2 * HEADS:(ch + 1) * 2 * HEADS], w_t[:, ch, :], att_block[:, :], start=True, stop=True)
                op.then_inc(w_folded, 1)
                pe.wait_ge(w_ready, 1)
                with batches(pe) as pair:
                    for p in range(2):
                        b = pair * 2 + p
                        for i in range(T + 1):
                            if i < T:
                                f.tensor(pe, nc, c, b, i)
                            if i >= 1:
                                k = i - 1
                                pe.wait_ge(f.xt_made, 1 + b * T + i)
                                pe.wait_ge(rows_copied, 1 + b * T + max(k - 1, 0))
                                for ch in range(2):
                                    op = nc.tensor.matmul(c.bank[2 + k % 2][:, 0:HW + 2 * HEADS], f.xt[:, k, ch, :], w_ext[:, ch, :], start=(ch == 0), stop=(ch == 1))
                                op.then_inc(projected, 1)


def edge_stage(nc, c, tag, heads, leaky, table, row, width, score_at, floor, acc):
    H, Q = heads, 4
    HS = H * G
    multi = H > 1
    with ExitStack() as ctx:
        def sb(name, shape, dt=F32):
            return ctx.enter_context(nc.sbuf_tensor(f"{tag}_{name}", shape, dt))

        def sem(name):
            return nc.alloc_semaphore(f"{tag}_{name}")

        rows = sb("rows", [P, 2, G, row])
        src_now = sb("src_now", [P, 2, G], I32)
        keep_prev = sb("keep_prev", [HS, 2, P])
        keep_next = sb("keep_next", [HS, 2, P])
        place = sb("place", [P, 2, G])
        step_rows = sb("step_rows", [1, 2, 4, G])
        tile_now = sb("tile_now", [1, 2, G], I32)
        place_row = sb("place_row", [1, 2, G * P], BF16)
        away = sb("away", [P, 2, Q * P])
        node_of = sb("node_of", [P, 2, Q * P])
        z = sb("z", [P, HS])
        zt = sb("zt", [HS, P])
        zf = sb("zf", [HS, P])
        scan0 = sb("scan0", [HS, P])
        fwd = sb("fwd", [HS, P])
        scan1 = sb("scan1", [HS, P])
        top = sb("top", [HS, P])
        diff = sb("diff", [HS, P])
        ex = sb("ex", [HS, P])
        fm = sb("fm", [HS, P])
        ends = sb("ends", [HS, 2])
        pen_f = sb("pen_f", [1, H, G + 1])
        pen_b = sb("pen_b", [1, H, G + 1])
        in_f = sb("in_f", [1, H, G + 1])
        in_b = sb("in_b", [1, H, G + 1])
        out_f = sb("out_f", [1, H, G + 1])
        out_b = sb("out_b", [1, H, G + 1])
        start_f = sb("start_f", [1, HS])
        start_b = sb("start_b", [1, HS])
        drop = sb("drop", [1, H])
        first = sb("first", [1, P])
        dropped_by = sb("dropped_by", [P, H])
        scale = sb("scale", [P, H])
        weight = sb("weight", [P, 2 * H, G])
        hot = sb("hot", [P, 2, Q, P])
        msg = sb("msg", [P, 2, Q, width]) if multi else None
        gathered = [sem("gathered0"), sem("gathered1")]
        kept = [sem("kept0"), sem("kept1")]
        placed = [sem("placed0"), sem("placed1")]
        src_staged = [sem("src_staged0"), sem("src_staged1")]
        passed, passed_sp, passed_pe = sem("passed"), sem("passed_sp"), sem("passed_pe")
        place_spread, node_of_made, scored = sem("place_spread"), sem("node_of_made"), sem("scored")
        z_made, z_turned, zt_made, scan0_made, row_f, start_f_made, col_f, ends_f = (sem(s) for s in (
            "z_made", "z_turned", "zt_made", "scan0_made", "row_f", "start_f_made", "col_f", "ends_f"))
        fwd_made, scan1_made, row_b, start_b_made, col_b, ends_b, top_made, diff_made = (sem(s) for s in (
            "fwd_made", "scan1_made", "row_b", "start_b_made", "col_b", "ends_b", "top_made", "diff_made"))
        ex_made, fm_made, weight_turned, weight_made, dropped, scale_made = (sem(s) for s in (
            "ex_made", "fm_made", "weight_turned", "weight_made", "dropped", "scale_made"))
        in_f_made, out_f_made, in_b_made, out_b_made, diff0, rescaled = (sem(s) for s in (
            "in_f_made", "out_f_made", "in_b_made", "out_b_made", "diff0", "rescaled"))
        hot_made, msg_made, msg_w_made, summed, added = (sem(s) for s in ("hot_made", "msg_made", "msg_w_made", "summed", "added"))
        set_up, away_made = sem("set_up"), sem("away_made")

        spread_bank = [c.bank[0], c.bank[1]]
        s_bank, t_bank = c.bank[2], c.bank[3]
        ring = c.bank[4:8]
        w_cols, row_cols, col_cols = s_bank[:, P:P + 2 * HS], t_bank, t_bank


        def tiles_now(engine, p, k, count):
            return nc.values_load_multi_w_load_instructions(tile_now[0:1, p, k:k + count], engines=[engine], min_val=0, max_val=NT - 1)[1]

        with nc.Block() as block:
            @block.sync
            def _(sp):
                def load(g, p):
                    for h in range(H):
                        nc.sync.dma_start(keep_prev[h * G:(h + 1) * G, p, :], c.keep_prev[bass.ds(g * G, G), :]).then_inc(kept[p], 16)
                        nc.sync.dma_start(keep_next[h * G:(h + 1) * G, p, :], c.keep_next[bass.ds(g * G, G), :]).then_inc(kept[p], 16)
                    nc.sync.dma_start(src_now[:, p, :], c.edge_src[bass.ds(g, 1), :, :].rearrange("g p s -> (g p) s")).then_inc(src_staged[p], 16)
                    nc.sync.dma_start(place_row[:, p, :], c.local_rows[:, bass.ds(g * G * P, G * P)]).then_inc(placed[p], 16)
                    nc.sync.dma_start(place[:, p, :], c.edge_place[bass.ds(g, 1), :, :].rearrange("g p s -> (g p) s")).then_inc(placed[p], 16)
                    nc.sync.dma_start(tile_now[:, p, :], c.step_tiles[:, bass.ds(g * G, G)]).then_inc(placed[p], 16)
                    nc.sync.dma_start(step_rows[:, p, :, :], c.step_rows[:, bass.ds(g * G, G)].rearrange("(o r) k -> o r k", o=1)).then_inc(placed[p], 16)

                for p in range(2):
                    load(p, p)
                with sp.Fori(0, NG // 2 - 1) as pair:
                    for p in range(2):
                        g = pair * 2 + p
                        sp.wait_ge(added, 1 + (g + 1) * G)
                        sp.sem_inc(passed_sp, 1)
                        load(g + 2, p)

            @block.gpsimd
            def _(pool):
                def gather(p, n, used=None):
                    pool.wait_ge(src_staged[p], 16 * n + 16)
                    pool.sem_inc(passed, 1)
                    for s in range(G):
                        if used is not None and s % Q == 0:
                            pool.wait_ge(summed, 1 + used + s + Q)
                            pool.sem_inc(passed, 1)
                        nc.gpsimd.indirect_dma_start(rows[:, p, s, :], None, table,
                                                     bass.IndirectOffsetOnAxis(ap=src_now[:, p, s:s + 1], axis=0)).then_inc(gathered[p], 16)

                for p in range(2):
                    gather(p, 0)
                with pool.Fori(0, NG // 2 - 1) as pair:
                    for p in range(2):
                        gather(p, pair + 1, (pair * 2 + p) * G)

            @block.vector
            def _(dve):
                prime(dve, z_made, added, rescaled)
                v = nc.vector
                v.memset(pen_f[:, :, 0:1], -BIG)
                v.memset(pen_b[:, :, G:G + 1], -BIG)
                v.memset(in_b[:, :, G:G + 1], -BIG)
                v.memset(out_f[:, :, :], 0.0)
                v.memset(acc[:, :], 0.0).then_inc(set_up, 1)
                dve.wait_ge(set_up, 1)
                with groups(dve) as pair:
                    for p in range(2):
                        g = pair * 2 + p
                        dve.wait_ge(scored, (g + 1) * (G // Q))
                        dve.wait_ge(gathered[p], (pair + 1) * 16 * G)
                        dve.wait_ge(z_turned, 1 + g)
                        v.tensor_tensor(z[:, :].rearrange("e (h s) -> e s h", h=H), rows[:, p, :, score_at:score_at + H],
                                        s_bank[:, 0:HS].rearrange("e (s h) -> e s h", h=H), ALU.add).then_inc(z_made, 1)
                        if leaky:
                            dve.wait_ge(z_made, 1 + 2 * g + 1)
                            v.scalar_tensor_tensor(z[:, :], z[:, :], leaky, z[:, :], ALU.mult, ALU.max).then_inc(z_made, 1)
                        dve.wait_ge(placed[p], 64 * (pair + 1))
                        v.tensor_copy(pen_f[:, :, 1:], step_rows[:, p, 0:1, :].broadcast_to([1, H, G]))
                        v.tensor_copy(pen_b[:, :, 0:G], step_rows[:, p, 1:2, :].broadcast_to([1, H, G]))
                        v.tensor_copy(in_f[:, :, 0:1], out_f[:, :, G:G + 1])
                        v.tensor_scalar(first[:, :], c.ramp_row[0:1, :], step_rows[:, p, 3, 0:1], None, ALU.is_equal)
                        dve.wait_ge(z_turned, 1 + g + 1)
                        v.tensor_copy(zt[:, :], t_bank[0:HS, 0:P]).then_inc(zt_made, 1)
                        dve.wait_ge(zt_made, g + 1)
                        v.tensor_scalar(zf[:, :], zt[:, :], floor, None, ALU.max).then_inc(diff0, 1)
                        dve.wait_ge(kept[p], (pair + 1) * 32 * H)
                        dve.wait_ge(diff0, 3 * g + 1)
                        v.tensor_tensor_scan(scan0[:, :], keep_prev[:, p, :], zf[:, :], -BIG, ALU.add, ALU.max).then_inc(scan0_made, 1)
                        dve.wait_ge(row_f, g + 1)
                        v.tensor_copy(in_f[:, :, 1:], t_bank[0:1, P:P + HS].rearrange("o (h s) -> o h s", h=H)).then_inc(in_f_made, 1)
                        dve.wait_ge(in_f_made, g + 1)
                        v.tensor_tensor_scan(out_f[:, :, :].rearrange("o h s -> o (h s)"), pen_f[:, :, :].rearrange("o h s -> o (h s)"),
                                             in_f[:, :, :].rearrange("o h s -> o (h s)"), -BIG, ALU.add, ALU.max).then_inc(out_f_made, 1)
                        dve.wait_ge(out_f_made, g + 1)
                        v.tensor_copy(start_f[:, :].rearrange("o (h s) -> o h s", h=H), out_f[:, :, 0:G]).then_inc(start_f_made, 1)
                        dve.wait_ge(col_f, g + 1)
                        v.tensor_copy(ends[:, 0:1], t_bank[0:HS, 2 * P:2 * P + 1]).then_inc(ends_f, 1)
                        dve.wait_ge(ends_f, g + 1)
                        v.tensor_tensor_scan(fwd[:, :], keep_prev[:, p, :], zf[:, :], ends[:, 0:1], ALU.add, ALU.max).then_inc(fwd_made, 1)
                        dve.wait_ge(fwd_made, g + 1)
                        v.tensor_tensor_scan(scan1[:, ::-1], keep_next[:, p, ::-1], fwd[:, ::-1], -BIG, ALU.add, ALU.max).then_inc(scan1_made, 1)
                        dve.wait_ge(row_b, g + 1)
                        v.tensor_copy(in_b[:, :, 0:G], t_bank[0:1, P:P + HS].rearrange("o (h s) -> o h s", h=H)).then_inc(in_b_made, 1)
                        dve.wait_ge(in_b_made, g + 1)
                        v.tensor_tensor_scan(out_b[:, :, :].rearrange("o h s -> o (h s)")[:, ::-1], pen_b[:, :, :].rearrange("o h s -> o (h s)")[:, ::-1],
                                             in_b[:, :, :].rearrange("o h s -> o (h s)")[:, ::-1], -BIG, ALU.add, ALU.max).then_inc(out_b_made, 1)
                        dve.wait_ge(out_b_made, g + 1)
                        v.tensor_tensor(drop[:, :], out_f[:, :, 0], out_b[:, :, 0], ALU.subtract).then_inc(diff0, 1)
                        v.tensor_copy(start_b[:, :].rearrange("o (h s) -> o h s", h=H), out_b[:, :, 1:]).then_inc(start_b_made, 1)
                        dve.wait_ge(diff0, 3 * g + 2)
                        v.tensor_scalar(drop[:, :], drop[:, :], step_rows[:, p, 2, 0:1], None, ALU.mult).then_inc(dropped, 1)
                        dve.wait_ge(col_b, g + 1)
                        v.tensor_copy(dropped_by[:, :], t_bank[:, 2 * P + 4:2 * P + 4 + H])
                        v.tensor_copy(ends[:, 1:2], t_bank[0:HS, 2 * P + 2:2 * P + 3]).then_inc(ends_b, 1)
                        dve.wait_ge(ends_b, g + 1)
                        v.tensor_tensor_scan(top[:, ::-1], keep_next[:, p, ::-1], fwd[:, ::-1], ends[:, 1:2], ALU.add, ALU.max).then_inc(top_made, 1)
                        dve.wait_ge(top_made, g + 1)
                        v.tensor_tensor(diff[:, :], zt[:, :], top[:, :], ALU.subtract).then_inc(diff_made, 1)
                        if multi:
                            v.scalar_tensor_tensor(fm[:, :], keep_prev[:, p, :], -1.0 / BIG, top[:, :], ALU.mult, ALU.mult).then_inc(fm_made, 1)
                        v.sem_inc(diff0, 1)
                        n = tiles_now(mybir.EngineType.DVE, p, 0, 1)[0]
                        dve.wait_ge(scale_made, g + 1)
                        dve.wait_ge(added, 1 + g * G)
                        if multi:
                            cols = acc[:, bass.ds(n * width, HEADS * HC)].rearrange("p (h c) -> p h c", h=H)
                            v.tensor_tensor(cols, cols, scale[:, :].rearrange("p (h o) -> p h o", o=1).broadcast_to([P, H, HC]), ALU.mult)
                            v.tensor_tensor(acc[:, bass.ds(n * width + HEADS * HC, H)], acc[:, bass.ds(n * width + HEADS * HC, H)], scale[:, :], ALU.mult)
                            v.tensor_tensor(acc[:, bass.ds(n * width + A_ROW, H)], acc[:, bass.ds(n * width + A_ROW, H)],
                                            dropped_by[:, :], ALU.subtract).then_inc(rescaled, 1)
                        else:
                            v.tensor_scalar(acc[:, bass.ds(n * width, width)], acc[:, bass.ds(n * width, width)], scale[:, 0:1], None, ALU.mult).then_inc(rescaled, 1)
                        dve.wait_ge(weight_made, g + 1)

                        def prepare(q, s):
                            k = q * Q + s
                            if multi:
                                one_hot = v.tensor_scalar(hot[:, q % 2, s, :], c.ramp_row[:, :], place[:, p, k:k + 1], None, ALU.is_equal)
                                message = v.tensor_tensor(msg[:, q % 2, s, 0:HEADS * HC].rearrange("p (h c) -> p h c", h=H),
                                                          rows[:, p, k, 0:HEADS * HC].rearrange("p (h c) -> p h c", h=H),
                                                          weight[:, 0:H, k:k + 1].broadcast_to([P, H, HC]), ALU.mult)
                            else:
                                one_hot = v.tensor_scalar(hot[:, q % 2, s, :], c.ramp_row[:, :], place[:, p, k:k + 1], weight[:, 0, k:k + 1], ALU.is_equal, ALU.mult)
                            if s == Q - 1:
                                one_hot.then_inc(hot_made, 1)
                                if multi:
                                    message.then_inc(msg_made, 1)

                        for q in range(2):
                            for s in range(Q):
                                prepare(q, s)
                        for q in range(G // Q):
                            node_tile = tiles_now(mybir.EngineType.DVE, p, q * Q, Q)
                            for s in range(Q):
                                k, n = q * Q + s, node_tile[s]
                                dve.wait_ge(added, 1 + g * G + k) if k else dve.wait_ge(rescaled, 1 + g + 1)
                                dve.wait_ge(summed, 1 + g * G + k + 1)
                                v.tensor_tensor(acc[:, bass.ds(n * width, width)], acc[:, bass.ds(n * width, width)], ring[s][:, 0:width], ALU.add).then_inc(added, 1)
                                if q + 2 < G // Q:
                                    prepare(q + 2, s)

            @block.scalar
            def _(act):
                prime(act, node_of_made)

                def node_one_hots(g, q):
                    act.wait_ge(place_spread, g * (G // Q) + q + 1)
                    nc.scalar.activation(away[:, q % 2, :], spread_bank[q % 2][:, :], ACT.Abs, bias=c.minus_ramp[:, 0:1]).then_inc(away_made, 1)
                    act.wait_ge(away_made, g * (G // Q) + q + 1)
                    nc.scalar.activation(node_of[:, q % 2, :], away[:, q % 2, :], ACT.Relu, bias=c.ones[:, 0:1], scale=-1.0).then_inc(node_of_made, 1)

                def group(g, p, more):
                    act.wait_ge(ends_b, g + 1)
                    act.wait_ge(rescaled, 1 + g)
                    nc.scalar.activation(scale[:, :], dropped_by[:, :], ACT.Exp).then_inc(scale_made, 1)
                    act.wait_ge(diff_made, g + 1)
                    act.wait_ge(weight_turned, 1 + g)
                    nc.scalar.activation(ex[:, :], diff[:, :], ACT.Exp).then_inc(ex_made, 1)
                    act.wait_ge(weight_turned, 1 + g + 1)
                    act.wait_ge(summed, 1 + g * G)
                    nc.scalar.copy(weight[:, 0:(2 * H if multi else H), :].rearrange("e h s -> e (h s)"), s_bank[:, P:P + (2 * HS if multi else HS)]).then_inc(weight_made, 1)
                    act.wait_ge(weight_made, g + 1)
                    for q in range(G // Q):
                        if multi:
                            act.wait_ge(summed, 1 + g * G + max(Q * (q - 1), 0))
                            nc.scalar.copy(msg[:, q % 2, :, HEADS * HC:].rearrange("p s h -> p h s"), weight[:, :, q * Q:(q + 1) * Q]).then_inc(msg_w_made, 1)
                        if more:
                            node_one_hots(g + 1, q)

                for q in range(G // Q):
                    node_one_hots(0, q)
                with act.Fori(0, NG // 2 - 1) as pair:
                    for p in range(2):
                        group(pair * 2 + p, p, True)
                for p in range(2):
                    group(NG - 2 + p, p, p == 0)

            @block.tensor
            def _(pe):
                prime(pe, z_turned, summed, weight_turned)

                def score_quad(g, q, p):
                    if q < G // Q:
                        pe.wait_ge(node_of_made, 1 + g * (G // Q) + max(q - 1, 0))
                        nc.tensor.matmul(spread_bank[q % 2][:, :], c.ones_bf[0:1, :], place_row[:, p, q * Q * P:(q + 1) * Q * P], start=True, stop=True).then_inc(place_spread, 1)
                    if q >= 1:
                        node_tile = tiles_now(mybir.EngineType.PE, p, (q - 1) * Q, Q)
                        pe.wait_ge(node_of_made, 1 + g * (G // Q) + q)
                        for s in range(Q):
                            k, n = (q - 1) * Q + s, node_tile[s]
                            op = nc.tensor.matmul(s_bank[:, k * H:(k + 1) * H], node_of[:, (q - 1) % 2, s * P:(s + 1) * P],
                                                  c.dst_score[:, bass.ds(n * H, H)], start=True, stop=True)
                        op.then_inc(scored, 1)

                def group(g, p, more, next_placed):
                    pe.wait_ge(z_made, 1 + (2 if leaky else 1) * (g + 1))
                    pe.wait_ge(rescaled, 1 + g)
                    nc.tensor.transpose(t_bank[0:HS, 0:P], z[:, :], c.ident[:, :]).then_inc(z_turned, 1)
                    pe.wait_ge(scan0_made, g + 1)
                    pe.sem_inc(passed_pe, 1)
                    nc.tensor.transpose(t_bank[0:1, P:P + HS], scan0[:, P - 1:P], c.ident[0:HS, 0:HS]).then_inc(row_f, 1)
                    pe.wait_ge(start_f_made, g + 1)
                    pe.sem_inc(passed_pe, 1)
                    nc.tensor.matmul(t_bank[0:HS, 2 * P:2 * P + 1], start_f[:, :], c.ones[0:1, 0:1], start=True, stop=True).then_inc(col_f, 1)
                    pe.wait_ge(scan1_made, g + 1)
                    pe.sem_inc(passed_pe, 1)
                    nc.tensor.transpose(t_bank[0:1, P:P + HS], scan1[:, 0:1], c.ident[0:HS, 0:HS]).then_inc(row_b, 1)
                    pe.wait_ge(start_b_made, g + 1)
                    pe.wait_ge(dropped, g + 1)
                    pe.sem_inc(passed_pe, 1)
                    nc.tensor.matmul(t_bank[0:HS, 2 * P + 2:2 * P + 3], start_b[:, :], c.ones[0:1, 0:1], start=True, stop=True)
                    nc.tensor.matmul(t_bank[:, 2 * P + 4:2 * P + 4 + H], first[:, :], drop[:, :], start=True, stop=True).then_inc(col_b, 1)
                    pe.wait_ge(ex_made, g + 1)
                    pe.sem_inc(passed_pe, 1)
                    op = nc.tensor.transpose(s_bank[:, P:P + HS], ex[:, :], c.ident[0:HS, 0:HS])
                    if multi:
                        pe.wait_ge(fm_made, g + 1)
                        pe.sem_inc(passed_pe, 1)
                        op = nc.tensor.transpose(s_bank[:, P + HS:P + 2 * HS], fm[:, :], c.ident[0:HS, 0:HS])
                    op.then_inc(weight_turned, 1)
                    if more:
                        pe.wait_ge(placed[1 - p], next_placed)
                        pe.sem_inc(passed_pe, 1)
                    for k in range(G):
                        if k % Q == 0:
                            pe.wait_ge(hot_made, g * (G // Q) + k // Q + 1)
                            if multi:
                                pe.wait_ge(msg_made, g * (G // Q) + k // Q + 1)
                                pe.wait_ge(msg_w_made, g * (G // Q) + k // Q + 1)
                        if k >= Q:
                            pe.wait_ge(added, 1 + g * G + k - Q + 1)
                        else:
                            pe.wait_ge(added, 1 + g * G)
                        rhs = msg[:, k // Q % 2, k % Q, :] if multi else rows[:, p, k, 0:width]
                        nc.tensor.matmul(ring[k % Q][:, 0:width], hot[:, k // Q % 2, k % Q, :], rhs, start=True, stop=True).then_inc(summed, 1)
                        if more and k % Q == Q - 1:
                            score_quad(g + 1, k // Q, 1 - p)
                    if more:
                        score_quad(g + 1, G // Q, 1 - p)

                pe.wait_ge(placed[0], 64)
                for q in range(G // Q + 1):
                    score_quad(0, q, 0)
                with pe.Fori(0, NG // 2 - 1) as pair:
                    group(pair * 2, 0, True, 64 * (pair + 1))
                    group(pair * 2 + 1, 1, True, 64 * (pair + 2))
                group(NG - 2, 0, True, 32 * NG)
                group(NG - 1, 1, False, None)


def spread_row(w_row, n):
    return w_row.rearrange("(one n) -> one n", one=1).broadcast_to([P, n])


def tiles_of(dram_ap, b):
    return dram_ap.rearrange("(n p) d -> p n d", p=P)[:, bass.ds(b * T, T), :]


def gat_finish(nc, c, w, acc):
    with ExitStack() as ctx:
        def sb(name, shape, dt=F32):
            return ctx.enter_context(nc.sbuf_tensor(f"gf_{name}", shape, dt))

        def sem(name):
            return nc.alloc_semaphore(f"gf_{name}")

        HW = HEADS * HC
        x = sb("x", [P, 2, T, D])
        h = sb("h", [P, 2, T, A_ROW])
        x_new = sb("x_new", [P, 2, T, D])
        wp = sb("wp", [P, D])
        bias = sb("bias", [P, HW])
        bp = sb("bp", [P, D])
        own = sb("own", [P, T, HEADS])
        top = sb("top", [P, T, HEADS])
        both = sb("both", [P, T, HEADS])
        gap = sb("gap", [P, 2, T, HEADS])
        factor = sb("factor", [P, 2, T, HEADS])
        den = sb("den", [P, T, HEADS])
        part = sb("part", [P, T, HW])
        o = sb("o", [P, T, HW])
        ot = sb("ot", [P, T, HW])
        loaded = [sem("loaded0"), sem("loaded1")]
        stored = [sem("stored0"), sem("stored1")]
        w_loaded, dv, gap_made, factor_made, o_made, turned, ot_made, projected, added, x_made = (sem(s) for s in (
            "w_loaded", "dv", "gap_made", "factor_made", "o_made", "turned", "ot_made", "projected", "added", "x_made"))
        V = 8
        passed = nc.alloc_semaphore("passed")
        with nc.Block() as block:
            @block.sync
            def _(sp):
                sp.dma_start(wp[:, :], w["L0_gnn_Wp"]).then_inc(w_loaded, 16)
                sp.dma_start(bias[:, :], spread_row(w["L0_gnn_bias"], HW)).then_inc(w_loaded, 16)
                sp.dma_start(bp[:, :], spread_row(w["L0_gnn_bp"], D)).then_inc(w_loaded, 16)
                for p in range(2):
                    sp.sem_inc(stored[p], 16)

                def load(b, p):
                    nc.sync.dma_start(x[:, p, :, :], tiles_of(c.x_in, b)).then_inc(loaded[p], 16)
                    nc.sync.dma_start(h[:, p, :, :], tiles_of(c.a_table, b)).then_inc(loaded[p], 16)

                def store(b, p):
                    sp.wait_ge(x_made, b + 1)
                    sp.sem_inc(passed, 1)
                    nc.sync.dma_start(tiles_of(c.x1, b), x_new[:, p, :, :]).then_inc(stored[p], 16)

                for p in range(2):
                    load(p, p)
                with sp.Fori(0, NB // 2 - 1) as pair:
                    for p in range(2):
                        b = pair * 2 + p
                        store(b, p)
                        load(b + 2, p)
                for p in range(2):
                    store(NB - 2 + p, p)
                for p in range(2):
                    sp.wait_ge(stored[p], 16 + 16 * (NB // 2))

            @block.vector
            def _(dve):
                prime(dve, added)
                v = nc.vector
                dve.wait_ge(w_loaded, 48)
                with batches(dve) as pair:
                    for p in range(2):
                        b = pair * 2 + p
                        sums = acc[:, bass.ds(b * T * A_ACC, T * A_ACC)].rearrange("p (t k) -> p t k", t=T)
                        score = c.dst_score[:, bass.ds(b * T * HEADS, T * HEADS)].rearrange("p (t k) -> p t k", t=T)
                        dve.wait_ge(loaded[p], 32 * pair + 32)

                        def chain(op, n):
                            op.then_inc(dv, 1)
                            dve.wait_ge(dv, b * V + n)

                        v.tensor_tensor(own[:, :, :], h[:, p, :, HW:A_ROW], score, ALU.add)
                        chain(v.tensor_scalar(top[:, :, :], sums[:, :, HW:A_ROW], 0.0, -BIG, ALU.is_equal, ALU.mult), 1)
                        v.scalar_tensor_tensor(own[:, :, :], own[:, :, :], 0.2, own[:, :, :], ALU.mult, ALU.max)
                        chain(v.tensor_tensor(top[:, :, :], top[:, :, :], sums[:, :, A_ROW:A_ACC], ALU.add), 2)
                        chain(v.tensor_tensor(both[:, :, :], top[:, :, :], own[:, :, :], ALU.max), 3)
                        v.tensor_tensor(gap[:, 0, :, :], top[:, :, :], both[:, :, :], ALU.subtract)
                        v.tensor_tensor(gap[:, 1, :, :], own[:, :, :], both[:, :, :], ALU.subtract).then_inc(gap_made, 1)
                        dve.wait_ge(factor_made, b + 1)
                        o4 = o[:, :, :].rearrange("p t (h c) -> p t h c", h=HEADS)
                        part4 = part[:, :, :].rearrange("p t (h c) -> p t h c", h=HEADS)

                        def wide(ap, i):
                            return ap[:, i, :].rearrange("p (h one) -> p h one", one=1).broadcast_to([P, HEADS, HC])

                        dve.wait_ge(turned, 1 + b * T)
                        for i in range(T):
                            v.tensor_tensor(o4[:, i, :, :], sums[:, i, 0:HW].rearrange("p (h c) -> p h c", h=HEADS), wide(factor[:, 0], i), ALU.mult)
                            v.tensor_tensor(part4[:, i, :, :], h[:, p, i, 0:HW].rearrange("p (h c) -> p h c", h=HEADS), wide(factor[:, 1], i), ALU.mult)
                        chain(v.tensor_tensor(den[:, :, :], sums[:, :, HW:A_ROW], factor[:, 0, :, :], ALU.mult), 4)
                        chain(v.tensor_tensor(den[:, :, :], den[:, :, :], factor[:, 1, :, :], ALU.add), 5)
                        v.tensor_tensor(o[:, :, :], o[:, :, :], part[:, :, :], ALU.add)
                        chain(v.tensor_scalar(den[:, :, :], den[:, :, :], 1e-16, None, ALU.add), 6)
                        chain(v.reciprocal(den[:, :, :], den[:, :, :]), 7)
                        for i in range(T):
                            op = v.tensor_tensor(o4[:, i, :, :], o4[:, i, :, :], wide(den, i), ALU.mult)
                        chain(op, 8)
                        for i in range(T):
                            v.tensor_tensor(o[:, i, :], o[:, i, :], bias[:, :], ALU.add).then_inc(o_made, 1)
                        dve.wait_ge(stored[p], 16 * pair + 16)
                        for i in range(T):
                            dve.wait_ge(projected, 1 + b * T + i + 1)
                            op = v.tensor_tensor(x_new[:, p, i, :], c.bank[2 + i % 2][:, 0:D], x[:, p, i, :], ALU.add)
                            op.then_inc(added, 1)
                        dve.wait_ge(added, 1 + (b + 1) * T)
                        for i in range(T):
                            op = v.tensor_tensor(x_new[:, p, i, :], x_new[:, p, i, :], bp[:, :], ALU.add)
                        op.then_inc(x_made, 1)

            @block.scalar
            def _(act):
                prime(act, ot_made)
                with batches(act) as pair:
                    for p in range(2):
                        b = pair * 2 + p
                        act.wait_ge(gap_made, b + 1)
                        nc.scalar.activation(factor[:, :, :, :], gap[:, :, :, :], ACT.Exp).then_inc(factor_made, 1)
                        act.wait_ge(projected, 1 + b * T)
                        for i in range(T):
                            act.wait_ge(turned, 1 + b * T + i + 1)
                            nc.scalar.copy(ot[:, i, :], c.bank[i % 2][:, 0:HW]).then_inc(ot_made, 1)

            @block.tensor
            def _(pe):
                prime(pe, turned, projected)
                pe.wait_ge(w_loaded, 48)
                with batches(pe) as pair:
                    for p in range(2):
                        b = pair * 2 + p
                        for i in range(T + 1):
                            if i < T:
                                pe.wait_ge(o_made, b * T + i + 1)
                                pe.wait_ge(ot_made, 1 + b * T + max(i - 1, 0))
                                nc.tensor.transpose(c.bank[i % 2][:, 0:HW], o[:, i, :], c.ident[:, :]).then_inc(turned, 1)
                            if i >= 1:
                                k = i - 1
                                pe.wait_ge(ot_made, 1 + b * T + i)
                                pe.wait_ge(added, 1 + b * T + max(k - 1, 0))
                                nc.tensor.matmul(c.bank[2 + k % 2][:, 0:D], ot[:, k, :], wp[:, :], start=True, stop=True).then_inc(projected, 1)


def slice_tokens(nc, c, w, pooled_out):
    with ExitStack() as ctx:
        def sb(name, shape, dt=F32):
            return ctx.enter_context(nc.sbuf_tensor(f"st_{name}", shape, dt))

        def sem(name):
            return nc.alloc_semaphore(f"st_{name}")

        NBK = INNER // P
        f = Front(nc, ctx, "st")
        wx = sb("wx", [P, 2, INNER])
        wx_t = sb("wx_t", [P, NBK, D])
        pair_slice = sb("pair_slice", [P, P])
        bx = sb("bx", [P, NBK])
        rows = sb("rows", [1, 4, INNER])
        temp = sb("temp", [1, FH])
        wc = sb("wc", [P, 2, INNER])
        inv_temp = sb("inv_temp", [P, INNER])
        brow = sb("brow", [P, INNER])
        lg = sb("lg", [P, 2, INNER])
        mx = sb("mx", [P, 2, FH])
        e = sb("e", [P, 2, INNER])
        total = sb("total", [P, 2, FH])
        inv = sb("inv", [P, 2, FH])
        sw = sb("sw", [P, 2, INNER])
        swt = sb("swt", [P, 2, T, INNER])
        zeros = sb("zeros", [P, P])
        zero_rows = sb("zero_rows", [P, D + 1])
        stored = [sem("stored0"), sem("stored1")]
        w_loaded, dv, pe_prep, logits, lg_made, mx_made, sub_made, e_made, total_made, inv_made, inv_masked, sw_made, pooled, sw_turned, swt_made = (sem(s) for s in (
            "w_loaded", "dv", "pe_prep", "logits", "lg_made", "mx_made", "sub_made", "e_made", "total_made", "inv_made", "inv_masked", "sw_made", "pooled", "sw_turned", "swt_made"))
        with nc.Block() as block:
            @block.sync
            def _(sp):
                sp.wait_ge(dv, 1)
                sp.dma_start(wx[:, :, :], w["L0_ffn_W_x"].rearrange("(c p) n -> p c n", p=P)).then_inc(w_loaded, 16)
                for h in range(2):
                    sp.dma_start(pair_slice[h * FG:(h + 1) * FG, h * FG:(h + 1) * FG], w["L0_ffn_W_slice"]).then_inc(w_loaded, 16)
                sp.dma_start(bx[:, :], w["L0_ffn_b_x"].rearrange("(k p) -> p k", p=P), allow_slow_non_contiguous=True).then_inc(w_loaded, 16)
                for h in range(FH):
                    sp.dma_start(rows[:, 1, h * FG:(h + 1) * FG], w["L0_ffn_b_slice"].rearrange("(one n) -> one n", one=1)).then_inc(w_loaded, 16)
                sp.dma_start(temp[:, :], w["L0_ffn_temperature"].rearrange("a h b c -> (a b c) h")).then_inc(w_loaded, 16)
                for p in range(2):
                    sp.sem_inc(stored[p], 16)

                def store(b, p):
                    sp.wait_ge(swt_made, 1 + (b + 1) * T)
                    sp.sem_inc(f.passed, 1)
                    nc.sync.dma_start(c.swt.rearrange("n p k -> p n k")[:, bass.ds(b * T, T), :], swt[:, p, :, :]).then_inc(stored[p], 16)

                f.sync(sp, nc, c.x1, pooled, store)
                for p in range(2):
                    sp.wait_ge(stored[p], 16 + 16 * (NB // 2))

            @block.tensor
            def _(pe):
                prime(pe, sw_turned, pooled)
                pe.wait_ge(w_loaded, 16 * 13)
                for k in range(NBK):
                    for ch in range(2):
                        op = nc.tensor.transpose(c.bank[k][:, ch * P:(ch + 1) * P], wx[:, ch, k * P:(k + 1) * P], c.ident[:, :])
                op.then_inc(pe_prep, 1)
                pe.wait_ge(dv, 3)
                for k in range(NBK):
                    for ch in range(2):
                        nc.tensor.matmul(c.bank[ch][:, k * P:(k + 1) * P], wx_t[:, k, ch * P:(ch + 1) * P], pair_slice[:, :], start=True, stop=True)
                    nc.tensor.matmul(c.bank[2][0:1, k * P:(k + 1) * P], bx[:, k:k + 1], pair_slice[:, :], start=True, stop=True)
                nc.tensor.matmul(c.bank[3][:, :], c.ones[0:1, :], rows[:, 0, :], start=True, stop=True).then_inc(pe_prep, 1)
                pe.wait_ge(dv, 6)
                nc.tensor.matmul(c.bank[3][:, :], c.ones[0:1, :], rows[:, 3, :], start=True, stop=True).then_inc(pe_prep, 1)
                for k in range(NBK):
                    nc.tensor.matmul(c.bank[4 + k][:, 0:D + 1], zeros[:, :], zero_rows[:, :], start=True, stop=False, skip_group_check=True)
                pe.wait_ge(dv, 7)
                with batches(pe) as pair:
                    for p in range(2):
                        b = pair * 2 + p
                        for i in range(T + 3):
                            if i < T:
                                f.tensor(pe, nc, c, b, i)
                            if 1 <= i <= T:
                                k = i - 1
                                pe.wait_ge(f.xt_made, 1 + b * T + i)
                                pe.wait_ge(lg_made, 1 + b * T + k)
                                for ch in range(2):
                                    op = nc.tensor.matmul(c.bank[2][:, :], f.xt[:, k, ch, :], wc[:, ch, :], start=(ch == 0), stop=(ch == 1))
                                op.then_inc(logits, 1)
                            if i >= 3:
                                k = i - 3
                                pe.wait_ge(sw_made, 1 + b * T + k + 1)
                                for q in range(NBK):
                                    op = nc.tensor.matmul(c.bank[4 + q][:, 0:D + 1], sw[:, k % 2, q * P:(q + 1) * P], f.xn[:, k, :], start=False, stop=True, skip_group_check=True)
                                op.then_inc(pooled, 1)
                                pe.wait_ge(swt_made, 1 + b * T + k)
                                for q in range(NBK):
                                    op = nc.tensor.transpose(c.bank[3][:, q * P:(q + 1) * P], sw[:, k % 2, q * P:(q + 1) * P], c.ident[:, :])
                                op.then_inc(sw_turned, 1)

            @block.vector
            def _(dve):
                prime(dve, lg_made, sw_made)
                v = nc.vector
                v.memset(zeros[:, :], 0.0)
                v.memset(zero_rows[:, :], 0.0)
                v.memset(f.xn[:, :, D:D + 1], 1.0)
                v.memset(pair_slice[:, :], 0.0).then_inc(dv, 1)
                dve.wait_ge(w_loaded, 16 * 13)
                v.tensor_scalar(temp[:, :], temp[:, :], 0.1, 5.0, ALU.max, ALU.min).then_inc(dv, 1)
                dve.wait_ge(dv, 2)
                v.reciprocal(temp[:, :], temp[:, :]).then_inc(mx_made, 1)
                dve.wait_ge(mx_made, 1)
                v.tensor_copy(rows[:, 0, :].rearrange("o (h g) -> o h g", h=FH), temp[:, :].rearrange("o (h g) -> o h g", g=1).broadcast_to([1, FH, FG]))
                dve.wait_ge(pe_prep, 1)
                for k in range(NBK):
                    op = v.tensor_copy(wx_t[:, k, :], c.bank[k][:, 0:D])
                op.then_inc(dv, 1)
                dve.wait_ge(pe_prep, 2)
                v.tensor_copy(inv_temp[:, :], c.bank[3][:, :])
                v.tensor_tensor(rows[:, 2, :], c.bank[2][0:1, :], rows[:, 1, :], ALU.add).then_inc(dv, 1)
                dve.wait_ge(dv, 4)
                for ch in range(2):
                    v.tensor_tensor(wc[:, ch, :], c.bank[ch][:, :], inv_temp[:, :], ALU.mult)
                v.tensor_tensor(rows[:, 3, :], rows[:, 2, :], rows[:, 0, :], ALU.mult).then_inc(dv, 1)
                dve.wait_ge(dv, 5)
                dve.sem_inc(dv, 1)
                dve.wait_ge(pe_prep, 3)
                v.tensor_copy(brow[:, :], c.bank[3][:, :]).then_inc(dv, 1)
                dve.wait_ge(dv, 7)
                with batches(dve) as pair:
                    for p in range(2):
                        b = pair * 2 + p
                        f.vector(dve, nc, b, pair, p)
                        for i in range(T + 1):
                            if i < T:
                                s, n = i % 2, b * T + i
                                heads = lg[:, s, :].rearrange("p (h g) -> p h g", h=FH)
                                dve.wait_ge(e_made, 1 + b * T + max(i - 1, 0))
                                dve.wait_ge(logits, n + 1)
                                v.tensor_tensor(lg[:, s, :], c.bank[2][:, :], brow[:, :], ALU.add).then_inc(lg_made, 1)
                                dve.wait_ge(lg_made, 1 + n + 1)
                                v.tensor_reduce(mx[:, s, :], heads, AX.X, ALU.max).then_inc(mx_made, 1)
                                dve.wait_ge(mx_made, n + 2)
                                v.tensor_tensor(heads, heads, mx[:, s, :].rearrange("p (h g) -> p h g", g=1).broadcast_to([P, FH, FG]), ALU.subtract).then_inc(sub_made, 1)
                            if i >= 1:
                                s, n = (i - 1) % 2, b * T + i - 1
                                heads = e[:, s, :].rearrange("p (h g) -> p h g", h=FH)
                                dve.wait_ge(e_made, 1 + n + 1)
                                v.tensor_reduce(total[:, s, :], heads, AX.X, ALU.add).then_inc(total_made, 1)
                                dve.wait_ge(total_made, n + 1)
                                v.reciprocal(inv[:, s, :], total[:, s, :]).then_inc(inv_made, 1)
                                dve.wait_ge(inv_made, n + 1)
                                v.tensor_scalar(inv[:, s, :], inv[:, s, :], c.valid[:, bass.ds(n, 1)], None, ALU.mult).then_inc(inv_masked, 1)
                                dve.wait_ge(inv_masked, n + 1)
                                dve.wait_ge(sw_turned, 1 + b * T + max(i - 2, 0))
                                v.tensor_tensor(sw[:, s, :].rearrange("p (h g) -> p h g", h=FH), heads,
                                                inv[:, s, :].rearrange("p (h g) -> p h g", g=1).broadcast_to([P, FH, FG]), ALU.mult).then_inc(sw_made, 1)

            @block.scalar
            def _(act):
                prime(act, swt_made, e_made, f.xt_made)
                with batches(act) as pair:
                    for p in range(2):
                        b = pair * 2 + p

                        def also(i):
                            if 2 <= i < T + 2:
                                k = i - 2
                                act.wait_ge(sub_made, b * T + k + 1)
                                act.wait_ge(sw_made, 1 + b * T + max(k - 1, 0))
                                nc.scalar.activation(e[:, k % 2, :], lg[:, k % 2, :], ACT.Exp).then_inc(e_made, 1)
                            if i == 0:
                                act.wait_ge(stored[p], 16 * pair + 16)
                            if i >= 4:
                                k = i - 4
                                act.wait_ge(sw_turned, 1 + b * T + k + 1)
                                nc.scalar.copy(swt[:, p, k, :], c.bank[3][:, :]).then_inc(swt_made, 1)

                        f.scalar(act, nc, c, b, p, pooled, also, 3)

        copied = sem("pooled_copied")
        with nc.Block() as block:
            @block.vector
            def _(dve):
                for k in range(NBK):
                    op = nc.vector.tensor_copy(pooled_out[:, k, :], c.bank[4 + k][:, 0:D + 1])
                op.then_inc(copied, 1)
                dve.wait_ge(copied, 1)


def token_attention(nc, c, w, pooled_in, w_comb):
    with ExitStack() as ctx:
        def sb(name, shape, dt=F32):
            return ctx.enter_context(nc.sbuf_tensor(f"ta_{name}", shape, dt))

        def sem(name):
            return nc.alloc_semaphore(f"ta_{name}")

        NBK = INNER // P
        wfx = sb("wfx", [P, 2, INNER])
        wout = sb("wout", [P, NBK, D])
        bfx = sb("bfx", [P, INNER])
        qkv = sb("qkv", [P, 3, P])
        mask = sb("mask", [P, P])
        hide = sb("hide", [P, P])
        half_row = sb("half_row", [P, P])
        half_col = sb("half_col", [P, 1])
        pt = sb("pt", [P, 2, P])
        tok = sb("tok", [P, P])
        tok_t = sb("tok_t", [P, P])
        qkv_out = sb("qkv_out", [P, 3, P])
        s = sb("s", [P, P])
        mx = sb("mx", [P, 1])
        e = sb("e", [P, P])
        total = sb("total", [P, 1])
        e_t = sb("e_t", [P, P])
        out_t = sb("out_t", [P, P])
        den = sb("den", [P, 1])
        w_loaded, dv, pv, av = sem("w_loaded"), sem("vector_step"), sem("tensor_step"), sem("block_projected")
        exp_made, inv_made, comb_made = sem("exp_made"), sem("inv_made"), sem("comb_made")
        V, PV = 15, 7
        scale = float(FG) ** -0.5
        with nc.Block() as block:
            @block.sync
            def _(sp):
                sp.dma_start(wfx[:, :, :], w["L0_ffn_W_fx"].rearrange("(c p) n -> p c n", p=P)).then_inc(w_loaded, 16)
                sp.dma_start(wout[:, :, :], w["L0_ffn_W_out"].rearrange("(k p) n -> p k n", p=P)).then_inc(w_loaded, 16)
                sp.dma_start(bfx[:, :], spread_row(w["L0_ffn_b_fx"], INNER)).then_inc(w_loaded, 16)
                sp.wait_ge(dv, 1)
                for n, name in enumerate(("L0_ffn_W_q", "L0_ffn_W_k", "L0_ffn_W_v")):
                    for h in range(2):
                        sp.dma_start(qkv[h * FG:(h + 1) * FG, n, h * FG:(h + 1) * FG], w[name]).then_inc(w_loaded, 16)

            @block.tensor
            def _(pe):
                pe.wait_ge(w_loaded, 16 * 9)
                t = nc.tensor
                for k in range(NBK):
                    d0 = 4 + V * k
                    pe.wait_ge(dv, d0)
                    for ch in range(2):
                        op = t.transpose(c.bank[0][:, ch * P:(ch + 1) * P], pooled_in[:, k, ch * P:(ch + 1) * P], c.ident[:, :])
                    op.then_inc(pv, 1)
                    pe.wait_ge(dv, d0 + 1)
                    for ch in range(2):
                        op = t.matmul(c.bank[1][:, 0:P], pt[:, ch, :], wfx[:, ch, k * P:(k + 1) * P], start=(ch == 0), stop=(ch == 1))
                    op.then_inc(pv, 1)
                    pe.wait_ge(dv, d0 + 6)
                    t.transpose(c.bank[2][:, 0:P], tok[:, :], c.ident[:, :]).then_inc(pv, 1)
                    pe.wait_ge(dv, d0 + 7)
                    t.matmul(c.bank[3][:, 0:P], qkv[:, 0, :], tok_t[:, :], start=True, stop=True)
                    t.matmul(c.bank[3][:, P:2 * P], qkv[:, 1, :], tok_t[:, :], start=True, stop=True)
                    t.matmul(c.bank[3][:, 2 * P:3 * P], tok_t[:, :], qkv[:, 2, :], start=True, stop=True).then_inc(pv, 1)
                    pe.wait_ge(dv, d0 + 8)
                    t.matmul(c.bank[4][:, 0:P], qkv_out[:, 0, :], qkv_out[:, 1, :], start=True, stop=True).then_inc(pv, 1)
                    pe.wait_ge(dv, d0 + 13)
                    t.transpose(c.bank[5][:, 0:P], e[:, :], c.ident[:, :]).then_inc(pv, 1)
                    pe.wait_ge(dv, d0 + 14)
                    t.matmul(c.bank[6][:, 0:P], qkv_out[:, 2, :], e_t[:, :], start=True, stop=True).then_inc(pv, 1)
                    pe.wait_ge(dv, d0 + 15)
                    t.matmul(c.bank[7][:, 0:D], out_t[:, :], wout[:, k, :], start=True, stop=True).then_inc(av, 1)

            @block.scalar
            def _(act):
                for k in range(NBK):
                    d0 = 4 + V * k
                    act.wait_ge(dv, d0 + 11)
                    nc.scalar.activation(e[:, :], s[:, :], ACT.Exp, scale=scale).then_inc(exp_made, 1)
                    act.wait_ge(av, k + 1)
                    nc.scalar.copy(w_comb[:, k, :], c.bank[7][:, 0:D]).then_inc(comb_made, 1)

            @block.vector
            def _(dve):
                v = nc.vector
                n = [0]

                def chain(op):
                    op.then_inc(dv, 1)
                    n[0] += 1
                    dve.wait_ge(dv, n[0])

                chain(v.memset(qkv[:, :, :], 0.0))
                v.tensor_scalar(half_col[:, :], c.ramp_col[:, :], float(FG), None, ALU.is_ge)
                chain(v.tensor_scalar(half_row[:, :], c.ramp_row[:, :], float(FG), None, ALU.is_ge))
                chain(v.tensor_scalar(mask[:, :], half_row[:, :], half_col[:, 0:1], None, ALU.is_equal))
                chain(v.tensor_scalar(hide[:, :], mask[:, :], 1.0, BIG, ALU.subtract, ALU.mult))
                dve.wait_ge(w_loaded, 16 * 9)
                for k in range(NBK):
                    norm = pooled_in[:, k, D:D + 1]
                    dve.wait_ge(pv, PV * k + 1)
                    if k:
                        dve.wait_ge(comb_made, k)
                    chain(v.tensor_copy(pt[:, :, :].rearrange("p c n -> p (c n)"), c.bank[0][:, 0:D]))
                    chain(v.tensor_scalar(den[:, :], norm, 1e-5, None, ALU.add))
                    chain(v.reciprocal(den[:, :], den[:, :]))
                    dve.wait_ge(pv, PV * k + 2)
                    chain(v.scalar_tensor_tensor(tok[:, :], bfx[:, k * P:(k + 1) * P], norm, c.bank[1][:, 0:P], ALU.mult, ALU.add))
                    chain(v.tensor_scalar(tok[:, :], tok[:, :], den[:, 0:1], None, ALU.mult))
                    chain(v.tensor_tensor(tok[:, :], tok[:, :], mask[:, :], ALU.mult))
                    dve.wait_ge(pv, PV * k + 3)
                    chain(v.tensor_copy(tok_t[:, :], c.bank[2][:, 0:P]))
                    dve.wait_ge(pv, PV * k + 4)
                    chain(v.tensor_copy(qkv_out[:, :, :].rearrange("p c n -> p (c n)"), c.bank[3][:, 0:3 * P]))
                    dve.wait_ge(pv, PV * k + 5)
                    chain(v.tensor_tensor(s[:, :], c.bank[4][:, 0:P], hide[:, :], ALU.add))
                    chain(v.tensor_reduce(mx[:, :], s[:, :], AX.X, ALU.max))
                    chain(v.tensor_scalar(s[:, :], s[:, :], mx[:, 0:1], None, ALU.subtract))
                    dve.wait_ge(exp_made, k + 1)
                    chain(v.tensor_reduce(total[:, :], e[:, :], AX.X, ALU.add))
                    dve.wait_ge(dv, n[0])
                    v.reciprocal(total[:, :], total[:, :]).then_inc(inv_made, 1)
                    dve.wait_ge(inv_made, k + 1)
                    chain(v.tensor_scalar(e[:, :], e[:, :], total[:, 0:1], None, ALU.mult))
                    dve.wait_ge(pv, PV * k + 6)
                    chain(v.tensor_copy(e_t[:, :], c.bank[5][:, 0:P]))
                    dve.wait_ge(pv, PV * k + 7)
                    chain(v.tensor_copy(out_t[:, :], c.bank[6][:, 0:P]))
                dve.wait_ge(comb_made, NBK)


def hyp_project(nc, c, w, w_comb):
    with ExitStack() as ctx:
        def sb(name, shape, dt=F32):
            return ctx.enter_context(nc.sbuf_tensor(f"hp_{name}", shape, dt))

        def sem(name):
            return nc.alloc_semaphore(f"hp_{name}")

        NBK = INNER // P
        f = Front(nc, ctx, "hp")
        swt = sb("swt", [P, 2, T, INNER])
        b_out = sb("b_out", [P, D])
        wg = sb("wg", [P, 2, D])
        w_ext = sb("w_ext", [P, 2, D + 1])
        b_row = sb("b_row", [P, D])
        att = sb("att", [P, 2, D])
        mag_b = sb("mag_b", [P, 1])
        raw = sb("raw", [P, T, D])
        z = sb("z", [P, T])
        junk = sb("junk", [P, 2, D])
        square = sb("square", [P, T])
        norm = sb("norm", [P, T])
        ez = sb("ez", [P, T])
        factor = sb("factor", [P, T])
        rows = sb("rows", [P, 2, T, B_ROW])
        dst_now = sb("dst_now", [P, T])
        act_junk = sb("act_junk", [P, D])
        swt_loaded = [sem("swt_loaded0"), sem("swt_loaded1")]
        x_stored = [sem("x_stored0"), sem("x_stored1")]
        rows_stored = [sem("rows_stored0"), sem("rows_stored1")]
        (w_loaded, mixed, x_mixed, x_made, w_turned, w_ready, projected, raw_made, squared, norm_made, ez_made, dv, scored, bias_added) = (sem(s) for s in (
            "w_loaded", "mixed", "x_mixed", "x_made", "w_turned", "w_ready", "projected", "raw_made", "squared", "norm_made", "ez_made", "dv", "scored", "bias_added"))
        row_made, passed_sp = sem("row_made"), sem("passed_sp")
        V = 5
        with nc.Block() as block:
            @block.sync
            def _(sp):
                sp.dma_start(b_out[:, :], spread_row(w["L0_ffn_b_out"], D)).then_inc(w_loaded, 16)
                sp.dma_start(b_row[:, :], spread_row(w["L1_gnn_b"], D)).then_inc(w_loaded, 16)
                sp.dma_start(att[:, :, :].rearrange("p a d -> p (a d)"), spread_row(w["L1_gnn_attn_w"].rearrange("o d -> (o d)"), 2 * D)).then_inc(w_loaded, 16)
                sp.dma_start(mag_b[:, :], spread_row(w["L1_gnn_mag_b"], 1)).then_inc(w_loaded, 16)
                sp.dma_start(wg[:, :, :], w["L1_gnn_W"].rearrange("(c p) n -> p c n", p=P)).then_inc(w_loaded, 16)
                sp.dma_start(w_ext[:, :, D:], w["L1_gnn_mag_w"].rearrange("one (c p) -> p c one", p=P), allow_slow_non_contiguous=True).then_inc(w_loaded, 16)
                for p in range(2):
                    sp.sem_inc(rows_stored[p], 16)

                def load(b, p):
                    f.load(sp, nc, c.x1, b, p)
                    nc.sync.dma_start(swt[:, p, :, :], c.swt.rearrange("n p k -> p n k")[:, bass.ds(b * T, T), :]).then_inc(swt_loaded[p], 16)

                def store(b, pair, p):
                    sp.wait_ge(x_made, b + 1)
                    sp.sem_inc(passed_sp, 1)
                    nc.sync.dma_start(tiles_of(c.x2, b), f.x[:, p, :, :]).then_inc(x_stored[p], 16)
                    sp.wait_ge(scored, (b + 1) * T)
                    sp.sem_inc(passed_sp, 1)
                    nc.sync.dma_start(tiles_of(c.b_table, b), rows[:, p, :, :]).then_inc(rows_stored[p], 16)

                for p in range(2):
                    load(p, p)
                with sp.Fori(0, NB // 2 - 1) as pair:
                    for p in range(2):
                        b = pair * 2 + p
                        store(b, pair, p)
                        sp.wait_ge(x_stored[p], 16 * pair + 16)
                        sp.sem_inc(passed_sp, 1)
                        sp.wait_ge(projected, 1 + (b + 1) * T)
                        sp.sem_inc(passed_sp, 1)
                        load(b + 2, p)
                for p in range(2):
                    store(NB - 2 + p, None, p)
                for p in range(2):
                    sp.wait_ge(x_stored[p], 16 * (NB // 2))
                    sp.wait_ge(rows_stored[p], 16 + 16 * (NB // 2))

            @block.vector
            def _(dve):
                prime(dve, x_mixed, raw_made)
                v = nc.vector
                v.memset(dst_now[:, :], 0.0)
                v.memset(rows[:, :, :, :], 1.0)
                dve.wait_ge(w_loaded, 96)
                dve.wait_ge(w_turned, 1)
                op = v.tensor_copy(w_ext[:, :, 0:D], c.bank[4][:, :].rearrange("p (c n) -> p c n", c=2))
                op.then_inc(w_ready, 1)
                with batches(dve) as pair:
                    for p in range(2):
                        b = pair * 2 + p

                        def update():
                            for i in range(T):
                                dve.wait_ge(mixed, b * T + i + 1)
                                v.tensor_tensor(f.x[:, p, i, :], f.x[:, p, i, :], c.bank[4 + i % 2][:, 0:D], ALU.add).then_inc(x_mixed, 1)
                            dve.wait_ge(x_mixed, 1 + (b + 1) * T)
                            for i in range(T):
                                op = v.tensor_tensor(f.x[:, p, i, :], f.x[:, p, i, :], b_out[:, :], ALU.add)
                            op.then_inc(x_made, 1)
                            dve.wait_ge(x_made, b + 1)

                        f.vector(dve, nc, b, pair, p, update)

                        def chain(op, n):
                            op.then_inc(dv, 1)
                            dve.wait_ge(dv, b * V + n)

                        for i in range(T):
                            dve.wait_ge(projected, 1 + b * T + i + 1)
                            v.tensor_tensor(raw[:, i, :], c.bank[2 + i % 2][:, 0:D], b_row[:, :], ALU.add)
                            v.tensor_copy(z[:, i:i + 1], c.bank[2 + i % 2][:, D:D + 1]).then_inc(raw_made, 1)
                        dve.wait_ge(raw_made, 1 + (b + 1) * T)
                        v.tensor_scalar(z[:, :], z[:, :], mag_b[:, 0:1], None, ALU.add).then_inc(bias_added, 1)
                        dve.wait_ge(norm_made, b + 1)
                        chain(v.tensor_scalar(norm[:, :], norm[:, :], 1e-12, None, ALU.max), 1)
                        dve.wait_ge(ez_made, b + 1)
                        chain(v.tensor_scalar(ez[:, :], ez[:, :], 1.0, None, ALU.add), 2)
                        chain(v.reciprocal(factor[:, :], ez[:, :]), 3)
                        chain(v.reciprocal(norm[:, :], norm[:, :]), 4)
                        chain(v.scalar_tensor_tensor(factor[:, :], factor[:, :], 1.5, norm[:, :], ALU.mult, ALU.mult), 5)
                        dve.wait_ge(rows_stored[p], 16 * pair + 16)
                        for i in range(T):
                            v.tensor_scalar(rows[:, p, i, 0:D], raw[:, i, :], factor[:, i:i + 1], None, ALU.mult).then_inc(row_made, 1)
                        dve.wait_ge(row_made, (b + 1) * T)
                        for i in range(T):
                            v.tensor_tensor_reduce(junk[:, 0, :], rows[:, p, i, 0:D], att[:, 0, :], 1.0, 0.0, ALU.mult, ALU.add, rows[:, p, i, D + 1:D + 2])
                            v.tensor_tensor_reduce(junk[:, 1, :], rows[:, p, i, 0:D], att[:, 1, :], 1.0, 0.0, ALU.mult, ALU.add, dst_now[:, i:i + 1]).then_inc(scored, 1)
                            dve.wait_ge(scored, b * T + i + 1)
                        v.tensor_copy(c.dst_score[:, bass.ds(b * T, T)], dst_now[:, :])

            @block.scalar
            def _(act):
                prime(act, f.xt_made)
                with batches(act) as pair:
                    for p in range(2):
                        b = pair * 2 + p
                        f.scalar(act, nc, c, b, p, projected)
                        for i in range(T):
                            act.wait_ge(raw_made, 1 + b * T + i + 1)
                            nc.scalar.activation(act_junk[:, :], raw[:, i, :], ACT.Square, accum_out=square[:, i:i + 1]).then_inc(squared, 1)
                            act.wait_ge(squared, b * T + i + 1)
                        nc.scalar.activation(norm[:, :], square[:, :], ACT.Sqrt).then_inc(norm_made, 1)
                        act.wait_ge(bias_added, b + 1)
                        nc.scalar.activation(ez[:, :], z[:, :], ACT.Exp, scale=-1.0).then_inc(ez_made, 1)

            @block.tensor
            def _(pe):
                prime(pe, projected)
                pe.wait_ge(w_loaded, 96)
                for a in range(2):
                    for ch in range(2):
                        op = nc.tensor.transpose(c.bank[4][:, ch * D + a * P:ch * D + (a + 1) * P], wg[:, a, ch * P:(ch + 1) * P], c.ident[:, :])
                op.then_inc(w_turned, 1)
                pe.wait_ge(w_ready, 1)
                with batches(pe) as pair:
                    for p in range(2):
                        b = pair * 2 + p
                        pe.wait_ge(swt_loaded[p], 16 * pair + 16)
                        for i in range(T):
                            pe.wait_ge(x_mixed, 1 + b * T + max(i - 1, 0))
                            for q in range(NBK):
                                op = nc.tensor.matmul(c.bank[4 + i % 2][:, 0:D], swt[:, p, i, q * P:(q + 1) * P], w_comb[:, q, :], start=(q == 0), stop=(q == NBK - 1))
                            op.then_inc(mixed, 1)
                        for i in range(T + 1):
                            if i < T:
                                f.tensor(pe, nc, c, b, i)
                            if i >= 1:
                                k = i - 1
                                pe.wait_ge(f.xt_made, 1 + b * T + i)
                                pe.wait_ge(raw_made, 1 + b * T + max(k - 1, 0))
                                for ch in range(2):
                                    op = nc.tensor.matmul(c.bank[2 + k % 2][:, 0:D + 1], f.xt[:, k, ch, :], w_ext[:, ch, :], start=(ch == 0), stop=(ch == 1))
                                op.then_inc(projected, 1)



def hyp_finish(nc, c, w, acc):
    MAX_NORM = 0.95
    with ExitStack() as ctx:
        def sb(name, shape, dt=F32):
            return ctx.enter_context(nc.sbuf_tensor(f"hf_{name}", shape, dt))

        def sem(name):
            return nc.alloc_semaphore(f"hf_{name}")

        x = sb("x", [P, 2, T, D])
        h = sb("h", [P, 2, T, B_ROW])
        den = sb("den", [P, T])
        hc = sb("hc", [P, T, D])
        act_junk = sb("act_junk", [P, D])
        square = sb("square", [P, T])
        norm = sb("norm", [P, T])
        clamped = sb("clamped", [P, T])
        th = sb("th", [P, T])
        ball = sb("ball", [P, T])
        over = sb("over", [P, T])
        loaded = [sem("loaded0"), sem("loaded1")]
        stored = [sem("stored0"), sem("stored1")]
        dv, row_made, squared, norm_made, clamped_made, th_made, x_made, passed = (sem(s) for s in (
            "dv", "row_made", "squared", "norm_made", "clamped_made", "th_made", "x_made", "passed"))
        V = 11
        with nc.Block() as block:
            @block.sync
            def _(sp):
                def load(b, p):
                    nc.sync.dma_start(x[:, p, :, :], tiles_of(c.x2, b)).then_inc(loaded[p], 16)
                    nc.sync.dma_start(h[:, p, :, :], tiles_of(c.b_table, b)).then_inc(loaded[p], 16)

                def store(b, p):
                    sp.wait_ge(x_made, 1 + (b + 1) * T)
                    sp.sem_inc(passed, 1)
                    nc.sync.dma_start(tiles_of(c.x3, b), x[:, p, :, :]).then_inc(stored[p], 16)

                for p in range(2):
                    load(p, p)
                with sp.Fori(0, NB // 2 - 1) as pair:
                    for p in range(2):
                        store(pair * 2 + p, p)
                        sp.wait_ge(stored[p], 16 * pair + 16)
                        sp.sem_inc(passed, 1)
                        load(pair * 2 + p + 2, p)
                for p in range(2):
                    store(NB - 2 + p, p)
                for p in range(2):
                    sp.wait_ge(stored[p], 16 * (NB // 2))

            @block.vector
            def _(dve):
                prime(dve, x_made)
                v = nc.vector
                with batches(dve) as pair:
                    for p in range(2):
                        b = pair * 2 + p

                        def chain(op, n):
                            op.then_inc(dv, 1)
                            dve.wait_ge(dv, b * V + n)

                        sums = acc[:, bass.ds(b * T * B_ACC, T * B_ACC)].rearrange("p (t k) -> p t k", t=T)
                        dve.wait_ge(loaded[p], 32 * pair + 32)
                        chain(v.tensor_scalar(den[:, :], sums[:, :, D], 1e-10, None, ALU.add), 1)
                        chain(v.reciprocal(den[:, :], den[:, :]), 2)
                        for i in range(T):
                            v.scalar_tensor_tensor(hc[:, i, :], sums[:, i, 0:D], den[:, i:i + 1], h[:, p, i, 0:D], ALU.mult, ALU.add).then_inc(row_made, 1)
                        dve.wait_ge(norm_made, b + 1)
                        v.tensor_scalar(clamped[:, :], norm[:, :], 1e-15, None, ALU.max).then_inc(clamped_made, 1)
                        dve.wait_ge(clamped_made, b + 1)
                        chain(v.reciprocal(ball[:, :], clamped[:, :]), 3)
                        dve.wait_ge(th_made, b + 1)
                        chain(v.tensor_tensor(ball[:, :], ball[:, :], th[:, :], ALU.mult), 4)
                        chain(v.tensor_tensor(norm[:, :], norm[:, :], ball[:, :], ALU.mult), 5)
                        chain(v.tensor_scalar(over[:, :], norm[:, :], MAX_NORM, None, ALU.is_gt), 6)
                        chain(v.tensor_scalar(norm[:, :], norm[:, :], 1e-8, None, ALU.add), 7)
                        chain(v.reciprocal(norm[:, :], norm[:, :]), 8)
                        chain(v.tensor_scalar(norm[:, :], norm[:, :], MAX_NORM, 1.0, ALU.mult, ALU.subtract), 9)
                        chain(v.tensor_tensor(norm[:, :], norm[:, :], over[:, :], ALU.mult), 10)
                        chain(v.scalar_tensor_tensor(ball[:, :], norm[:, :], 1.0, ball[:, :], ALU.add, ALU.mult), 11)
                        for i in range(T):
                            v.scalar_tensor_tensor(x[:, p, i, :], hc[:, i, :], ball[:, i:i + 1], x[:, p, i, :], ALU.mult, ALU.add).then_inc(x_made, 1)

            @block.scalar
            def _(act):
                with batches(act) as pair:
                    for p in range(2):
                        b = pair * 2 + p
                        for i in range(T):
                            act.wait_ge(row_made, b * T + i + 1)
                            nc.scalar.activation(act_junk[:, :], hc[:, i, :], ACT.Square, accum_out=square[:, i:i + 1]).then_inc(squared, 1)
                            act.wait_ge(squared, b * T + i + 1)
                        act.wait_ge(x_made, 1 + b * T)
                        nc.scalar.activation(norm[:, :], square[:, :], ACT.Sqrt).then_inc(norm_made, 1)
                        act.wait_ge(clamped_made, b + 1)
                        nc.scalar.activation(th[:, :], clamped[:, :], ACT.Tanh).then_inc(th_made, 1)


def experts(nc, c, w, out):
    with ExitStack() as ctx:
        def sb(name, shape, dt=F32):
            return ctx.enter_context(nc.sbuf_tensor(f"ex_{name}", shape, dt))

        def sem(name):
            return nc.alloc_semaphore(f"ex_{name}")

        FB = FF // P
        SEGS = [(0, 4), (4, T)]
        NS = len(SEGS)
        f = Front(nc, ctx, "ex")
        w1 = sb("w1", [P, NX, 2, FF])
        w2 = sb("w2", [P, NX, FB, D])
        b1 = sb("b1", [P, NX, FB])
        b2 = sb("b2", [NX, D])
        wgate = sb("wgate", [P, 2, NX])
        bgate = sb("bgate", [P, 2, NX])
        lg = sb("lg", [P, T, NX])
        best = sb("best", [P, T, 8])
        best_at = sb("best_at", [P, T, 8], mybir.dt.uint32)
        best_f = sb("best_f", [P, T, 8])
        gap = sb("gap", [P, T])
        share = sb("share", [P, 2, T])
        comb = sb("comb", [P, T, NX])
        comb2 = sb("comb2", [P, T, NX])
        comb_t = sb("comb_t", [NX, T, P])
        hid = sb("hid", [P, 2, FB, T * P])
        w_loaded, x_stored = sem("w_loaded"), [sem("x_stored0"), sem("x_stored1")]
        (gated, lg_made, dv, gap_made, e2_made, comb_made, comb_turned, comb_t_made, b2_mixed, b2_added, base_made, up, hid_made, down, summed, passed, passed_v) = (sem(s) for s in (
            "gated", "lg_made", "dv", "gap_made", "e2_made", "comb_made", "comb_turned", "comb_t_made", "b2_mixed", "b2_added", "base_made", "up", "hid_made", "down", "summed", "passed", "passed_v"))
        xt_used = sem("xt_used")
        V = 7
        with nc.Block() as block:
            @block.sync
            def _(sp):
                for ch in range(2):
                    sp.dma_start(wgate[:, ch, :], w["L1_ffn_Wg"].rearrange("(c p) n -> c p n", p=P)[ch]).then_inc(w_loaded, 16)
                sp.dma_start(b1[:, :, :], w["L1_ffn_b1"].rearrange("e (k p) -> p e k", p=P), allow_slow_non_contiguous=True).then_inc(w_loaded, 16)
                sp.dma_start(b2[:, :], w["L1_ffn_b2"]).then_inc(w_loaded, 16)
                sp.dma_start(bgate[:, 0, :], spread_row(w["L1_ffn_bg"], NX)).then_inc(w_loaded, 16)
                sp.dma_start(bgate[:, 1, :], spread_row(w["L1_ffn_bias"], NX)).then_inc(w_loaded, 16)
                for n in range(NX):
                    sp.dma_start(w1[:, n, :, :], w["L1_ffn_W1"][n].rearrange("(c p) n -> p c n", p=P)).then_inc(w_loaded, 16)
                    sp.dma_start(w2[:, n, :, :], w["L1_ffn_W2"][n].rearrange("(k p) n -> p k n", p=P)).then_inc(w_loaded, 16)

                def store(b, p):
                    sp.wait_ge(summed, 1 + (b + 1) * NX * T)
                    sp.sem_inc(passed, 1)
                    nc.sync.dma_start(tiles_of(out, b), f.x[:, p, :, :]).then_inc(x_stored[p], 16)

                for p in range(2):
                    f.load(sp, nc, c.x3, p, p)
                with sp.Fori(0, NB // 2 - 1) as pair:
                    for p in range(2):
                        store(pair * 2 + p, p)
                        sp.wait_ge(x_stored[p], 16 * pair + 16)
                        sp.sem_inc(passed, 1)
                        f.load(sp, nc, c.x3, pair * 2 + p + 2, p)
                for p in range(2):
                    store(NB - 2 + p, p)
                for p in range(2):
                    sp.wait_ge(x_stored[p], 16 * (NB // 2))

            @block.vector
            def _(dve):
                prime(dve, b2_added, summed)
                v = nc.vector
                dve.wait_ge(w_loaded, 16 * (6 + 2 * NX))
                v.tensor_tensor(bgate[:, 0, :], bgate[:, 0, :], bgate[:, 1, :], ALU.add).then_inc(base_made, 1)
                dve.wait_ge(base_made, 1)
                with batches(dve) as pair:
                    for p in range(2):
                        b = pair * 2 + p
                        f.vector(dve, nc, b, pair, p)

                        def chain(op, n):
                            op.then_inc(dv, 1)
                            dve.wait_ge(dv, b * V + n)
                            dve.sem_inc(passed_v, 1)

                        dve.wait_ge(gated, b + 1)
                        for i in range(T):
                            op = v.tensor_tensor(lg[:, i, :], c.bank[2][:, i * NX:(i + 1) * NX], bgate[:, 0, :], ALU.add)
                        chain(op, 1)
                        for i in range(T):
                            op = v.max(best[:, i, :], lg[:, i, :])
                        chain(op, 2)
                        v.tensor_tensor(gap[:, :], best[:, :, 1], best[:, :, 0], ALU.subtract).then_inc(gap_made, 1)
                        for i in range(T):
                            op = v.max_index(best_at[:, i, :], best[:, i, :], lg[:, i, :])
                        chain(op, 3)
                        v.tensor_copy(best_f[:, :, :], best_at[:, :, :])
                        dve.wait_ge(e2_made, b + 1)
                        chain(v.tensor_scalar(share[:, 0, :], share[:, 1, :], 1.0, None, ALU.add), 4)
                        chain(v.reciprocal(share[:, 0, :], share[:, 0, :]), 5)
                        chain(v.tensor_tensor(share[:, 1, :], share[:, 1, :], share[:, 0, :], ALU.mult), 6)
                        for i in range(T):
                            v.tensor_scalar(comb[:, i, :], c.ramp_row[:, 0:NX], best_f[:, i, 0:1], share[:, 0, i:i + 1], ALU.is_equal, ALU.mult)
                            op = v.tensor_scalar(comb2[:, i, :], c.ramp_row[:, 0:NX], best_f[:, i, 1:2], share[:, 1, i:i + 1], ALU.is_equal, ALU.mult)
                        chain(op, 7)
                        v.tensor_tensor(comb[:, :, :], comb[:, :, :], comb2[:, :, :], ALU.add).then_inc(comb_made, 1)
                        for i in range(T):
                            dve.wait_ge(b2_mixed, b * T + i + 1)
                            v.tensor_tensor(f.x[:, p, i, :], f.x[:, p, i, :], c.bank[3][:, 0:D], ALU.add).then_inc(b2_added, 1)
                        dve.wait_ge(b2_added, 1 + (b + 1) * T)
                        for n in range(NX):
                            for i in range(T):
                                m = (b * NX + n) * T + i
                                if n:
                                    dve.wait_ge(summed, 1 + m - T + 1)
                                dve.wait_ge(down, 1 + m + 1)
                                v.scalar_tensor_tensor(f.x[:, p, i, :], c.bank[6 + (n * T + i) % 2][:, 0:D], comb[:, i, n:n + 1], f.x[:, p, i, :], ALU.mult, ALU.add).then_inc(summed, 1)

            @block.scalar
            def _(act):
                prime(act, comb_t_made, hid_made, f.xt_made)
                with batches(act) as pair:
                    for p in range(2):
                        b = pair * 2 + p
                        f.scalar(act, nc, c, b, p, xt_used)
                        act.wait_ge(gap_made, b + 1)
                        nc.scalar.activation(share[:, 1, :], gap[:, :], ACT.Exp).then_inc(e2_made, 1)
                        for n in range(NX):
                            if n >= 2:
                                act.wait_ge(down, 1 + (b * NX + n - 1) * T)
                            for k in range(FB):
                                for s, (lo, hi) in enumerate(SEGS):
                                    m = ((b * NX + n) * FB + k) * NS + s
                                    act.wait_ge(up, m + 1)
                                    nc.scalar.activation(hid[:, n % 2, k, lo * P:hi * P], c.bank[4 + s][:, 0:(hi - lo) * P], ACT.Relu, bias=b1[:, n, k:k + 1]).then_inc(hid_made, 1)
                            if n == 0:
                                for i in range(T):
                                    act.wait_ge(comb_turned, b * T + i + 1)
                                    nc.scalar.copy(comb_t[:, i, :], c.bank[i % 2][0:NX, 0:P]).then_inc(comb_t_made, 1)

            @block.tensor
            def _(pe):
                prime(pe, down, xt_used)
                t = nc.tensor
                pe.wait_ge(w_loaded, 16 * (6 + 2 * NX))
                with batches(pe) as pair:
                    for p in range(2):
                        b = pair * 2 + p
                        for i in range(T + 1):
                            if i < T:
                                f.tensor(pe, nc, c, b, i)
                            if i >= 1:
                                pe.wait_ge(f.xt_made, 1 + b * T + i)
                                for ch in range(2):
                                    op = t.matmul(c.bank[2][:, (i - 1) * NX:i * NX], f.xt[:, i - 1, ch, :], wgate[:, ch, :], start=(ch == 0), stop=(ch == 1))
                        op.then_inc(gated, 1)

                        def hidden(n):
                            for k in range(FB):
                                for s, (lo, hi) in enumerate(SEGS):
                                    m = ((b * NX + n) * FB + k) * NS + s
                                    pe.wait_ge(hid_made, 1 + m - NS + 1) if n or k else pe.wait_ge(hid_made, 1 + b * NX * FB * NS)
                                    for ch in range(2):
                                        op = t.matmul(c.bank[4 + s][:, 0:(hi - lo) * P].rearrange("p (t n) -> p t n", n=P), w1[:, n, ch, k * P:(k + 1) * P], f.xt[:, lo:hi, ch, :],
                                                      start=(ch == 0), stop=(ch == 1))
                                    op.then_inc(up, 1)

                        hidden(0)
                        pe.wait_ge(comb_made, b + 1)
                        for i in range(T + 1):
                            if i < T:
                                pe.wait_ge(comb_t_made, 1 + b * T + max(i - 1, 0))
                                t.transpose(c.bank[i % 2][0:NX, 0:P], comb[:, i, :], c.ident[:, :]).then_inc(comb_turned, 1)
                            if i >= 1:
                                pe.wait_ge(comb_t_made, 1 + b * T + i)
                                pe.wait_ge(b2_added, 1 + b * T + i - 1)
                                t.matmul(c.bank[3][:, 0:D], comb_t[:, i - 1, :], b2[:, :], start=True, stop=True).then_inc(b2_mixed, 1)
                        for n in range(NX):
                            if n + 1 < NX:
                                hidden(n + 1)
                            if n + 1 == NX:
                                pe.sem_inc(xt_used, T)
                            for i in range(T):
                                m = (b * NX + n) * T + i
                                if i == 0:
                                    pe.wait_ge(hid_made, 1 + (b * NX + n + 1) * FB * NS)
                                pe.wait_ge(summed, 1 + m - 1) if n or i >= 2 else pe.wait_ge(summed, 1 + b * NX * T)
                                for k in range(FB):
                                    op = t.matmul(c.bank[6 + (n * T + i) % 2][:, 0:D], hid[:, n % 2, k, i * P:(i + 1) * P], w2[:, n, k, :], start=(k == 0), stop=(k == FB - 1))
                                op.then_inc(down, 1)


def program(nc, w, out):
    def dram(name, shape, dt=F32):
        return nc.dram_tensor(name, shape, dt).ap()

    with ExitStack() as ctx:
        def sb(name, shape, dt=F32):
            return ctx.enter_context(nc.sbuf_tensor(name, shape, dt))

        def sem(name):
            return nc.alloc_semaphore(name)

        c = Core()
        c.bank = [ctx.enter_context(nc.psum_tensor(f"bank{b}", [P, 512], F32)) for b in range(8)]
        c.x_in, c.x1, c.x2, c.x3 = w["x"], dram("x1", [NPAD, D]), dram("x2", [NPAD, D]), dram("x3", [NPAD, D])
        c.a_table, c.b_table = dram("a_table", [NPAD, A_ROW]), dram("b_table", [NPAD, B_ROW])
        c.swt = dram("swt", [NT, P, INNER])
        make_constants(nc, c, sb, sem)
        c.dst_score = sb("dst_score", [P, NT * HEADS])
        with nc.cleanup_on_exit():
            make_schedule(nc, c, w["src"], w["dst"], dram)
        with nc.cleanup_on_exit():
            gat_project(nc, c, w)
        with nc.sbuf_tensor("a_sums", [P, NT * A_ACC], F32) as sums:
            with nc.cleanup_on_exit():
                edge_stage(nc, c, "ea", HEADS, 0.2, c.a_table, A_ROW, A_ACC, HEADS * HC, -BIG, sums)
            with nc.cleanup_on_exit():
                gat_finish(nc, c, w, sums)
        with nc.sbuf_tensor("w_comb", [P, INNER // P, D], F32) as w_comb:
            with nc.sbuf_tensor("pooled", [P, INNER // P, D + 1], F32) as pooled:
                with nc.cleanup_on_exit():
                    slice_tokens(nc, c, w, pooled)
                with nc.cleanup_on_exit():
                    token_attention(nc, c, w, pooled, w_comb)
            with nc.cleanup_on_exit():
                hyp_project(nc, c, w, w_comb)
        with nc.sbuf_tensor("b_sums", [P, NT * B_ACC], F32) as sums:
            with nc.cleanup_on_exit():
                edge_stage(nc, c, "eb", 1, None, c.b_table, B_ROW, B_ACC, D + 1, -1e9, sums)
            with nc.cleanup_on_exit():
                hyp_finish(nc, c, w, sums)
        with nc.cleanup_on_exit():
            experts(nc, c, w, out)


_WEIGHTS = ["L0_gnn_W", "L0_gnn_att_src", "L0_gnn_att_dst", "L0_gnn_bias", "L0_gnn_Wp", "L0_gnn_bp",
            "L0_ffn_W_fx", "L0_ffn_b_fx", "L0_ffn_W_x", "L0_ffn_b_x", "L0_ffn_W_slice", "L0_ffn_b_slice",
            "L0_ffn_W_q", "L0_ffn_W_k", "L0_ffn_W_v", "L0_ffn_W_out", "L0_ffn_b_out", "L0_ffn_temperature",
            "L1_gnn_W", "L1_gnn_b", "L1_gnn_mag_w", "L1_gnn_mag_b", "L1_gnn_attn_w",
            "L1_ffn_Wg", "L1_ffn_bg", "L1_ffn_bias", "L1_ffn_W1", "L1_ffn_b1", "L1_ffn_W2", "L1_ffn_b2"]


def kernel(**inputs):
    import numpy as _np
    import concourse.bacc as _bacc
    from concourse import mybir as _mybir
    from concourse.bass_utils import run_bass_kernel_spmd as _run

    def padded(a, shape, fill):
        a = _np.asarray(a)
        out = _np.full(shape, fill, a.dtype)
        out.reshape(-1)[:a.size] = a.reshape(-1)
        return out

    arrays = {
        "x": padded(inputs["x"], (NPAD, D), 0),
        "src": padded(inputs["src"], (K, P), 0),
        "dst": padded(inputs["dst"], (K, P), NPAD - 1),
    }
    for name in _WEIGHTS:
        arrays[name] = _np.ascontiguousarray(inputs[name])
    nc = _bacc.Bacc("TRN2", target_bir_lowering=False, num_devices=1)
    w = {name: nc.dram_tensor(name, a.shape, _mybir.dt.from_np(a.dtype), kind="ExternalInput").ap() for name, a in arrays.items()}
    out = nc.dram_tensor("out", (NPAD, D), F32, kind="ExternalOutput").ap()
    program(nc, w, out)
    r = _run(nc, [arrays], core_ids=[0])
    return r.results[0]["out"][:N]
```

```python
from contextlib import ExitStack

import numpy as np
import concourse.bass as bass
from concourse import mybir

F32 = mybir.dt.float32
BF16 = mybir.dt.bfloat16
I32 = mybir.dt.int32
ALU = mybir.AluOpType
ACT = mybir.ActivationFunctionType
AX = mybir.AxisListType

P = 128
N = 12500
D = 256
E = 200000
NT = -(-N // P)
NPAD = NT * P
ET = -(-E // P)
G = 32
NG = 2 * (-(-(ET + NT - 1) // (2 * G)))
K = NG * G
KC = K // P
EPAD = K * P
T = 7
NB = NT // T
assert NB * T == NT and NB % 2 == 0 and KC * P == K
BIG = float(2 ** 100)
EPS = 1e-5
HEADS, HC = 4, 32
A_ROW = HEADS * HC + HEADS
A_ACC = A_ROW + HEADS
B_ROW = D + 2
B_ACC = D + 1
FH, FG = 8, 64
INNER = FH * FG
NX, FF = 8, 512
REG = (NT + 1) * P
SLOTS = -(-(2 * NT + NX) // 4) * 4


class Core:
    pass


def batches(eng):
    return eng.Fori(0, NB // 2)


def groups(eng):
    return eng.Fori(0, NG // 2)


def prime(eng, *events):
    for event in events:
        eng.sem_inc(event, 1)


def make_constants(nc, c, sb, sem):
    c.ident = sb("ident", [P, P])
    c.ramp_row = sb("ramp_row", [P, P])
    c.ramp_col = sb("ramp_col", [P, 1])
    c.minus_ramp = sb("minus_ramp", [P, 1])
    c.ones = sb("ones", [P, P])
    c.ones_bf = sb("ones_bf", [P, P], BF16)
    c.valid = sb("valid", [P, NT])
    c.eps = sb("eps", [P, 1])
    ints = sb("ramp_ints", [P, P + 1 + NT], I32)
    ramps_made, ramps_copied, constants_made = sem("ramps_made"), sem("ramps_copied"), sem("constants_made")
    with nc.Block() as block:
        @block.gpsimd
        def _(pool):
            nc.gpsimd.iota(ints[:, 0:P], [[1, P]], base=0, channel_multiplier=0)
            nc.gpsimd.iota(ints[:, P:P + 1], [[1, 1]], base=0, channel_multiplier=1)
            nc.gpsimd.iota(ints[:, P + 1:], [[P, NT]], base=0, channel_multiplier=1).then_inc(ramps_made, 1)

        @block.vector
        def _(dve):
            nc.vector.memset(c.ones[:, :], 1.0)
            nc.vector.memset(c.eps[:, :], EPS)
            nc.vector.memset(c.ones_bf[:, :], 1.0)
            dve.wait_ge(ramps_made, 1)
            nc.vector.tensor_copy(c.ramp_row[:, :], ints[:, 0:P])
            nc.vector.tensor_copy(c.ramp_col[:, :], ints[:, P:P + 1])
            nc.vector.tensor_copy(c.valid[:, :], ints[:, P + 1:]).then_inc(ramps_copied, 1)
            dve.wait_ge(ramps_copied, 1)
            nc.vector.tensor_scalar(c.minus_ramp[:, :], c.ramp_col[:, :], -1.0, None, ALU.mult)
            nc.vector.tensor_scalar(c.ident[:, :], c.ramp_row[:, :], c.ramp_col[:, 0:1], None, ALU.is_equal)
            nc.vector.tensor_scalar(c.valid[:, :], c.valid[:, :], float(N), None, ALU.is_lt).then_inc(constants_made, 1)
            dve.wait_ge(constants_made, 1)


def make_schedule(nc, c, src, dst, dram):
    flat = dram("dst_flat", [1, EPAD + 2], F32)
    c.keep_prev = dram("keep_prev", [K, P], F32)
    c.keep_next = dram("keep_next", [K, P], F32)
    c.local_rows = dram("local_rows", [1, EPAD], BF16)
    c.step_rows = dram("step_rows", [4, K], F32)
    c.step_tiles = dram("step_tiles", [1, K], I32)
    c.edge_src = dram("edge_src", [NG, P, G], I32)
    c.edge_place = dram("edge_place", [NG, P, G], F32)
    small, tiles = c.step_rows, c.step_tiles
    with ExitStack() as ctx:
        def sb(name, shape, dt=F32):
            return ctx.enter_context(nc.sbuf_tensor(name, shape, dt))

        def sem(name):
            return nc.alloc_semaphore(name)

        dst_in = sb("dst_in", [P, KC, P], I32)
        last = sb("last", [P, KC], I32)
        key = sb("key", [P, KC])
        step = sb("step", [P, KC])
        step_i = sb("step_i", [P, KC], I32)
        diag = sb("diag", [P, KC, P])
        keys = sb("keys", [P, K])
        below = sb("below", [P, K])
        t_f = sb("t_f", [P, KC])
        t_i = sb("t_i", [P, KC], I32)
        n_f = sb("n_f", [P, KC])
        n_i = sb("n_i", [P, KC], I32)
        n_p = sb("n_p", [P, KC])
        rows_i = sb("rows_i", [P, 2, KC, P], I32)
        dst_f = sb("dst_f", [P, KC, P])
        src_f = sb("src_f", [P, KC, P])
        local = sb("local", [P, KC, P])
        local_bf = sb("local_bf", [P, KC, P], BF16)
        near = sb("near", [P, 2, KC, P])
        one_seg = sb("one_seg", [P, KC])
        four = sb("four", [P, 4, KC])
        turned_src = sb("turned_src", [P, K], I32)
        turned_place = sb("turned_place", [P, K])
        margin = sb("margin", [1, 2])
        dst_loaded, ramp, told, dv = sem("dst_loaded"), sem("step_ramp"), sem("step_told"), sem("schedule_vector")
        keys_spread, rows_found, flat_stored, near_loaded = sem("keys_spread"), sem("rows_found"), sem("flat_stored"), sem("near_loaded")
        turned, all_stored, by_edge_stored = sem("turned"), sem("all_stored"), sem("by_edge_stored")
        with nc.Block() as block:
            @block.sync
            def _(sp):
                sp.dma_start(dst_in[:, :, :], dst.rearrange("(j p) e -> p j e", p=P)).then_inc(dst_loaded, 16)
                sp.wait_ge(dv, 7)
                sp.dma_start(flat[0, 1:1 + EPAD].rearrange("(j p e) -> p j e", p=P, e=P), dst_f[:, :, :]).then_inc(flat_stored, 16)
                sp.dma_start(flat[0:1, 0:1], margin[:, 0:1]).then_inc(flat_stored, 16)
                sp.dma_start(flat[0:1, EPAD + 1:EPAD + 2], margin[:, 1:2]).then_inc(flat_stored, 16)
                sp.wait_ge(flat_stored, 48)
                sp.dma_start(near[:, 0, :, :], flat[0, 0:EPAD].rearrange("(j p e) -> p j e", p=P, e=P)).then_inc(near_loaded, 16)
                sp.dma_start(near[:, 1, :, :], flat[0, 2:2 + EPAD].rearrange("(j p e) -> p j e", p=P, e=P)).then_inc(near_loaded, 16)
                sp.wait_ge(dv, 12)
                sp.dma_start(c.keep_prev.rearrange("(j p) e -> p j e", p=P), near[:, 0, :, :]).then_inc(all_stored, 16)
                sp.dma_start(c.keep_next.rearrange("(j p) e -> p j e", p=P), near[:, 1, :, :]).then_inc(all_stored, 16)
                sp.dma_start(c.local_rows[0, :].rearrange("(j p e) -> p j e", p=P, e=P), local_bf[:, :, :]).then_inc(all_stored, 16)
                sp.dma_start(tiles[0, :].rearrange("(j p one) -> p j one", p=P, one=1), n_i[:, :].rearrange("p (j one) -> p j one", one=1), allow_slow_non_contiguous=True).then_inc(all_stored, 16)
                for r in range(4):
                    sp.dma_start(small[r, :].rearrange("(j p one) -> p j one", p=P, one=1), four[:, r, :].rearrange("p (j one) -> p j one", one=1), allow_slow_non_contiguous=True).then_inc(all_stored, 16)
                sp.wait_ge(all_stored, 16 * 8)
                sp.wait_ge(dv, 13)
                sp.dma_start(c.edge_src.rearrange("g p s -> p g s"), turned_src[:, :].rearrange("p (g s) -> p g s", s=G)).then_inc(by_edge_stored, 16)
                sp.dma_start(c.edge_place.rearrange("g p s -> p g s"), turned_place[:, :].rearrange("p (g s) -> p g s", s=G)).then_inc(by_edge_stored, 16)
                sp.wait_ge(by_edge_stored, 32)

            @block.gpsimd
            def _(pool):
                nc.gpsimd.iota(step_i[:, :], [[P, KC]], base=0, channel_multiplier=1).then_inc(ramp, 1)
                pool.wait_ge(dv, 5)
                for j in range(KC):
                    for which, rows in ((0, src), (1, dst)):
                        nc.gpsimd.indirect_dma_start(rows_i[:, which, j, :], None, rows,
                                                     bass.IndirectOffsetOnAxis(ap=t_i[:, j:j + 1], axis=0)).then_inc(rows_found, 16)

            @block.tensor
            def _(pe):
                pe.wait_ge(dv, 3)
                for j in range(KC):
                    last_mm = nc.tensor.matmul(c.bank[j // 4][:, (j % 4) * P:(j % 4 + 1) * P], c.ones[:, :], diag[:, j, :], start=True, stop=True)
                last_mm.then_inc(keys_spread, 1)
                pe.wait_ge(dv, 9)
                for j in range(KC):
                    nc.tensor.transpose(c.bank[j // 4][:, (j % 4) * P:(j % 4 + 1) * P], local[:, j, :], c.ident[:, :])
                    last_mm = nc.tensor.transpose(c.bank[4 + j // 4][:, (j % 4) * P:(j % 4 + 1) * P], src_f[:, j, :], c.ident[:, :])
                last_mm.then_inc(turned, 1)

            @block.vector
            def _(dve):
                v = nc.vector
                v.memset(margin[:, 0:1], -5.0)
                v.memset(margin[:, 1:2], -7.0)
                dve.wait_ge(ramp, 1)
                v.tensor_copy(step[:, :], step_i[:, :])
                dve.wait_ge(dst_loaded, 16)
                v.tensor_scalar(last[:, :], dst_in[:, :, P - 1], 7, None, ALU.arith_shift_right).then_inc(dv, 1)
                dve.wait_ge(dv, 1)
                v.tensor_tensor(key[:, :], last[:, :], step[:, :], ALU.add).then_inc(dv, 1)
                dve.wait_ge(dv, 2)
                for j in range(KC):
                    op = v.tensor_scalar(diag[:, j, :], c.ident[:, :], key[:, j:j + 1], None, ALU.mult)
                op.then_inc(dv, 1)
                dve.wait_ge(keys_spread, 1)
                for b in range(-(-KC // 4)):
                    w = min(512, K - b * 512)
                    op = v.tensor_copy(keys[:, b * 512:b * 512 + w], c.bank[b][:, 0:w])
                op.then_inc(dv, 1)
                dve.wait_ge(dv, 4)
                for j in range(KC):
                    v.tensor_scalar(below[:, :], keys[:, :], step[:, j:j + 1], 0.0, ALU.is_lt, ALU.add, accum_out=t_f[:, j:j + 1]).then_inc(told, 1)
                    dve.wait_ge(told, j + 1)
                v.tensor_copy(t_i[:, :], t_f[:, :]).then_inc(dv, 1)
                v.tensor_tensor(n_f[:, :], step[:, :], t_f[:, :], ALU.subtract).then_inc(dv, 1)
                dve.wait_ge(dv, 6)
                v.tensor_copy(n_i[:, :], n_f[:, :])
                v.tensor_scalar(n_p[:, :], n_f[:, :], float(P), None, ALU.mult)
                dve.wait_ge(rows_found, 32 * KC)
                v.tensor_copy(dst_f[:, :, :], rows_i[:, 1, :, :]).then_inc(dv, 1)
                v.tensor_copy(src_f[:, :, :], rows_i[:, 0, :, :])
                dve.wait_ge(dv, 7)
                for j in range(KC):
                    op = v.tensor_scalar(local[:, j, :], dst_f[:, j, :], n_p[:, j:j + 1], -1.0, ALU.subtract, ALU.max)
                op.then_inc(dv, 1)
                dve.wait_ge(dv, 8)
                v.tensor_scalar(local[:, :, :], local[:, :, :], float(P), None, ALU.min).then_inc(dv, 1)
                dve.wait_ge(dv, 9)
                v.tensor_copy(local_bf[:, :, :], local[:, :, :])
                v.tensor_tensor(one_seg[:, :], dst_f[:, :, 0], dst_f[:, :, P - 1], ALU.is_equal)
                v.tensor_copy(four[:, 3, :], local[:, :, 0])
                dve.wait_ge(near_loaded, 32)
                for w in range(2):
                    op = v.tensor_tensor(near[:, w, :, :], near[:, w, :, :], dst_f[:, :, :], ALU.is_equal)
                op.then_inc(dv, 1)
                dve.wait_ge(dv, 10)
                v.tensor_copy(four[:, 2, :], near[:, 0, :, 0])
                v.tensor_tensor(four[:, 0, :], near[:, 0, :, 0], one_seg[:, :], ALU.mult)
                v.tensor_tensor(four[:, 1, :], near[:, 1, :, P - 1], one_seg[:, :], ALU.mult).then_inc(dv, 1)
                dve.wait_ge(dv, 11)
                v.tensor_scalar(near[:, :, :, :], near[:, :, :, :], 1.0, BIG, ALU.subtract, ALU.mult)
                v.tensor_scalar(four[:, 0:2, :], four[:, 0:2, :], 1.0, BIG, ALU.subtract, ALU.mult).then_inc(dv, 1)
                dve.wait_ge(turned, 1)
                for b in range(-(-KC // 4)):
                    w = min(512, K - b * 512)
                    v.tensor_copy(turned_place[:, b * 512:b * 512 + w], c.bank[b][:, 0:w])
                    op = v.tensor_copy(turned_src[:, b * 512:b * 512 + w], c.bank[4 + b][:, 0:w])
                op.then_inc(dv, 1)
                dve.wait_ge(dv, 13)


class Front:

    def __init__(self, nc, ctx, tag, deep=1):
        def sb(name, shape, dt=F32):
            return ctx.enter_context(nc.sbuf_tensor(f"{name}_{tag}", shape, dt))

        def sem(name):
            return nc.alloc_semaphore(f"{name}_{tag}")

        self.x = sb("x", [P, 2, T, D])
        self.stats = sb("stats", [P, 2, T, 6])
        self.mv = sb("mv", [P, 2, T, 2])
        self.sd = sb("sd", [P, 2, T])
        self.rstd = sb("rstd", [P, 2, T])
        self.shift = sb("shift", [P, 2, T])
        self.deep = deep
        self.xn = sb("xn", [P, deep, T, D + 1])
        self.xt = sb("xt", [P, T, 2, P])
        self.loaded = [sem("x_loaded0"), sem("x_loaded1")]
        self.passed = sem("passed")
        self.stats_made, self.mv_made, self.sd_made = sem("stats_made"), sem("mv_made"), sem("sd_made")
        self.rstd_made, self.shift_made, self.xn_made = sem("rstd_made"), sem("shift_made"), sem("xn_made")
        self.turned, self.xt_made = sem("turned"), sem("xt_made")

    def load(self, sp, nc, x_dram, b, p):
        nc.sync.dma_start(self.x[:, p, :, :], x_dram.rearrange("(n p) d -> p n d", p=P)[:, bass.ds(b * T, T), :]).then_inc(self.loaded[p], 16)

    def sync(self, sp, nc, x_dram, used, store):
        for p in range(2):
            self.load(sp, nc, x_dram, p, p)
        with sp.Fori(0, NB // 2 - 1) as pair:
            for p in range(2):
                sp.wait_ge(used, 1 + (pair * 2 + p + 1) * T)
                sp.sem_inc(self.passed, 1)
                self.load(sp, nc, x_dram, pair * 2 + p + 2, p)
                store(pair * 2 + p, p)
        for p in range(2):
            store(NB - 2 + p, p)

    def vector(self, dve, nc, b, pair, p, update=None):
        dve.wait_ge(self.loaded[p], 16 * pair + 16)
        if update:
            update()
        for i in range(T):
            op = nc.vector.bn_stats(self.stats[:, p, i, :], self.x[:, p, i, :])
        op.then_inc(self.stats_made, 1)
        dve.wait_ge(self.stats_made, b + 1)
        dve.sem_inc(self.passed, 1)
        for i in range(T):
            op = nc.vector.bn_aggr(self.mv[:, p, i, :], self.stats[:, p, i, :])
        op.then_inc(self.mv_made, 1)
        dve.wait_ge(self.sd_made, b + 1)
        nc.vector.reciprocal(self.rstd[:, p, :], self.sd[:, p, :]).then_inc(self.rstd_made, 1)
        dve.wait_ge(self.rstd_made, b + 1)
        nc.vector.scalar_tensor_tensor(self.shift[:, p, :], self.mv[:, p, :, 0], -1.0, self.rstd[:, p, :], ALU.mult, ALU.mult).then_inc(self.shift_made, 1)

    def scalar(self, act, nc, c, b, p, used, also=None, more=0, free=None):
        act.wait_ge(self.mv_made, b + 1)
        nc.scalar.activation(self.sd[:, p, :], self.mv[:, p, :, 1], ACT.Sqrt, bias=c.eps[:, 0:1]).then_inc(self.sd_made, 1)
        act.wait_ge(self.shift_made, b + 1)
        act.wait_ge(used, 1 + b * T)
        if free:
            free()
        for i in range(T + 1 + more):
            if i < T:
                nc.scalar.activation(self.xn[:, p % self.deep, i, 0:D], self.x[:, p, i, :], ACT.Identity,
                                     bias=self.shift[:, p, i:i + 1], scale=self.rstd[:, p, i:i + 1]).then_inc(self.xn_made, 1)
            if 1 <= i <= T:
                act.wait_ge(self.turned, b * T + i)
                nc.scalar.copy(self.xt[:, i - 1, :, :].rearrange("p c n -> p (c n)"), c.bank[(i - 1) % 2][:, 0:D]).then_inc(self.xt_made, 1)
            if also:
                also(i)

    def tensor(self, pe, nc, c, b, p, i):
        pe.wait_ge(self.xn_made, b * T + i + 1)
        pe.wait_ge(self.xt_made, 1 + b * T + max(i - 1, 0))
        for h in range(2):
            op = nc.tensor.transpose(c.bank[i % 2][:, h * P:(h + 1) * P], self.xn[:, p % self.deep, i, h * P:(h + 1) * P], c.ident[:, :])
        op.then_inc(self.turned, 1)


def gat_project(nc, c, w):
    with ExitStack() as ctx:
        def sb(name, shape, dt=F32):
            return ctx.enter_context(nc.sbuf_tensor(name, shape, dt))

        def sem(name):
            return nc.alloc_semaphore(name)

        HW = HEADS * HC
        w_ext = sb("w_ext", [P, 2, HW + 2 * HEADS])
        w_t = sb("w_t", [P, 2, P])
        att = sb("att", [P, 2])
        att_block = sb("att_block", [P, 2 * HEADS])
        head_of = sb("head_of", [P, HEADS])
        head_lo = sb("head_lo", [P, HEADS])
        rows = sb("rows", [P, 2, T, A_ROW])
        w_loaded, w_turned, block_made, w_copied, w_folded, w_ready = (sem(s) for s in ("gp_w_loaded", "gp_w_turned", "gp_block_made", "gp_w_copied", "gp_w_folded", "gp_w_ready"))
        projected, rows_copied, rows_stored0, rows_stored1 = sem("gp_projected"), sem("gp_rows_copied"), sem("gp_rows_stored0"), sem("gp_rows_stored1")
        rows_stored = [rows_stored0, rows_stored1]
        f = Front(nc, ctx, "gp")
        with nc.Block() as block:
            @block.sync
            def _(sp):
                sp.dma_start(w_ext[:, :, 0:HW], w["L0_gnn_W"].rearrange("(c p) n -> p c n", p=P)).then_inc(w_loaded, 16)
                sp.dma_start(att[:, 0:1], w["L0_gnn_att_src"].rearrange("h (c one) -> (h c) one", one=1)).then_inc(w_loaded, 16)
                sp.dma_start(att[:, 1:2], w["L0_gnn_att_dst"].rearrange("h (c one) -> (h c) one", one=1)).then_inc(w_loaded, 16)
                for p in range(2):
                    sp.sem_inc(rows_stored[p], 16)

                def store(b, p):
                    sp.wait_ge(rows_copied, 1 + (b + 1) * T)
                    sp.sem_inc(f.passed, 1)
                    nc.sync.dma_start(c.a_table.rearrange("(n p) d -> p n d", p=P)[:, bass.ds(b * T, T), :], rows[:, p, :, :]).then_inc(rows_stored[p], 16)

                f.sync(sp, nc, c.x_in, projected, store)
                for p in range(2):
                    sp.wait_ge(rows_stored[p], 16 + 16 * (NB // 2))

            @block.vector
            def _(dve):
                prime(dve, rows_copied)
                v = nc.vector
                v.tensor_scalar(head_of[:, :], c.ramp_row[:, 0:HEADS], float(HC), None, ALU.mult).then_inc(block_made, 1)
                dve.wait_ge(block_made, 1)
                v.tensor_scalar(head_lo[:, :], head_of[:, :], c.ramp_col[:, 0:1], None, ALU.is_le)
                v.tensor_scalar(head_of[:, :], head_of[:, :], float(HC), c.ramp_col[:, 0:1], ALU.add, ALU.is_gt).then_inc(block_made, 1)
                dve.wait_ge(block_made, 2)
                v.tensor_tensor(head_of[:, :], head_of[:, :], head_lo[:, :], ALU.mult).then_inc(block_made, 1)
                dve.wait_ge(block_made, 3)
                dve.wait_ge(w_loaded, 48)
                for s in range(2):
                    op = v.tensor_scalar(att_block[:, s * HEADS:(s + 1) * HEADS], head_of[:, :], att[:, s:s + 1], None, ALU.mult)
                op.then_inc(block_made, 1)
                dve.wait_ge(w_turned, 1)
                v.tensor_copy(w_t[:, :, :].rearrange("p c n -> p (c n)"), c.bank[2][:, 0:2 * P]).then_inc(w_copied, 1)
                dve.wait_ge(w_folded, 1)
                v.tensor_copy(w_ext[:, :, HW:], c.bank[3][:, 0:4 * HEADS].rearrange("p (c n) -> p c n", c=2)).then_inc(w_ready, 1)
                with batches(dve) as pair:
                    for p in range(2):
                        b = pair * 2 + p
                        f.vector(dve, nc, b, pair, p)
                        dve.wait_ge(rows_stored[p], 16 * pair + 16)
                        for i in range(T):
                            dve.wait_ge(projected, 1 + b * T + i + 1)
                            v.tensor_copy(rows[:, p, i, :], c.bank[2 + i % 2][:, 0:A_ROW])
                            op = v.tensor_copy(c.dst_score[:, bass.ds((b * T + i) * HEADS, HEADS)], c.bank[2 + i % 2][:, A_ROW:A_ROW + HEADS])
                            op.then_inc(rows_copied, 1)

            @block.scalar
            def _(act):
                prime(act, f.xt_made)
                with batches(act) as pair:
                    for p in range(2):
                        b = pair * 2 + p
                        f.scalar(act, nc, c, b, p, projected)

            @block.tensor
            def _(pe):
                prime(pe, projected)
                pe.wait_ge(w_loaded, 48)
                for ch in range(2):
                    op = nc.tensor.transpose(c.bank[2][:, ch * P:(ch + 1) * P], w_ext[:, ch, 0:HW], c.ident[:, :])
                op.then_inc(w_turned, 1)
                pe.wait_ge(w_copied, 1)
                pe.wait_ge(block_made, 4)
                for ch in range(2):
                    op = nc.tensor.matmul(c.bank[3][:, ch * 2 * HEADS:(ch + 1) * 2 * HEADS], w_t[:, ch, :], att_block[:, :], start=True, stop=True)
                op.then_inc(w_folded, 1)
                pe.wait_ge(w_ready, 1)
                with batches(pe) as pair:
                    for p in range(2):
                        b = pair * 2 + p
                        for i in range(T + 1):
                            if i < T:
                                f.tensor(pe, nc, c, b, p, i)
                            if i >= 1:
                                k = i - 1
                                pe.wait_ge(f.xt_made, 1 + b * T + i)
                                pe.wait_ge(rows_copied, 1 + b * T + max(k - 1, 0))
                                for ch in range(2):
                                    op = nc.tensor.matmul(c.bank[2 + k % 2][:, 0:HW + 2 * HEADS], f.xt[:, k, ch, :], w_ext[:, ch, :], start=(ch == 0), stop=(ch == 1))
                                op.then_inc(projected, 1)


def edge_stage(nc, c, tag, heads, leaky, table, row, width, score_at, floor, acc):
    H, Q = heads, 4
    HS = H * G
    multi = H > 1
    with ExitStack() as ctx:
        def sb(name, shape, dt=F32):
            return ctx.enter_context(nc.sbuf_tensor(f"{tag}_{name}", shape, dt))

        def sem(name):
            return nc.alloc_semaphore(f"{tag}_{name}")

        rows = sb("rows", [P, 2, G, row])
        src_now = sb("src_now", [P, 2, G], I32)
        keep_prev = sb("keep_prev", [HS, 2, P])
        keep_next = sb("keep_next", [HS, 2, P])
        place = sb("place", [P, 2, G])
        step_rows = sb("step_rows", [1, 2, 4, G])
        tile_now = sb("tile_now", [1, 2, G], I32)
        place_row = sb("place_row", [1, 2, G * P], BF16)
        away = sb("away", [P, 2, Q * P])
        node_of = sb("node_of", [P, 2, Q * P])
        z = sb("z", [P, HS])
        zt = sb("zt", [HS, P])
        zf = sb("zf", [HS, P])
        scan0 = sb("scan0", [HS, P])
        fwd = sb("fwd", [HS, P])
        scan1 = sb("scan1", [HS, P])
        top = sb("top", [HS, P])
        diff = sb("diff", [HS, P])
        ex = sb("ex", [HS, P])
        fm = sb("fm", [HS, P])
        ends = sb("ends", [HS, 2])
        pen_f = sb("pen_f", [1, H, G + 1])
        pen_b = sb("pen_b", [1, H, G + 1])
        in_f = sb("in_f", [1, H, G + 1])
        in_b = sb("in_b", [1, H, G + 1])
        out_f = sb("out_f", [1, H, G + 1])
        out_b = sb("out_b", [1, H, G + 1])
        start_f = sb("start_f", [1, HS])
        start_b = sb("start_b", [1, HS])
        drop = sb("drop", [1, H])
        first = sb("first", [1, P])
        dropped_by = sb("dropped_by", [P, H])
        scale = sb("scale", [P, H])
        weight = sb("weight", [P, 2 * H, G])
        hot = sb("hot", [P, 2, Q, P])
        msg = sb("msg", [P, 2, Q, width]) if multi else None
        gathered = [sem("gathered0"), sem("gathered1")]
        kept = [sem("kept0"), sem("kept1")]
        placed = [sem("placed0"), sem("placed1")]
        src_staged = [sem("src_staged0"), sem("src_staged1")]
        passed, passed_sp, passed_pe = sem("passed"), sem("passed_sp"), sem("passed_pe")
        place_spread, node_of_made, scored = sem("place_spread"), sem("node_of_made"), sem("scored")
        z_made, z_turned, zt_made, scan0_made, row_f, start_f_made, col_f, ends_f = (sem(s) for s in (
            "z_made", "z_turned", "zt_made", "scan0_made", "row_f", "start_f_made", "col_f", "ends_f"))
        fwd_made, scan1_made, row_b, start_b_made, col_b, ends_b, top_made, diff_made = (sem(s) for s in (
            "fwd_made", "scan1_made", "row_b", "start_b_made", "col_b", "ends_b", "top_made", "diff_made"))
        ex_made, fm_made, weight_turned, weight_made, dropped, scale_made = (sem(s) for s in (
            "ex_made", "fm_made", "weight_turned", "weight_made", "dropped", "scale_made"))
        in_f_made, out_f_made, in_b_made, out_b_made, diff0, rescaled = (sem(s) for s in (
            "in_f_made", "out_f_made", "in_b_made", "out_b_made", "diff0", "rescaled"))
        hot_made, msg_made, msg_w_made, summed, added = (sem(s) for s in ("hot_made", "msg_made", "msg_w_made", "summed", "added"))
        set_up, away_made = sem("set_up"), sem("away_made")

        spread_bank = [c.bank[0], c.bank[1]]
        s_bank, t_bank = c.bank[2], c.bank[3]
        ring = c.bank[4:8]
        w_cols, row_cols, col_cols = s_bank[:, P:P + 2 * HS], t_bank, t_bank


        def tiles_now(engine, p, k, count):
            return nc.values_load_multi_w_load_instructions(tile_now[0:1, p, k:k + count], engines=[engine], min_val=0, max_val=NT - 1)[1]

        with nc.Block() as block:
            @block.sync
            def _(sp):
                def load(g, p):
                    for h in range(H):
                        nc.sync.dma_start(keep_prev[h * G:(h + 1) * G, p, :], c.keep_prev[bass.ds(g * G, G), :]).then_inc(kept[p], 16)
                        nc.sync.dma_start(keep_next[h * G:(h + 1) * G, p, :], c.keep_next[bass.ds(g * G, G), :]).then_inc(kept[p], 16)
                    nc.sync.dma_start(src_now[:, p, :], c.edge_src[bass.ds(g, 1), :, :].rearrange("g p s -> (g p) s")).then_inc(src_staged[p], 16)
                    nc.sync.dma_start(place_row[:, p, :], c.local_rows[:, bass.ds(g * G * P, G * P)]).then_inc(placed[p], 16)
                    nc.sync.dma_start(place[:, p, :], c.edge_place[bass.ds(g, 1), :, :].rearrange("g p s -> (g p) s")).then_inc(placed[p], 16)
                    nc.sync.dma_start(tile_now[:, p, :], c.step_tiles[:, bass.ds(g * G, G)]).then_inc(placed[p], 16)
                    nc.sync.dma_start(step_rows[:, p, :, :], c.step_rows[:, bass.ds(g * G, G)].rearrange("(o r) k -> o r k", o=1)).then_inc(placed[p], 16)

                for p in range(2):
                    load(p, p)
                with sp.Fori(0, NG // 2 - 1) as pair:
                    for p in range(2):
                        g = pair * 2 + p
                        sp.wait_ge(added, 1 + (g + 1) * G)
                        sp.sem_inc(passed_sp, 1)
                        load(g + 2, p)

            @block.gpsimd
            def _(pool):
                def gather(p, n, used=None):
                    pool.wait_ge(src_staged[p], 16 * n + 16)
                    pool.sem_inc(passed, 1)
                    for s in range(G):
                        if used is not None and s % Q == 0:
                            pool.wait_ge(summed, 1 + used + s + Q)
                            pool.sem_inc(passed, 1)
                        nc.gpsimd.indirect_dma_start(rows[:, p, s, :], None, table,
                                                     bass.IndirectOffsetOnAxis(ap=src_now[:, p, s:s + 1], axis=0)).then_inc(gathered[p], 16)

                for p in range(2):
                    gather(p, 0)
                with pool.Fori(0, NG // 2 - 1) as pair:
                    for p in range(2):
                        gather(p, pair + 1, (pair * 2 + p) * G)

            @block.vector
            def _(dve):
                prime(dve, z_made, added, rescaled)
                v = nc.vector
                v.memset(pen_f[:, :, 0:1], -BIG)
                v.memset(pen_b[:, :, G:G + 1], -BIG)
                v.memset(in_b[:, :, G:G + 1], -BIG)
                v.memset(out_f[:, :, :], 0.0)
                v.memset(acc[:, :], 0.0).then_inc(set_up, 1)
                dve.wait_ge(set_up, 1)
                with groups(dve) as pair:
                    for p in range(2):
                        g = pair * 2 + p
                        dve.wait_ge(scored, (g + 1) * (G // Q))
                        dve.wait_ge(gathered[p], (pair + 1) * 16 * G)
                        dve.wait_ge(z_turned, 1 + g)
                        v.tensor_tensor(z[:, :].rearrange("e (h s) -> e s h", h=H), rows[:, p, :, score_at:score_at + H],
                                        s_bank[:, 0:HS].rearrange("e (s h) -> e s h", h=H), ALU.add).then_inc(z_made, 1)
                        if leaky:
                            dve.wait_ge(z_made, 1 + 2 * g + 1)
                            v.scalar_tensor_tensor(z[:, :], z[:, :], leaky, z[:, :], ALU.mult, ALU.max).then_inc(z_made, 1)
                        dve.wait_ge(placed[p], 64 * (pair + 1))
                        v.tensor_copy(pen_f[:, :, 1:], step_rows[:, p, 0:1, :].broadcast_to([1, H, G]))
                        v.tensor_copy(pen_b[:, :, 0:G], step_rows[:, p, 1:2, :].broadcast_to([1, H, G]))
                        v.tensor_copy(in_f[:, :, 0:1], out_f[:, :, G:G + 1])
                        v.tensor_scalar(first[:, :], c.ramp_row[0:1, :], step_rows[:, p, 3, 0:1], None, ALU.is_equal)
                        dve.wait_ge(z_turned, 1 + g + 1)
                        v.tensor_copy(zt[:, :], t_bank[0:HS, 0:P]).then_inc(zt_made, 1)
                        dve.wait_ge(zt_made, g + 1)
                        v.tensor_scalar(zf[:, :], zt[:, :], floor, None, ALU.max).then_inc(diff0, 1)
                        dve.wait_ge(kept[p], (pair + 1) * 32 * H)
                        dve.wait_ge(diff0, 3 * g + 1)
                        v.tensor_tensor_scan(scan0[:, :], keep_prev[:, p, :], zf[:, :], -BIG, ALU.add, ALU.max).then_inc(scan0_made, 1)
                        dve.wait_ge(row_f, g + 1)
                        v.tensor_copy(in_f[:, :, 1:], t_bank[0:1, P:P + HS].rearrange("o (h s) -> o h s", h=H)).then_inc(in_f_made, 1)
                        dve.wait_ge(in_f_made, g + 1)
                        v.tensor_tensor_scan(out_f[:, :, :].rearrange("o h s -> o (h s)"), pen_f[:, :, :].rearrange("o h s -> o (h s)"),
                                             in_f[:, :, :].rearrange("o h s -> o (h s)"), -BIG, ALU.add, ALU.max).then_inc(out_f_made, 1)
                        dve.wait_ge(out_f_made, g + 1)
                        v.tensor_copy(start_f[:, :].rearrange("o (h s) -> o h s", h=H), out_f[:, :, 0:G]).then_inc(start_f_made, 1)
                        dve.wait_ge(col_f, g + 1)
                        v.tensor_copy(ends[:, 0:1], t_bank[0:HS, 2 * P:2 * P + 1]).then_inc(ends_f, 1)
                        dve.wait_ge(ends_f, g + 1)
                        v.tensor_tensor_scan(fwd[:, :], keep_prev[:, p, :], zf[:, :], ends[:, 0:1], ALU.add, ALU.max).then_inc(fwd_made, 1)
                        dve.wait_ge(fwd_made, g + 1)
                        v.tensor_tensor_scan(scan1[:, ::-1], keep_next[:, p, ::-1], fwd[:, ::-1], -BIG, ALU.add, ALU.max).then_inc(scan1_made, 1)
                        dve.wait_ge(row_b, g + 1)
                        v.tensor_copy(in_b[:, :, 0:G], t_bank[0:1, P:P + HS].rearrange("o (h s) -> o h s", h=H)).then_inc(in_b_made, 1)
                        dve.wait_ge(in_b_made, g + 1)
                        v.tensor_tensor_scan(out_b[:, :, :].rearrange("o h s -> o (h s)")[:, ::-1], pen_b[:, :, :].rearrange("o h s -> o (h s)")[:, ::-1],
                                             in_b[:, :, :].rearrange("o h s -> o (h s)")[:, ::-1], -BIG, ALU.add, ALU.max).then_inc(out_b_made, 1)
                        dve.wait_ge(out_b_made, g + 1)
                        v.tensor_tensor(drop[:, :], out_f[:, :, 0], out_b[:, :, 0], ALU.subtract).then_inc(diff0, 1)
                        v.tensor_copy(start_b[:, :].rearrange("o (h s) -> o h s", h=H), out_b[:, :, 1:]).then_inc(start_b_made, 1)
                        dve.wait_ge(diff0, 3 * g + 2)
                        v.tensor_scalar(drop[:, :], drop[:, :], step_rows[:, p, 2, 0:1], None, ALU.mult).then_inc(dropped, 1)
                        dve.wait_ge(col_b, g + 1)
                        v.tensor_copy(dropped_by[:, :], t_bank[:, 2 * P + 4:2 * P + 4 + H])
                        v.tensor_copy(ends[:, 1:2], t_bank[0:HS, 2 * P + 2:2 * P + 3]).then_inc(ends_b, 1)
                        dve.wait_ge(ends_b, g + 1)
                        v.tensor_tensor_scan(top[:, ::-1], keep_next[:, p, ::-1], fwd[:, ::-1], ends[:, 1:2], ALU.add, ALU.max).then_inc(top_made, 1)
                        dve.wait_ge(top_made, g + 1)
                        v.tensor_tensor(diff[:, :], zt[:, :], top[:, :], ALU.subtract).then_inc(diff_made, 1)
                        if multi:
                            v.scalar_tensor_tensor(fm[:, :], keep_prev[:, p, :], -1.0 / BIG, top[:, :], ALU.mult, ALU.mult).then_inc(fm_made, 1)
                        v.sem_inc(diff0, 1)
                        n = tiles_now(mybir.EngineType.DVE, p, 0, 1)[0]
                        dve.wait_ge(scale_made, g + 1)
                        dve.wait_ge(added, 1 + g * G)
                        if multi:
                            cols = acc[:, bass.ds(n * width, HEADS * HC)].rearrange("p (h c) -> p h c", h=H)
                            v.tensor_tensor(cols, cols, scale[:, :].rearrange("p (h o) -> p h o", o=1).broadcast_to([P, H, HC]), ALU.mult)
                            v.tensor_tensor(acc[:, bass.ds(n * width + HEADS * HC, H)], acc[:, bass.ds(n * width + HEADS * HC, H)], scale[:, :], ALU.mult)
                            v.tensor_tensor(acc[:, bass.ds(n * width + A_ROW, H)], acc[:, bass.ds(n * width + A_ROW, H)],
                                            dropped_by[:, :], ALU.subtract).then_inc(rescaled, 1)
                        else:
                            v.tensor_scalar(acc[:, bass.ds(n * width, width)], acc[:, bass.ds(n * width, width)], scale[:, 0:1], None, ALU.mult).then_inc(rescaled, 1)
                        dve.wait_ge(weight_made, g + 1)

                        def prepare(q, s):
                            k = q * Q + s
                            if multi:
                                one_hot = v.tensor_scalar(hot[:, q % 2, s, :], c.ramp_row[:, :], place[:, p, k:k + 1], None, ALU.is_equal)
                                message = v.tensor_tensor(msg[:, q % 2, s, 0:HEADS * HC].rearrange("p (h c) -> p h c", h=H),
                                                          rows[:, p, k, 0:HEADS * HC].rearrange("p (h c) -> p h c", h=H),
                                                          weight[:, 0:H, k:k + 1].broadcast_to([P, H, HC]), ALU.mult)
                            else:
                                one_hot = v.tensor_scalar(hot[:, q % 2, s, :], c.ramp_row[:, :], place[:, p, k:k + 1], weight[:, 0, k:k + 1], ALU.is_equal, ALU.mult)
                            if s == Q - 1:
                                one_hot.then_inc(hot_made, 1)
                                if multi:
                                    message.then_inc(msg_made, 1)

                        for q in range(2):
                            for s in range(Q):
                                prepare(q, s)
                        for q in range(G // Q):
                            node_tile = tiles_now(mybir.EngineType.DVE, p, q * Q, Q)
                            for s in range(Q):
                                k, n = q * Q + s, node_tile[s]
                                dve.wait_ge(added, 1 + g * G + k) if k else dve.wait_ge(rescaled, 1 + g + 1)
                                dve.wait_ge(summed, 1 + g * G + k + 1)
                                v.tensor_tensor(acc[:, bass.ds(n * width, width)], acc[:, bass.ds(n * width, width)], ring[s][:, 0:width], ALU.add).then_inc(added, 1)
                                if q + 2 < G // Q:
                                    prepare(q + 2, s)

            @block.scalar
            def _(act):
                prime(act, node_of_made)

                def node_one_hots(g, q):
                    act.wait_ge(place_spread, g * (G // Q) + q + 1)
                    nc.scalar.activation(away[:, q % 2, :], spread_bank[q % 2][:, :], ACT.Abs, bias=c.minus_ramp[:, 0:1]).then_inc(away_made, 1)
                    act.wait_ge(away_made, g * (G // Q) + q + 1)
                    nc.scalar.activation(node_of[:, q % 2, :], away[:, q % 2, :], ACT.Relu, bias=c.ones[:, 0:1], scale=-1.0).then_inc(node_of_made, 1)

                def group(g, p, more):
                    act.wait_ge(ends_b, g + 1)
                    act.wait_ge(rescaled, 1 + g)
                    nc.scalar.activation(scale[:, :], dropped_by[:, :], ACT.Exp).then_inc(scale_made, 1)
                    act.wait_ge(diff_made, g + 1)
                    act.wait_ge(weight_turned, 1 + g)
                    nc.scalar.activation(ex[:, :], diff[:, :], ACT.Exp).then_inc(ex_made, 1)
                    act.wait_ge(weight_turned, 1 + g + 1)
                    act.wait_ge(summed, 1 + g * G)
                    nc.scalar.copy(weight[:, 0:(2 * H if multi else H), :].rearrange("e h s -> e (h s)"), s_bank[:, P:P + (2 * HS if multi else HS)]).then_inc(weight_made, 1)
                    act.wait_ge(weight_made, g + 1)
                    for q in range(G // Q):
                        if multi:
                            act.wait_ge(summed, 1 + g * G + max(Q * (q - 1), 0))
                            nc.scalar.copy(msg[:, q % 2, :, HEADS * HC:].rearrange("p s h -> p h s"), weight[:, :, q * Q:(q + 1) * Q]).then_inc(msg_w_made, 1)
                        if more:
                            node_one_hots(g + 1, q)

                for q in range(G // Q):
                    node_one_hots(0, q)
                with act.Fori(0, NG // 2 - 1) as pair:
                    for p in range(2):
                        group(pair * 2 + p, p, True)
                for p in range(2):
                    group(NG - 2 + p, p, p == 0)

            @block.tensor
            def _(pe):
                prime(pe, z_turned, summed, weight_turned)

                def score_quad(g, q, p):
                    if q < G // Q:
                        pe.wait_ge(node_of_made, 1 + g * (G // Q) + max(q - 1, 0))
                        nc.tensor.matmul(spread_bank[q % 2][:, :], c.ones_bf[0:1, :], place_row[:, p, q * Q * P:(q + 1) * Q * P], start=True, stop=True).then_inc(place_spread, 1)
                    if q >= 1:
                        node_tile = tiles_now(mybir.EngineType.PE, p, (q - 1) * Q, Q)
                        pe.wait_ge(node_of_made, 1 + g * (G // Q) + q)
                        for s in range(Q):
                            k, n = (q - 1) * Q + s, node_tile[s]
                            op = nc.tensor.matmul(s_bank[:, k * H:(k + 1) * H], node_of[:, (q - 1) % 2, s * P:(s + 1) * P],
                                                  c.dst_score[:, bass.ds(n * H, H)], start=True, stop=True)
                        op.then_inc(scored, 1)

                def group(g, p, more, next_placed):
                    pe.wait_ge(z_made, 1 + (2 if leaky else 1) * (g + 1))
                    pe.wait_ge(rescaled, 1 + g)
                    nc.tensor.transpose(t_bank[0:HS, 0:P], z[:, :], c.ident[:, :]).then_inc(z_turned, 1)
                    pe.wait_ge(scan0_made, g + 1)
                    pe.sem_inc(passed_pe, 1)
                    nc.tensor.transpose(t_bank[0:1, P:P + HS], scan0[:, P - 1:P], c.ident[0:HS, 0:HS]).then_inc(row_f, 1)
                    pe.wait_ge(start_f_made, g + 1)
                    pe.sem_inc(passed_pe, 1)
                    nc.tensor.matmul(t_bank[0:HS, 2 * P:2 * P + 1], start_f[:, :], c.ones[0:1, 0:1], start=True, stop=True).then_inc(col_f, 1)
                    pe.wait_ge(scan1_made, g + 1)
                    pe.sem_inc(passed_pe, 1)
                    nc.tensor.transpose(t_bank[0:1, P:P + HS], scan1[:, 0:1], c.ident[0:HS, 0:HS]).then_inc(row_b, 1)
                    pe.wait_ge(start_b_made, g + 1)
                    pe.wait_ge(dropped, g + 1)
                    pe.sem_inc(passed_pe, 1)
                    nc.tensor.matmul(t_bank[0:HS, 2 * P + 2:2 * P + 3], start_b[:, :], c.ones[0:1, 0:1], start=True, stop=True)
                    nc.tensor.matmul(t_bank[:, 2 * P + 4:2 * P + 4 + H], first[:, :], drop[:, :], start=True, stop=True).then_inc(col_b, 1)
                    pe.wait_ge(ex_made, g + 1)
                    pe.sem_inc(passed_pe, 1)
                    op = nc.tensor.transpose(s_bank[:, P:P + HS], ex[:, :], c.ident[0:HS, 0:HS])
                    if multi:
                        pe.wait_ge(fm_made, g + 1)
                        pe.sem_inc(passed_pe, 1)
                        op = nc.tensor.transpose(s_bank[:, P + HS:P + 2 * HS], fm[:, :], c.ident[0:HS, 0:HS])
                    op.then_inc(weight_turned, 1)
                    if more:
                        pe.wait_ge(placed[1 - p], next_placed)
                        pe.sem_inc(passed_pe, 1)
                    for k in range(G):
                        if k % Q == 0:
                            pe.wait_ge(hot_made, g * (G // Q) + k // Q + 1)
                            if multi:
                                pe.wait_ge(msg_made, g * (G // Q) + k // Q + 1)
                                pe.wait_ge(msg_w_made, g * (G // Q) + k // Q + 1)
                        if k >= Q:
                            pe.wait_ge(added, 1 + g * G + k - Q + 1)
                        else:
                            pe.wait_ge(added, 1 + g * G)
                        rhs = msg[:, k // Q % 2, k % Q, :] if multi else rows[:, p, k, 0:width]
                        nc.tensor.matmul(ring[k % Q][:, 0:width], hot[:, k // Q % 2, k % Q, :], rhs, start=True, stop=True).then_inc(summed, 1)
                        if more and k % Q == Q - 1:
                            score_quad(g + 1, k // Q, 1 - p)
                    if more:
                        score_quad(g + 1, G // Q, 1 - p)

                pe.wait_ge(placed[0], 64)
                for q in range(G // Q + 1):
                    score_quad(0, q, 0)
                with pe.Fori(0, NG // 2 - 1) as pair:
                    group(pair * 2, 0, True, 64 * (pair + 1))
                    group(pair * 2 + 1, 1, True, 64 * (pair + 2))
                group(NG - 2, 0, True, 32 * NG)
                group(NG - 1, 1, False, None)


def spread_row(w_row, n):
    return w_row.rearrange("(one n) -> one n", one=1).broadcast_to([P, n])


def tiles_of(dram_ap, b):
    return dram_ap.rearrange("(n p) d -> p n d", p=P)[:, bass.ds(b * T, T), :]


def gat_finish(nc, c, w, acc):
    with ExitStack() as ctx:
        def sb(name, shape, dt=F32):
            return ctx.enter_context(nc.sbuf_tensor(f"gf_{name}", shape, dt))

        def sem(name):
            return nc.alloc_semaphore(f"gf_{name}")

        HW = HEADS * HC
        x = sb("x", [P, 2, T, D])
        h = sb("h", [P, 2, T, A_ROW])
        x_new = sb("x_new", [P, 2, T, D])
        wp = sb("wp", [P, D])
        bias = sb("bias", [P, HW])
        bp = sb("bp", [P, D])
        own = sb("own", [P, T, HEADS])
        top = sb("top", [P, T, HEADS])
        both = sb("both", [P, T, HEADS])
        gap = sb("gap", [P, 2, T, HEADS])
        factor = sb("factor", [P, 2, T, HEADS])
        den = sb("den", [P, T, HEADS])
        part = sb("part", [P, T, HW])
        o = sb("o", [P, T, HW])
        ot = sb("ot", [P, T, HW])
        loaded = [sem("loaded0"), sem("loaded1")]
        stored = [sem("stored0"), sem("stored1")]
        w_loaded, dv, gap_made, factor_made, o_made, turned, ot_made, projected, added, x_made = (sem(s) for s in (
            "w_loaded", "dv", "gap_made", "factor_made", "o_made", "turned", "ot_made", "projected", "added", "x_made"))
        V = 8
        passed = nc.alloc_semaphore("passed")
        with nc.Block() as block:
            @block.sync
            def _(sp):
                sp.dma_start(wp[:, :], w["L0_gnn_Wp"]).then_inc(w_loaded, 16)
                sp.dma_start(bias[:, :], spread_row(w["L0_gnn_bias"], HW)).then_inc(w_loaded, 16)
                sp.dma_start(bp[:, :], spread_row(w["L0_gnn_bp"], D)).then_inc(w_loaded, 16)
                for p in range(2):
                    sp.sem_inc(stored[p], 16)

                def load(b, p):
                    nc.sync.dma_start(x[:, p, :, :], tiles_of(c.x_in, b)).then_inc(loaded[p], 16)
                    nc.sync.dma_start(h[:, p, :, :], tiles_of(c.a_table, b)).then_inc(loaded[p], 16)

                def store(b, p):
                    sp.wait_ge(x_made, b + 1)
                    sp.sem_inc(passed, 1)
                    nc.sync.dma_start(tiles_of(c.x1, b), x_new[:, p, :, :]).then_inc(stored[p], 16)

                for p in range(2):
                    load(p, p)
                with sp.Fori(0, NB // 2 - 1) as pair:
                    for p in range(2):
                        b = pair * 2 + p
                        store(b, p)
                        load(b + 2, p)
                for p in range(2):
                    store(NB - 2 + p, p)
                for p in range(2):
                    sp.wait_ge(stored[p], 16 + 16 * (NB // 2))

            @block.vector
            def _(dve):
                prime(dve, added)
                v = nc.vector
                dve.wait_ge(w_loaded, 48)
                with batches(dve) as pair:
                    for p in range(2):
                        b = pair * 2 + p
                        sums = acc[:, bass.ds(b * T * A_ACC, T * A_ACC)].rearrange("p (t k) -> p t k", t=T)
                        score = c.dst_score[:, bass.ds(b * T * HEADS, T * HEADS)].rearrange("p (t k) -> p t k", t=T)
                        dve.wait_ge(loaded[p], 32 * pair + 32)

                        def chain(op, n):
                            op.then_inc(dv, 1)
                            dve.wait_ge(dv, b * V + n)

                        v.tensor_tensor(own[:, :, :], h[:, p, :, HW:A_ROW], score, ALU.add)
                        chain(v.tensor_scalar(top[:, :, :], sums[:, :, HW:A_ROW], 0.0, -BIG, ALU.is_equal, ALU.mult), 1)
                        v.scalar_tensor_tensor(own[:, :, :], own[:, :, :], 0.2, own[:, :, :], ALU.mult, ALU.max)
                        chain(v.tensor_tensor(top[:, :, :], top[:, :, :], sums[:, :, A_ROW:A_ACC], ALU.add), 2)
                        chain(v.tensor_tensor(both[:, :, :], top[:, :, :], own[:, :, :], ALU.max), 3)
                        v.tensor_tensor(gap[:, 0, :, :], top[:, :, :], both[:, :, :], ALU.subtract)
                        v.tensor_tensor(gap[:, 1, :, :], own[:, :, :], both[:, :, :], ALU.subtract).then_inc(gap_made, 1)
                        dve.wait_ge(factor_made, b + 1)
                        o4 = o[:, :, :].rearrange("p t (h c) -> p t h c", h=HEADS)
                        part4 = part[:, :, :].rearrange("p t (h c) -> p t h c", h=HEADS)

                        def wide(ap, i):
                            return ap[:, i, :].rearrange("p (h one) -> p h one", one=1).broadcast_to([P, HEADS, HC])

                        dve.wait_ge(turned, 1 + b * T)
                        for i in range(T):
                            v.tensor_tensor(o4[:, i, :, :], sums[:, i, 0:HW].rearrange("p (h c) -> p h c", h=HEADS), wide(factor[:, 0], i), ALU.mult)
                            v.tensor_tensor(part4[:, i, :, :], h[:, p, i, 0:HW].rearrange("p (h c) -> p h c", h=HEADS), wide(factor[:, 1], i), ALU.mult)
                        chain(v.tensor_tensor(den[:, :, :], sums[:, :, HW:A_ROW], factor[:, 0, :, :], ALU.mult), 4)
                        chain(v.tensor_tensor(den[:, :, :], den[:, :, :], factor[:, 1, :, :], ALU.add), 5)
                        v.tensor_tensor(o[:, :, :], o[:, :, :], part[:, :, :], ALU.add)
                        chain(v.tensor_scalar(den[:, :, :], den[:, :, :], 1e-16, None, ALU.add), 6)
                        chain(v.reciprocal(den[:, :, :], den[:, :, :]), 7)
                        for i in range(T):
                            op = v.tensor_tensor(o4[:, i, :, :], o4[:, i, :, :], wide(den, i), ALU.mult)
                        chain(op, 8)
                        for i in range(T):
                            v.tensor_tensor(o[:, i, :], o[:, i, :], bias[:, :], ALU.add).then_inc(o_made, 1)
                        dve.wait_ge(stored[p], 16 * pair + 16)
                        for i in range(T):
                            dve.wait_ge(projected, 1 + b * T + i + 1)
                            op = v.tensor_tensor(x_new[:, p, i, :], c.bank[2 + i % 2][:, 0:D], x[:, p, i, :], ALU.add)
                            op.then_inc(added, 1)
                        dve.wait_ge(added, 1 + (b + 1) * T)
                        for i in range(T):
                            op = v.tensor_tensor(x_new[:, p, i, :], x_new[:, p, i, :], bp[:, :], ALU.add)
                        op.then_inc(x_made, 1)

            @block.scalar
            def _(act):
                prime(act, ot_made)
                with batches(act) as pair:
                    for p in range(2):
                        b = pair * 2 + p
                        act.wait_ge(gap_made, b + 1)
                        nc.scalar.activation(factor[:, :, :, :], gap[:, :, :, :], ACT.Exp).then_inc(factor_made, 1)
                        act.wait_ge(projected, 1 + b * T)
                        for i in range(T):
                            act.wait_ge(turned, 1 + b * T + i + 1)
                            nc.scalar.copy(ot[:, i, :], c.bank[i % 2][:, 0:HW]).then_inc(ot_made, 1)

            @block.tensor
            def _(pe):
                prime(pe, turned, projected)
                pe.wait_ge(w_loaded, 48)
                with batches(pe) as pair:
                    for p in range(2):
                        b = pair * 2 + p
                        for i in range(T + 1):
                            if i < T:
                                pe.wait_ge(o_made, b * T + i + 1)
                                pe.wait_ge(ot_made, 1 + b * T + max(i - 1, 0))
                                nc.tensor.transpose(c.bank[i % 2][:, 0:HW], o[:, i, :], c.ident[:, :]).then_inc(turned, 1)
                            if i >= 1:
                                k = i - 1
                                pe.wait_ge(ot_made, 1 + b * T + i)
                                pe.wait_ge(added, 1 + b * T + max(k - 1, 0))
                                nc.tensor.matmul(c.bank[2 + k % 2][:, 0:D], ot[:, k, :], wp[:, :], start=True, stop=True).then_inc(projected, 1)


def slice_tokens(nc, c, w, pooled_out):
    with ExitStack() as ctx:
        def sb(name, shape, dt=F32):
            return ctx.enter_context(nc.sbuf_tensor(f"st_{name}", shape, dt))

        def sem(name):
            return nc.alloc_semaphore(f"st_{name}")

        NBK = INNER // P
        f = Front(nc, ctx, "st")
        wx = sb("wx", [P, 2, INNER])
        wx_t = sb("wx_t", [P, NBK, D])
        pair_slice = sb("pair_slice", [P, P])
        bx = sb("bx", [P, NBK])
        rows = sb("rows", [1, 4, INNER])
        temp = sb("temp", [1, FH])
        wc = sb("wc", [P, 2, INNER])
        inv_temp = sb("inv_temp", [P, INNER])
        brow = sb("brow", [P, INNER])
        lg = sb("lg", [P, 2, INNER])
        mx = sb("mx", [P, 2, FH])
        e = sb("e", [P, 2, INNER])
        total = sb("total", [P, 2, FH])
        inv = sb("inv", [P, 2, FH])
        sw = sb("sw", [P, 2, INNER])
        swt = sb("swt", [P, 2, T, INNER])
        zeros = sb("zeros", [P, P])
        zero_rows = sb("zero_rows", [P, D + 1])
        stored = [sem("stored0"), sem("stored1")]
        w_loaded, dv, pe_prep, logits, lg_made, mx_made, sub_made, e_made, total_made, inv_made, inv_masked, sw_made, pooled, sw_turned, swt_made = (sem(s) for s in (
            "w_loaded", "dv", "pe_prep", "logits", "lg_made", "mx_made", "sub_made", "e_made", "total_made", "inv_made", "inv_masked", "sw_made", "pooled", "sw_turned", "swt_made"))
        with nc.Block() as block:
            @block.sync
            def _(sp):
                sp.wait_ge(dv, 1)
                sp.dma_start(wx[:, :, :], w["L0_ffn_W_x"].rearrange("(c p) n -> p c n", p=P)).then_inc(w_loaded, 16)
                for h in range(2):
                    sp.dma_start(pair_slice[h * FG:(h + 1) * FG, h * FG:(h + 1) * FG], w["L0_ffn_W_slice"]).then_inc(w_loaded, 16)
                sp.dma_start(bx[:, :], w["L0_ffn_b_x"].rearrange("(k p) -> p k", p=P), allow_slow_non_contiguous=True).then_inc(w_loaded, 16)
                for h in range(FH):
                    sp.dma_start(rows[:, 1, h * FG:(h + 1) * FG], w["L0_ffn_b_slice"].rearrange("(one n) -> one n", one=1)).then_inc(w_loaded, 16)
                sp.dma_start(temp[:, :], w["L0_ffn_temperature"].rearrange("a h b c -> (a b c) h")).then_inc(w_loaded, 16)
                for p in range(2):
                    sp.sem_inc(stored[p], 16)

                def store(b, p):
                    sp.wait_ge(swt_made, 1 + (b + 1) * T)
                    sp.sem_inc(f.passed, 1)
                    nc.sync.dma_start(c.swt.rearrange("n p k -> p n k")[:, bass.ds(b * T, T), :], swt[:, p, :, :]).then_inc(stored[p], 16)

                f.sync(sp, nc, c.x1, pooled, store)
                for p in range(2):
                    sp.wait_ge(stored[p], 16 + 16 * (NB // 2))

            @block.tensor
            def _(pe):
                prime(pe, sw_turned, pooled)
                pe.wait_ge(w_loaded, 16 * 13)
                for k in range(NBK):
                    for ch in range(2):
                        op = nc.tensor.transpose(c.bank[k][:, ch * P:(ch + 1) * P], wx[:, ch, k * P:(k + 1) * P], c.ident[:, :])
                op.then_inc(pe_prep, 1)
                pe.wait_ge(dv, 3)
                for k in range(NBK):
                    for ch in range(2):
                        nc.tensor.matmul(c.bank[ch][:, k * P:(k + 1) * P], wx_t[:, k, ch * P:(ch + 1) * P], pair_slice[:, :], start=True, stop=True)
                    nc.tensor.matmul(c.bank[2][0:1, k * P:(k + 1) * P], bx[:, k:k + 1], pair_slice[:, :], start=True, stop=True)
                nc.tensor.matmul(c.bank[3][:, :], c.ones[0:1, :], rows[:, 0, :], start=True, stop=True).then_inc(pe_prep, 1)
                pe.wait_ge(dv, 6)
                nc.tensor.matmul(c.bank[3][:, :], c.ones[0:1, :], rows[:, 3, :], start=True, stop=True).then_inc(pe_prep, 1)
                for k in range(NBK):
                    nc.tensor.matmul(c.bank[4 + k][:, 0:D + 1], zeros[:, :], zero_rows[:, :], start=True, stop=False, skip_group_check=True)
                pe.wait_ge(dv, 7)
                with batches(pe) as pair:
                    for p in range(2):
                        b = pair * 2 + p
                        for i in range(T + 3):
                            if i < T:
                                f.tensor(pe, nc, c, b, p, i)
                            if 1 <= i <= T:
                                k = i - 1
                                pe.wait_ge(f.xt_made, 1 + b * T + i)
                                pe.wait_ge(lg_made, 1 + b * T + k)
                                for ch in range(2):
                                    op = nc.tensor.matmul(c.bank[2][:, :], f.xt[:, k, ch, :], wc[:, ch, :], start=(ch == 0), stop=(ch == 1))
                                op.then_inc(logits, 1)
                            if i >= 3:
                                k = i - 3
                                pe.wait_ge(sw_made, 1 + b * T + k + 1)
                                for q in range(NBK):
                                    op = nc.tensor.matmul(c.bank[4 + q][:, 0:D + 1], sw[:, k % 2, q * P:(q + 1) * P], f.xn[:, 0, k, :], start=False, stop=True, skip_group_check=True)
                                op.then_inc(pooled, 1)
                                pe.wait_ge(swt_made, 1 + b * T + k)
                                for q in range(NBK):
                                    op = nc.tensor.transpose(c.bank[3][:, q * P:(q + 1) * P], sw[:, k % 2, q * P:(q + 1) * P], c.ident[:, :])
                                op.then_inc(sw_turned, 1)

            @block.vector
            def _(dve):
                prime(dve, lg_made, sw_made)
                v = nc.vector
                v.memset(zeros[:, :], 0.0)
                v.memset(zero_rows[:, :], 0.0)
                v.memset(f.xn[:, 0, :, D:D + 1], 1.0)
                v.memset(pair_slice[:, :], 0.0).then_inc(dv, 1)
                dve.wait_ge(w_loaded, 16 * 13)
                v.tensor_scalar(temp[:, :], temp[:, :], 0.1, 5.0, ALU.max, ALU.min).then_inc(dv, 1)
                dve.wait_ge(dv, 2)
                v.reciprocal(temp[:, :], temp[:, :]).then_inc(mx_made, 1)
                dve.wait_ge(mx_made, 1)
                v.tensor_copy(rows[:, 0, :].rearrange("o (h g) -> o h g", h=FH), temp[:, :].rearrange("o (h g) -> o h g", g=1).broadcast_to([1, FH, FG]))
                dve.wait_ge(pe_prep, 1)
                for k in range(NBK):
                    op = v.tensor_copy(wx_t[:, k, :], c.bank[k][:, 0:D])
                op.then_inc(dv, 1)
                dve.wait_ge(pe_prep, 2)
                v.tensor_copy(inv_temp[:, :], c.bank[3][:, :])
                v.tensor_tensor(rows[:, 2, :], c.bank[2][0:1, :], rows[:, 1, :], ALU.add).then_inc(dv, 1)
                dve.wait_ge(dv, 4)
                for ch in range(2):
                    v.tensor_tensor(wc[:, ch, :], c.bank[ch][:, :], inv_temp[:, :], ALU.mult)
                v.tensor_tensor(rows[:, 3, :], rows[:, 2, :], rows[:, 0, :], ALU.mult).then_inc(dv, 1)
                dve.wait_ge(dv, 5)
                dve.sem_inc(dv, 1)
                dve.wait_ge(pe_prep, 3)
                v.tensor_copy(brow[:, :], c.bank[3][:, :]).then_inc(dv, 1)
                dve.wait_ge(dv, 7)
                with batches(dve) as pair:
                    for p in range(2):
                        b = pair * 2 + p
                        f.vector(dve, nc, b, pair, p)
                        for i in range(T + 1):
                            if i < T:
                                s, n = i % 2, b * T + i
                                heads = lg[:, s, :].rearrange("p (h g) -> p h g", h=FH)
                                dve.wait_ge(e_made, 1 + b * T + max(i - 1, 0))
                                dve.wait_ge(logits, n + 1)
                                v.tensor_tensor(lg[:, s, :], c.bank[2][:, :], brow[:, :], ALU.add).then_inc(lg_made, 1)
                                dve.wait_ge(lg_made, 1 + n + 1)
                                v.tensor_reduce(mx[:, s, :], heads, AX.X, ALU.max).then_inc(mx_made, 1)
                                dve.wait_ge(mx_made, n + 2)
                                v.tensor_tensor(heads, heads, mx[:, s, :].rearrange("p (h g) -> p h g", g=1).broadcast_to([P, FH, FG]), ALU.subtract).then_inc(sub_made, 1)
                            if i >= 1:
                                s, n = (i - 1) % 2, b * T + i - 1
                                heads = e[:, s, :].rearrange("p (h g) -> p h g", h=FH)
                                dve.wait_ge(e_made, 1 + n + 1)
                                v.tensor_reduce(total[:, s, :], heads, AX.X, ALU.add).then_inc(total_made, 1)
                                dve.wait_ge(total_made, n + 1)
                                v.reciprocal(inv[:, s, :], total[:, s, :]).then_inc(inv_made, 1)
                                dve.wait_ge(inv_made, n + 1)
                                v.tensor_scalar(inv[:, s, :], inv[:, s, :], c.valid[:, bass.ds(n, 1)], None, ALU.mult).then_inc(inv_masked, 1)
                                dve.wait_ge(inv_masked, n + 1)
                                dve.wait_ge(sw_turned, 1 + b * T + max(i - 2, 0))
                                v.tensor_tensor(sw[:, s, :].rearrange("p (h g) -> p h g", h=FH), heads,
                                                inv[:, s, :].rearrange("p (h g) -> p h g", g=1).broadcast_to([P, FH, FG]), ALU.mult).then_inc(sw_made, 1)

            @block.scalar
            def _(act):
                prime(act, swt_made, e_made, f.xt_made)
                with batches(act) as pair:
                    for p in range(2):
                        b = pair * 2 + p

                        def also(i):
                            if 2 <= i < T + 2:
                                k = i - 2
                                act.wait_ge(sub_made, b * T + k + 1)
                                act.wait_ge(sw_made, 1 + b * T + max(k - 1, 0))
                                nc.scalar.activation(e[:, k % 2, :], lg[:, k % 2, :], ACT.Exp).then_inc(e_made, 1)
                            if i == 0:
                                act.wait_ge(stored[p], 16 * pair + 16)
                            if i >= 4:
                                k = i - 4
                                act.wait_ge(sw_turned, 1 + b * T + k + 1)
                                nc.scalar.copy(swt[:, p, k, :], c.bank[3][:, :]).then_inc(swt_made, 1)

                        f.scalar(act, nc, c, b, p, pooled, also, 3)

        copied = sem("pooled_copied")
        with nc.Block() as block:
            @block.vector
            def _(dve):
                for k in range(NBK):
                    op = nc.vector.tensor_copy(pooled_out[:, k, :], c.bank[4 + k][:, 0:D + 1])
                op.then_inc(copied, 1)
                dve.wait_ge(copied, 1)


def token_attention(nc, c, w, pooled_in, w_comb):
    with ExitStack() as ctx:
        def sb(name, shape, dt=F32):
            return ctx.enter_context(nc.sbuf_tensor(f"ta_{name}", shape, dt))

        def sem(name):
            return nc.alloc_semaphore(f"ta_{name}")

        NBK = INNER // P
        wfx = sb("wfx", [P, 2, INNER])
        wout = sb("wout", [P, NBK, D])
        bfx = sb("bfx", [P, INNER])
        qkv = sb("qkv", [P, 3, P])
        mask = sb("mask", [P, P])
        hide = sb("hide", [P, P])
        half_row = sb("half_row", [P, P])
        half_col = sb("half_col", [P, 1])
        pt = sb("pt", [P, 2, P])
        tok = sb("tok", [P, P])
        tok_t = sb("tok_t", [P, P])
        qkv_out = sb("qkv_out", [P, 3, P])
        s = sb("s", [P, P])
        mx = sb("mx", [P, 1])
        e = sb("e", [P, P])
        total = sb("total", [P, 1])
        e_t = sb("e_t", [P, P])
        out_t = sb("out_t", [P, P])
        den = sb("den", [P, 1])
        w_loaded, dv, pv, av = sem("w_loaded"), sem("vector_step"), sem("tensor_step"), sem("block_projected")
        exp_made, inv_made, comb_made = sem("exp_made"), sem("inv_made"), sem("comb_made")
        V, PV = 15, 7
        scale = float(FG) ** -0.5
        with nc.Block() as block:
            @block.sync
            def _(sp):
                sp.dma_start(wfx[:, :, :], w["L0_ffn_W_fx"].rearrange("(c p) n -> p c n", p=P)).then_inc(w_loaded, 16)
                sp.dma_start(wout[:, :, :], w["L0_ffn_W_out"].rearrange("(k p) n -> p k n", p=P)).then_inc(w_loaded, 16)
                sp.dma_start(bfx[:, :], spread_row(w["L0_ffn_b_fx"], INNER)).then_inc(w_loaded, 16)
                sp.wait_ge(dv, 1)
                for n, name in enumerate(("L0_ffn_W_q", "L0_ffn_W_k", "L0_ffn_W_v")):
                    for h in range(2):
                        sp.dma_start(qkv[h * FG:(h + 1) * FG, n, h * FG:(h + 1) * FG], w[name]).then_inc(w_loaded, 16)

            @block.tensor
            def _(pe):
                pe.wait_ge(w_loaded, 16 * 9)
                t = nc.tensor
                for k in range(NBK):
                    d0 = 4 + V * k
                    pe.wait_ge(dv, d0)
                    for ch in range(2):
                        op = t.transpose(c.bank[0][:, ch * P:(ch + 1) * P], pooled_in[:, k, ch * P:(ch + 1) * P], c.ident[:, :])
                    op.then_inc(pv, 1)
                    pe.wait_ge(dv, d0 + 1)
                    for ch in range(2):
                        op = t.matmul(c.bank[1][:, 0:P], pt[:, ch, :], wfx[:, ch, k * P:(k + 1) * P], start=(ch == 0), stop=(ch == 1))
                    op.then_inc(pv, 1)
                    pe.wait_ge(dv, d0 + 6)
                    t.transpose(c.bank[2][:, 0:P], tok[:, :], c.ident[:, :]).then_inc(pv, 1)
                    pe.wait_ge(dv, d0 + 7)
                    t.matmul(c.bank[3][:, 0:P], qkv[:, 0, :], tok_t[:, :], start=True, stop=True)
                    t.matmul(c.bank[3][:, P:2 * P], qkv[:, 1, :], tok_t[:, :], start=True, stop=True)
                    t.matmul(c.bank[3][:, 2 * P:3 * P], tok_t[:, :], qkv[:, 2, :], start=True, stop=True).then_inc(pv, 1)
                    pe.wait_ge(dv, d0 + 8)
                    t.matmul(c.bank[4][:, 0:P], qkv_out[:, 0, :], qkv_out[:, 1, :], start=True, stop=True).then_inc(pv, 1)
                    pe.wait_ge(dv, d0 + 13)
                    t.transpose(c.bank[5][:, 0:P], e[:, :], c.ident[:, :]).then_inc(pv, 1)
                    pe.wait_ge(dv, d0 + 14)
                    t.matmul(c.bank[6][:, 0:P], qkv_out[:, 2, :], e_t[:, :], start=True, stop=True).then_inc(pv, 1)
                    pe.wait_ge(dv, d0 + 15)
                    t.matmul(c.bank[7][:, 0:D], out_t[:, :], wout[:, k, :], start=True, stop=True).then_inc(av, 1)

            @block.scalar
            def _(act):
                for k in range(NBK):
                    d0 = 4 + V * k
                    act.wait_ge(dv, d0 + 11)
                    nc.scalar.activation(e[:, :], s[:, :], ACT.Exp, scale=scale).then_inc(exp_made, 1)
                    act.wait_ge(av, k + 1)
                    nc.scalar.copy(w_comb[:, k, :], c.bank[7][:, 0:D]).then_inc(comb_made, 1)

            @block.vector
            def _(dve):
                v = nc.vector
                n = [0]

                def chain(op):
                    op.then_inc(dv, 1)
                    n[0] += 1
                    dve.wait_ge(dv, n[0])

                chain(v.memset(qkv[:, :, :], 0.0))
                v.tensor_scalar(half_col[:, :], c.ramp_col[:, :], float(FG), None, ALU.is_ge)
                chain(v.tensor_scalar(half_row[:, :], c.ramp_row[:, :], float(FG), None, ALU.is_ge))
                chain(v.tensor_scalar(mask[:, :], half_row[:, :], half_col[:, 0:1], None, ALU.is_equal))
                chain(v.tensor_scalar(hide[:, :], mask[:, :], 1.0, BIG, ALU.subtract, ALU.mult))
                dve.wait_ge(w_loaded, 16 * 9)
                for k in range(NBK):
                    norm = pooled_in[:, k, D:D + 1]
                    dve.wait_ge(pv, PV * k + 1)
                    if k:
                        dve.wait_ge(comb_made, k)
                    chain(v.tensor_copy(pt[:, :, :].rearrange("p c n -> p (c n)"), c.bank[0][:, 0:D]))
                    chain(v.tensor_scalar(den[:, :], norm, 1e-5, None, ALU.add))
                    chain(v.reciprocal(den[:, :], den[:, :]))
                    dve.wait_ge(pv, PV * k + 2)
                    chain(v.scalar_tensor_tensor(tok[:, :], bfx[:, k * P:(k + 1) * P], norm, c.bank[1][:, 0:P], ALU.mult, ALU.add))
                    chain(v.tensor_scalar(tok[:, :], tok[:, :], den[:, 0:1], None, ALU.mult))
                    chain(v.tensor_tensor(tok[:, :], tok[:, :], mask[:, :], ALU.mult))
                    dve.wait_ge(pv, PV * k + 3)
                    chain(v.tensor_copy(tok_t[:, :], c.bank[2][:, 0:P]))
                    dve.wait_ge(pv, PV * k + 4)
                    chain(v.tensor_copy(qkv_out[:, :, :].rearrange("p c n -> p (c n)"), c.bank[3][:, 0:3 * P]))
                    dve.wait_ge(pv, PV * k + 5)
                    chain(v.tensor_tensor(s[:, :], c.bank[4][:, 0:P], hide[:, :], ALU.add))
                    chain(v.tensor_reduce(mx[:, :], s[:, :], AX.X, ALU.max))
                    chain(v.tensor_scalar(s[:, :], s[:, :], mx[:, 0:1], None, ALU.subtract))
                    dve.wait_ge(exp_made, k + 1)
                    chain(v.tensor_reduce(total[:, :], e[:, :], AX.X, ALU.add))
                    dve.wait_ge(dv, n[0])
                    v.reciprocal(total[:, :], total[:, :]).then_inc(inv_made, 1)
                    dve.wait_ge(inv_made, k + 1)
                    chain(v.tensor_scalar(e[:, :], e[:, :], total[:, 0:1], None, ALU.mult))
                    dve.wait_ge(pv, PV * k + 6)
                    chain(v.tensor_copy(e_t[:, :], c.bank[5][:, 0:P]))
                    dve.wait_ge(pv, PV * k + 7)
                    chain(v.tensor_copy(out_t[:, :], c.bank[6][:, 0:P]))
                dve.wait_ge(comb_made, NBK)


def hyp_project(nc, c, w, w_comb):
    with ExitStack() as ctx:
        def sb(name, shape, dt=F32):
            return ctx.enter_context(nc.sbuf_tensor(f"hp_{name}", shape, dt))

        def sem(name):
            return nc.alloc_semaphore(f"hp_{name}")

        NBK = INNER // P
        f = Front(nc, ctx, "hp")
        swt = sb("swt", [P, 2, T, INNER])
        b_out = sb("b_out", [P, D])
        wg = sb("wg", [P, 2, D])
        w_ext = sb("w_ext", [P, 2, D + 1])
        b_row = sb("b_row", [P, D])
        att = sb("att", [P, 2, D])
        mag_b = sb("mag_b", [P, 1])
        raw = sb("raw", [P, T, D])
        z = sb("z", [P, T])
        junk = sb("junk", [P, 2, D])
        square = sb("square", [P, T])
        norm = sb("norm", [P, T])
        ez = sb("ez", [P, T])
        factor = sb("factor", [P, T])
        rows = sb("rows", [P, 2, T, B_ROW])
        dst_now = sb("dst_now", [P, T])
        act_junk = sb("act_junk", [P, D])
        swt_loaded = [sem("swt_loaded0"), sem("swt_loaded1")]
        x_stored = [sem("x_stored0"), sem("x_stored1")]
        rows_stored = [sem("rows_stored0"), sem("rows_stored1")]
        (w_loaded, mixed, x_mixed, x_made, w_turned, w_ready, projected, raw_made, squared, norm_made, ez_made, dv, scored, bias_added) = (sem(s) for s in (
            "w_loaded", "mixed", "x_mixed", "x_made", "w_turned", "w_ready", "projected", "raw_made", "squared", "norm_made", "ez_made", "dv", "scored", "bias_added"))
        row_made, passed_sp = sem("row_made"), sem("passed_sp")
        V = 5
        with nc.Block() as block:
            @block.sync
            def _(sp):
                sp.dma_start(b_out[:, :], spread_row(w["L0_ffn_b_out"], D)).then_inc(w_loaded, 16)
                sp.dma_start(b_row[:, :], spread_row(w["L1_gnn_b"], D)).then_inc(w_loaded, 16)
                sp.dma_start(att[:, :, :].rearrange("p a d -> p (a d)"), spread_row(w["L1_gnn_attn_w"].rearrange("o d -> (o d)"), 2 * D)).then_inc(w_loaded, 16)
                sp.dma_start(mag_b[:, :], spread_row(w["L1_gnn_mag_b"], 1)).then_inc(w_loaded, 16)
                sp.dma_start(wg[:, :, :], w["L1_gnn_W"].rearrange("(c p) n -> p c n", p=P)).then_inc(w_loaded, 16)
                sp.dma_start(w_ext[:, :, D:], w["L1_gnn_mag_w"].rearrange("one (c p) -> p c one", p=P), allow_slow_non_contiguous=True).then_inc(w_loaded, 16)
                for p in range(2):
                    sp.sem_inc(rows_stored[p], 16)

                def load(b, p):
                    f.load(sp, nc, c.x1, b, p)
                    nc.sync.dma_start(swt[:, p, :, :], c.swt.rearrange("n p k -> p n k")[:, bass.ds(b * T, T), :]).then_inc(swt_loaded[p], 16)

                def store(b, pair, p):
                    sp.wait_ge(x_made, b + 1)
                    sp.sem_inc(passed_sp, 1)
                    nc.sync.dma_start(tiles_of(c.x2, b), f.x[:, p, :, :]).then_inc(x_stored[p], 16)
                    sp.wait_ge(scored, (b + 1) * T)
                    sp.sem_inc(passed_sp, 1)
                    nc.sync.dma_start(tiles_of(c.b_table, b), rows[:, p, :, :]).then_inc(rows_stored[p], 16)

                for p in range(2):
                    load(p, p)
                with sp.Fori(0, NB // 2 - 1) as pair:
                    for p in range(2):
                        b = pair * 2 + p
                        store(b, pair, p)
                        sp.wait_ge(x_stored[p], 16 * pair + 16)
                        sp.sem_inc(passed_sp, 1)
                        sp.wait_ge(projected, 1 + (b + 1) * T)
                        sp.sem_inc(passed_sp, 1)
                        load(b + 2, p)
                for p in range(2):
                    store(NB - 2 + p, None, p)
                for p in range(2):
                    sp.wait_ge(x_stored[p], 16 * (NB // 2))
                    sp.wait_ge(rows_stored[p], 16 + 16 * (NB // 2))

            @block.vector
            def _(dve):
                prime(dve, x_mixed, raw_made)
                v = nc.vector
                v.memset(dst_now[:, :], 0.0)
                v.memset(rows[:, :, :, :], 1.0)
                dve.wait_ge(w_loaded, 96)
                dve.wait_ge(w_turned, 1)
                op = v.tensor_copy(w_ext[:, :, 0:D], c.bank[4][:, :].rearrange("p (c n) -> p c n", c=2))
                op.then_inc(w_ready, 1)
                with batches(dve) as pair:
                    for p in range(2):
                        b = pair * 2 + p

                        def update():
                            for i in range(T):
                                dve.wait_ge(mixed, b * T + i + 1)
                                v.tensor_tensor(f.x[:, p, i, :], f.x[:, p, i, :], c.bank[4 + i % 2][:, 0:D], ALU.add).then_inc(x_mixed, 1)
                            dve.wait_ge(x_mixed, 1 + (b + 1) * T)
                            for i in range(T):
                                op = v.tensor_tensor(f.x[:, p, i, :], f.x[:, p, i, :], b_out[:, :], ALU.add)
                            op.then_inc(x_made, 1)
                            dve.wait_ge(x_made, b + 1)

                        f.vector(dve, nc, b, pair, p, update)

                        def chain(op, n):
                            op.then_inc(dv, 1)
                            dve.wait_ge(dv, b * V + n)

                        for i in range(T):
                            dve.wait_ge(projected, 1 + b * T + i + 1)
                            v.tensor_tensor(raw[:, i, :], c.bank[2 + i % 2][:, 0:D], b_row[:, :], ALU.add)
                            v.tensor_copy(z[:, i:i + 1], c.bank[2 + i % 2][:, D:D + 1]).then_inc(raw_made, 1)
                        dve.wait_ge(raw_made, 1 + (b + 1) * T)
                        v.tensor_scalar(z[:, :], z[:, :], mag_b[:, 0:1], None, ALU.add).then_inc(bias_added, 1)
                        dve.wait_ge(norm_made, b + 1)
                        chain(v.tensor_scalar(norm[:, :], norm[:, :], 1e-12, None, ALU.max), 1)
                        dve.wait_ge(ez_made, b + 1)
                        chain(v.tensor_scalar(ez[:, :], ez[:, :], 1.0, None, ALU.add), 2)
                        chain(v.reciprocal(factor[:, :], ez[:, :]), 3)
                        chain(v.reciprocal(norm[:, :], norm[:, :]), 4)
                        chain(v.scalar_tensor_tensor(factor[:, :], factor[:, :], 1.5, norm[:, :], ALU.mult, ALU.mult), 5)
                        dve.wait_ge(rows_stored[p], 16 * pair + 16)
                        for i in range(T):
                            v.tensor_scalar(rows[:, p, i, 0:D], raw[:, i, :], factor[:, i:i + 1], None, ALU.mult).then_inc(row_made, 1)
                        dve.wait_ge(row_made, (b + 1) * T)
                        for i in range(T):
                            v.tensor_tensor_reduce(junk[:, 0, :], rows[:, p, i, 0:D], att[:, 0, :], 1.0, 0.0, ALU.mult, ALU.add, rows[:, p, i, D + 1:D + 2])
                            v.tensor_tensor_reduce(junk[:, 1, :], rows[:, p, i, 0:D], att[:, 1, :], 1.0, 0.0, ALU.mult, ALU.add, dst_now[:, i:i + 1]).then_inc(scored, 1)
                            dve.wait_ge(scored, b * T + i + 1)
                        v.tensor_copy(c.dst_score[:, bass.ds(b * T, T)], dst_now[:, :])

            @block.scalar
            def _(act):
                prime(act, f.xt_made)
                with batches(act) as pair:
                    for p in range(2):
                        b = pair * 2 + p
                        f.scalar(act, nc, c, b, p, projected)
                        for i in range(T):
                            act.wait_ge(raw_made, 1 + b * T + i + 1)
                            nc.scalar.activation(act_junk[:, :], raw[:, i, :], ACT.Square, accum_out=square[:, i:i + 1]).then_inc(squared, 1)
                            act.wait_ge(squared, b * T + i + 1)
                        nc.scalar.activation(norm[:, :], square[:, :], ACT.Sqrt).then_inc(norm_made, 1)
                        act.wait_ge(bias_added, b + 1)
                        nc.scalar.activation(ez[:, :], z[:, :], ACT.Exp, scale=-1.0).then_inc(ez_made, 1)

            @block.tensor
            def _(pe):
                prime(pe, projected)
                pe.wait_ge(w_loaded, 96)
                for a in range(2):
                    for ch in range(2):
                        op = nc.tensor.transpose(c.bank[4][:, ch * D + a * P:ch * D + (a + 1) * P], wg[:, a, ch * P:(ch + 1) * P], c.ident[:, :])
                op.then_inc(w_turned, 1)
                pe.wait_ge(w_ready, 1)
                with batches(pe) as pair:
                    for p in range(2):
                        b = pair * 2 + p
                        pe.wait_ge(swt_loaded[p], 16 * pair + 16)
                        for i in range(T):
                            pe.wait_ge(x_mixed, 1 + b * T + max(i - 1, 0))
                            for q in range(NBK):
                                op = nc.tensor.matmul(c.bank[4 + i % 2][:, 0:D], swt[:, p, i, q * P:(q + 1) * P], w_comb[:, q, :], start=(q == 0), stop=(q == NBK - 1))
                            op.then_inc(mixed, 1)
                        for i in range(T + 1):
                            if i < T:
                                f.tensor(pe, nc, c, b, p, i)
                            if i >= 1:
                                k = i - 1
                                pe.wait_ge(f.xt_made, 1 + b * T + i)
                                pe.wait_ge(raw_made, 1 + b * T + max(k - 1, 0))
                                for ch in range(2):
                                    op = nc.tensor.matmul(c.bank[2 + k % 2][:, 0:D + 1], f.xt[:, k, ch, :], w_ext[:, ch, :], start=(ch == 0), stop=(ch == 1))
                                op.then_inc(projected, 1)



def hyp_finish(nc, c, w, acc):
    MAX_NORM = 0.95
    with ExitStack() as ctx:
        def sb(name, shape, dt=F32):
            return ctx.enter_context(nc.sbuf_tensor(f"hf_{name}", shape, dt))

        def sem(name):
            return nc.alloc_semaphore(f"hf_{name}")

        x = sb("x", [P, 2, T, D])
        h = sb("h", [P, 2, T, B_ROW])
        den = sb("den", [P, T])
        hc = sb("hc", [P, T, D])
        act_junk = sb("act_junk", [P, D])
        square = sb("square", [P, T])
        norm = sb("norm", [P, T])
        clamped = sb("clamped", [P, T])
        th = sb("th", [P, T])
        ball = sb("ball", [P, T])
        over = sb("over", [P, T])
        loaded = [sem("loaded0"), sem("loaded1")]
        stored = [sem("stored0"), sem("stored1")]
        dv, row_made, squared, norm_made, clamped_made, th_made, x_made, passed = (sem(s) for s in (
            "dv", "row_made", "squared", "norm_made", "clamped_made", "th_made", "x_made", "passed"))
        V = 11
        with nc.Block() as block:
            @block.sync
            def _(sp):
                def load(b, p):
                    nc.sync.dma_start(x[:, p, :, :], tiles_of(c.x2, b)).then_inc(loaded[p], 16)
                    nc.sync.dma_start(h[:, p, :, :], tiles_of(c.b_table, b)).then_inc(loaded[p], 16)

                def store(b, p):
                    sp.wait_ge(x_made, 1 + (b + 1) * T)
                    sp.sem_inc(passed, 1)
                    nc.sync.dma_start(tiles_of(c.x3, b), x[:, p, :, :]).then_inc(stored[p], 16)

                for p in range(2):
                    load(p, p)
                with sp.Fori(0, NB // 2 - 1) as pair:
                    for p in range(2):
                        store(pair * 2 + p, p)
                        sp.wait_ge(stored[p], 16 * pair + 16)
                        sp.sem_inc(passed, 1)
                        load(pair * 2 + p + 2, p)
                for p in range(2):
                    store(NB - 2 + p, p)
                for p in range(2):
                    sp.wait_ge(stored[p], 16 * (NB // 2))

            @block.vector
            def _(dve):
                prime(dve, x_made)
                v = nc.vector
                with batches(dve) as pair:
                    for p in range(2):
                        b = pair * 2 + p

                        def chain(op, n):
                            op.then_inc(dv, 1)
                            dve.wait_ge(dv, b * V + n)

                        sums = acc[:, bass.ds(b * T * B_ACC, T * B_ACC)].rearrange("p (t k) -> p t k", t=T)
                        dve.wait_ge(loaded[p], 32 * pair + 32)
                        chain(v.tensor_scalar(den[:, :], sums[:, :, D], 1e-10, None, ALU.add), 1)
                        chain(v.reciprocal(den[:, :], den[:, :]), 2)
                        for i in range(T):
                            v.scalar_tensor_tensor(hc[:, i, :], sums[:, i, 0:D], den[:, i:i + 1], h[:, p, i, 0:D], ALU.mult, ALU.add).then_inc(row_made, 1)
                        dve.wait_ge(norm_made, b + 1)
                        v.tensor_scalar(clamped[:, :], norm[:, :], 1e-15, None, ALU.max).then_inc(clamped_made, 1)
                        dve.wait_ge(clamped_made, b + 1)
                        chain(v.reciprocal(ball[:, :], clamped[:, :]), 3)
                        dve.wait_ge(th_made, b + 1)
                        chain(v.tensor_tensor(ball[:, :], ball[:, :], th[:, :], ALU.mult), 4)
                        chain(v.tensor_tensor(norm[:, :], norm[:, :], ball[:, :], ALU.mult), 5)
                        chain(v.tensor_scalar(over[:, :], norm[:, :], MAX_NORM, None, ALU.is_gt), 6)
                        chain(v.tensor_scalar(norm[:, :], norm[:, :], 1e-8, None, ALU.add), 7)
                        chain(v.reciprocal(norm[:, :], norm[:, :]), 8)
                        chain(v.tensor_scalar(norm[:, :], norm[:, :], MAX_NORM, 1.0, ALU.mult, ALU.subtract), 9)
                        chain(v.tensor_tensor(norm[:, :], norm[:, :], over[:, :], ALU.mult), 10)
                        chain(v.scalar_tensor_tensor(ball[:, :], norm[:, :], 1.0, ball[:, :], ALU.add, ALU.mult), 11)
                        for i in range(T):
                            v.scalar_tensor_tensor(x[:, p, i, :], hc[:, i, :], ball[:, i:i + 1], x[:, p, i, :], ALU.mult, ALU.add).then_inc(x_made, 1)

            @block.scalar
            def _(act):
                with batches(act) as pair:
                    for p in range(2):
                        b = pair * 2 + p
                        for i in range(T):
                            act.wait_ge(row_made, b * T + i + 1)
                            nc.scalar.activation(act_junk[:, :], hc[:, i, :], ACT.Square, accum_out=square[:, i:i + 1]).then_inc(squared, 1)
                            act.wait_ge(squared, b * T + i + 1)
                        act.wait_ge(x_made, 1 + b * T)
                        nc.scalar.activation(norm[:, :], square[:, :], ACT.Sqrt).then_inc(norm_made, 1)
                        act.wait_ge(clamped_made, b + 1)
                        nc.scalar.activation(th[:, :], clamped[:, :], ACT.Tanh).then_inc(th_made, 1)


def route(nc, c, w):
    with ExitStack() as ctx:
        def sb(name, shape, dt=F32):
            return ctx.enter_context(nc.sbuf_tensor(f"ro_{name}", shape, dt))

        def sem(name):
            return nc.alloc_semaphore(f"ro_{name}")

        f = Front(nc, ctx, "ro", deep=2)
        wgate = sb("wgate", [P, 2, NX])
        bgate = sb("bgate", [P, 2, NX])
        before = sb("before", [P, P])
        lg = sb("lg", [P, T, NX])
        best = sb("best", [P, T, 8])
        best_at = sb("best_at", [P, T, 8], mybir.dt.uint32)
        best_f = sb("best_f", [P, T, 8])
        gap = sb("gap", [P, T])
        share = sb("share", [P, 2, T])
        chosen = sb("chosen", [P, 2, T, NX])
        mask = sb("mask", [P, T, NX])
        base = sb("base", [P, T + 1, NX])
        rank = sb("rank", [P, T, NX])
        placed = sb("placed", [P, 2, T, NX])
        place_f = sb("place_f", [P, 2, T])
        place = sb("place", [P, 2, 2 * T], I32)
        w_loaded, set_up, gated, dv, gap_made, e2_made, mask_made, counted, place_made, scattered0, scattered1, rows_gone, passed_v = (sem(s) for s in (
            "w_loaded", "set_up", "gated", "dv", "gap_made", "e2_made", "mask_made", "counted", "place_made", "scattered0", "scattered1", "rows_gone", "passed_v"))
        scattered = [scattered0, scattered1]
        V = 12 + T
        with nc.Block() as block:
            @block.sync
            def _(sp):
                for ch in range(2):
                    sp.dma_start(wgate[:, ch, :], w["L1_ffn_Wg"].rearrange("(c p) n -> c p n", p=P)[ch]).then_inc(w_loaded, 16)
                sp.dma_start(bgate[:, 0, :], spread_row(w["L1_ffn_bg"], NX)).then_inc(w_loaded, 16)
                sp.dma_start(bgate[:, 1, :], spread_row(w["L1_ffn_bias"], NX)).then_inc(w_loaded, 16)

                def store(b, p):
                    pass

                f.sync(sp, nc, c.x3, gated, store)

            @block.gpsimd
            def _(pool):
                pool.sem_inc(rows_gone, 2)
                with batches(pool) as pair:
                    for p in range(2):
                        pool.wait_ge(place_made, pair * 2 + p + 1)
                        pool.sem_inc(passed_v, 1)
                        for k in range(2):
                            for i in range(T):
                                nc.gpsimd.indirect_dma_start(c.routed, bass.IndirectOffsetOnAxis(ap=place[:, p, k * T + i:k * T + i + 1], axis=0),
                                                             f.xn[:, p, i, 0:D], None).then_inc(scattered[p], 16)
                        pool.wait_ge(scattered[p], 16 * 2 * T * (pair + 1))
                        pool.sem_inc(rows_gone, 1)

            @block.vector
            def _(dve):
                v = nc.vector
                v.tensor_scalar(before[:, :], c.ramp_row[:, :], c.ramp_col[:, 0:1], None, ALU.is_gt)
                v.tensor_scalar(base[:, 0, :], c.ramp_row[:, 0:NX], float(REG), None, ALU.mult)
                dve.wait_ge(w_loaded, 64)
                v.tensor_tensor(bgate[:, 0, :], bgate[:, 0, :], bgate[:, 1, :], ALU.add).then_inc(set_up, 1)
                dve.wait_ge(set_up, 1)
                with batches(dve) as pair:
                    for p in range(2):
                        b = pair * 2 + p
                        f.vector(dve, nc, b, pair, p)

                        def chain(op, n):
                            op.then_inc(dv, 1)
                            dve.wait_ge(dv, b * V + n)
                            dve.sem_inc(passed_v, 1)

                        dve.wait_ge(gated, 1 + (b + 1) * T)
                        chain(v.tensor_tensor(lg[:, :, :], c.bank[2][:, 0:T * NX].rearrange("p (t e) -> p t e", e=NX),
                                              bgate[:, 0:1, :].broadcast_to([P, T, NX]), ALU.add), 1)
                        for i in range(T):
                            op = v.max(best[:, i, :], lg[:, i, :])
                        chain(op, 2)
                        v.tensor_tensor(gap[:, :], best[:, :, 1], best[:, :, 0], ALU.subtract).then_inc(gap_made, 1)
                        for i in range(T):
                            op = v.max_index(best_at[:, i, :], best[:, i, :], lg[:, i, :])
                        chain(op, 3)
                        chain(v.tensor_copy(best_f[:, :, :], best_at[:, :, :]), 4)
                        ramp = c.ramp_row[:, 0:NX].rearrange("p (o e) -> p o e", o=1).broadcast_to([P, T, NX])
                        for k in range(2):
                            op = v.tensor_tensor(chosen[:, k, :, :], ramp, best_f[:, :, k:k + 1].broadcast_to([P, T, NX]), ALU.is_equal)
                        chain(op, 5)
                        v.tensor_tensor(mask[:, :, :], chosen[:, 0, :, :], chosen[:, 1, :, :], ALU.add).then_inc(mask_made, 1)
                        dve.wait_ge(e2_made, b + 1)
                        chain(v.tensor_scalar(share[:, 0, :], share[:, 1, :], 1.0, None, ALU.add), 6)
                        chain(v.reciprocal(share[:, 0, :], share[:, 0, :]), 7)
                        chain(v.tensor_tensor(share[:, 1, :], share[:, 1, :], share[:, 0, :], ALU.mult), 8)
                        v.tensor_copy(c.shares[:, bass.ds(b * 2 * T, 2 * T)], share[:, :, :].rearrange("p k t -> p (k t)"))
                        dve.wait_ge(counted, b + 1)
                        for i in range(T):
                            chain(v.tensor_tensor(base[:, i + 1, :], base[:, i, :], c.bank[3][:, (T + i) * NX:(T + i + 1) * NX], ALU.add), 9 + i)
                        chain(v.tensor_tensor(rank[:, :, :], base[:, 0:T, :], c.bank[3][:, 0:T * NX].rearrange("p (t e) -> p t e", e=NX), ALU.add), 9 + T)
                        v.tensor_copy(base[:, 0, :], base[:, T, :])
                        for k in range(2):
                            op = v.tensor_tensor(placed[:, k, :, :], rank[:, :, :], chosen[:, k, :, :], ALU.mult)
                        chain(op, 10 + T)
                        chain(v.tensor_reduce(place_f[:, :, :].rearrange("p k t -> p (k t)"), placed[:, :, :, :].rearrange("p k t e -> p (k t) e"), AX.X, ALU.add), 11 + T)
                        dve.wait_ge(rows_gone, b + 1)
                        v.tensor_copy(place[:, p, :], place_f[:, :, :].rearrange("p k t -> p (k t)")).then_inc(place_made, 1)
                        chain(v.tensor_copy(c.places_f[:, bass.ds(b * 2 * T, 2 * T)], place_f[:, :, :].rearrange("p k t -> p (k t)")), 12 + T)
                v.tensor_copy(c.next_row[:, :], base[:, 0, :]).then_inc(dv, 1)
                dve.wait_ge(dv, NB * V + 1)

            @block.scalar
            def _(act):
                prime(act, f.xt_made)
                with batches(act) as pair:
                    for p in range(2):
                        b = pair * 2 + p

                        def free():
                            act.wait_ge(rows_gone, b + 1)
                            act.sem_inc(passed_v, 1)

                        f.scalar(act, nc, c, b, p, gated, free=free)
                        act.wait_ge(gap_made, b + 1)
                        nc.scalar.activation(share[:, 1, :], gap[:, :], ACT.Exp).then_inc(e2_made, 1)

            @block.tensor
            def _(pe):
                prime(pe, gated)
                t = nc.tensor
                pe.wait_ge(w_loaded, 64)
                pe.wait_ge(set_up, 1)
                with batches(pe) as pair:
                    for p in range(2):
                        b = pair * 2 + p
                        for i in range(T + 1):
                            if i < T:
                                f.tensor(pe, nc, c, b, p, i)
                            if i >= 1:
                                pe.wait_ge(f.xt_made, 1 + b * T + i)
                                for ch in range(2):
                                    op = t.matmul(c.bank[2][:, (i - 1) * NX:i * NX], f.xt[:, i - 1, ch, :], wgate[:, ch, :], start=(ch == 0), stop=(ch == 1))
                                op.then_inc(gated, 1)
                        pe.wait_ge(mask_made, b + 1)
                        tokens = mask[:, :, :].rearrange("p t e -> p (t e)")
                        t.matmul(c.bank[3][:, 0:T * NX], before[:, :], tokens, start=True, stop=True)
                        t.matmul(c.bank[3][:, T * NX:2 * T * NX], c.ones[:, :], tokens, start=True, stop=True).then_inc(counted, 1)


def plan_tiles(nc, c):
    with ExitStack() as ctx:
        def sb(name, shape, dt=F32):
            return ctx.enter_context(nc.sbuf_tensor(f"pt_{name}", shape, dt))

        def sem(name):
            return nc.alloc_semaphore(f"pt_{name}")

        zeros = sb("zeros", [P, D])
        next_i = sb("next_i", [P, NX], I32)
        count = sb("count", [P, NX])
        tiles_i = sb("tiles_i", [P, NX], I32)
        tiles = sb("tiles", [P, NX])
        ends = sb("ends", [P, NX])
        skip = sb("skip", [P, NX])
        ramp_i = sb("ramp_i", [P, SLOTS], I32)
        slot = sb("slot", [P, SLOTS])
        last = sb("last", [P, 1])
        past = sb("past", [P, NX, SLOTS])
        two = sb("two", [P, 2, SLOTS])
        behind = sb("behind", [P, NX, 2 * NT])
        place = sb("place", [P, 2 * NT])
        dv, ramp_made, padded = sem("dv"), sem("ramp_made"), sem("padded")
        with nc.Block() as block:
            @block.gpsimd
            def _(pool):
                nc.gpsimd.iota(ramp_i[:, :], [[1, SLOTS]], base=0, channel_multiplier=0).then_inc(ramp_made, 1)

            @block.vector
            def _(dve):
                v = nc.vector
                steps = iter(range(1, 1000))

                def chain(op):
                    op.then_inc(dv, 1)
                    dve.wait_ge(dv, next(steps))

                v.memset(zeros[:, :], 0.0)
                chain(v.tensor_copy(next_i[:, :], c.next_row[:, :]))
                dve.wait_ge(ramp_made, 1)
                v.tensor_copy(slot[:, :], ramp_i[:, :])
                v.tensor_scalar(count[:, :], c.ramp_row[:, 0:NX], float(-REG), float(P - 1), ALU.mult, ALU.add).then_inc(dv, 1)
                dve.wait_ge(dv, next(steps))
                chain(v.tensor_tensor(count[:, :], count[:, :], c.next_row[:, :], ALU.add))
                chain(v.tensor_copy(tiles_i[:, :], count[:, :]))
                chain(v.tensor_scalar(tiles_i[:, :], tiles_i[:, :], 7, None, ALU.logical_shift_right))
                chain(v.tensor_copy(tiles[:, :], tiles_i[:, :]))
                chain(v.tensor_scalar(tiles[:, :], tiles[:, :], 1.0, None, ALU.max))
                v.tensor_scalar(skip[:, :], tiles[:, :], float(-P), float(REG), ALU.mult, ALU.add)
                chain(v.tensor_copy(ends[:, 0:1], tiles[:, 0:1]))
                for e in range(1, NX):
                    chain(v.tensor_tensor(ends[:, e:e + 1], ends[:, e - 1:e], tiles[:, e:e + 1], ALU.add))
                chain(v.tensor_scalar(last[:, :], ends[:, NX - 1:NX], -1.0, None, ALU.add))
                chain(v.tensor_scalar(slot[:, :], slot[:, :], last[:, 0:1], None, ALU.min))
                for e in range(NX - 1):
                    op = v.tensor_scalar(past[:, e, :], slot[:, :], ends[:, e:e + 1], None, ALU.is_ge)
                chain(v.tensor_scalar(two[:, 0, :], slot[:, :], float(P), None, ALU.mult))
                chain(v.tensor_copy(two[:, 1, :], past[:, 0, :]))
                for e in range(NX - 1):
                    op = v.scalar_tensor_tensor(two[:, 0, :], past[:, e, :], skip[:, e:e + 1], two[:, 0, :], ALU.mult, ALU.add)
                    if e:
                        op = v.tensor_tensor(two[:, 1, :], two[:, 1, :], past[:, e, :], ALU.add)
                    chain(op)
                v.tensor_copy(c.slot_row[:, :], two[0:1, 0, :])
                for e in range(NX - 1):
                    op = v.tensor_scalar(behind[:, e, :], c.places_f[:, :], float((e + 1) * REG), skip[:, e:e + 1], ALU.is_ge, ALU.mult)
                chain(op)
                for e in range(NX - 1):
                    chain(v.tensor_tensor(place[:, :], place[:, :] if e else c.places_f[:, :], behind[:, e, :], ALU.subtract))
                v.tensor_copy(c.places[:, :], place[:, :])
                chain(v.tensor_copy(c.slot_expert[:, :], two[0:1, 1, :]))

            @block.sync
            def _(sp):
                sp.wait_ge(dv, 1)
                at = nc.values_load_multi_w_load_instructions(next_i[0:1, 0:NX], engines=[mybir.EngineType.SP], min_val=0, max_val=NX * REG - P)[1]
                for e in range(NX):
                    nc.sync.dma_start(c.routed[bass.ds(at[e], P), :], zeros[:, :]).then_inc(padded, 16)
                sp.wait_ge(padded, 16 * NX)


def experts(nc, c, w):
    with ExitStack() as ctx:
        def sb(name, shape, dt=F32):
            return ctx.enter_context(nc.sbuf_tensor(f"ex_{name}", shape, dt))

        def sem(name):
            return nc.alloc_semaphore(f"ex_{name}")

        FB = FF // P
        W1, B1 = 2 * FF, 2 * FF + FB
        UPW = B1 + D
        R = 4
        up_w = sb("up_w", [P, NX, UPW])
        w2 = sb("w2", [P, NX * FB, D])
        now = sb("now", [P, R, UPW])
        xs = sb("xs", [P, R, D])
        xt = sb("xt", [P, 2, D])
        hid = sb("hid", [P, 2, FF])
        y = sb("y", [P, R, D])
        w_loaded, turned, xt_made, now_made, up, hid_made, down, y_made, passed = (sem(s) for s in (
            "w_loaded", "turned", "xt_made", "now_made", "up", "hid_made", "down", "y_made", "passed"))
        loaded, stored = [sem(f"loaded{q}") for q in range(R)], [sem(f"stored{q}") for q in range(R)]
        rounds = SLOTS // R

        def first_rows(first, n):
            return nc.values_load_multi_w_load_instructions(c.slot_row[0:1, bass.ds(first, n)], engines=[mybir.EngineType.SP], min_val=0, max_val=NX * REG - P)[1]

        def experts_of(first, n, engine):
            return nc.values_load_multi_w_load_instructions(c.slot_expert[0:1, bass.ds(first, n)], engines=[engine], min_val=0, max_val=NX - 1)[1]

        with nc.Block() as block:
            @block.sync
            def _(sp):
                for e in range(NX):
                    sp.dma_start(up_w[:, e, 0:W1].rearrange("p (c n) -> p c n", n=FF), w["L1_ffn_W1"][e].rearrange("(c p) n -> p c n", p=P)).then_inc(w_loaded, 16)
                    sp.dma_start(w2[:, e * FB:(e + 1) * FB, :], w["L1_ffn_W2"][e].rearrange("(k p) n -> p k n", p=P)).then_inc(w_loaded, 16)
                    sp.dma_start(up_w[:, e, B1:], spread_row(w["L1_ffn_b2"].rearrange("e d -> (e d)")[e * D:(e + 1) * D], D)).then_inc(w_loaded, 16)
                    sp.dma_start(up_w[:, e, W1:B1], w["L1_ffn_b1"].rearrange("e (k p) -> p e k", p=P)[:, e, :], allow_slow_non_contiguous=True).then_inc(w_loaded, 16)

                def load(row, q):
                    nc.sync.dma_start(xs[:, q, :], c.routed[bass.ds(row, P), :]).then_inc(loaded[q], 16)

                def store(tile, q):
                    sp.wait_ge(y_made, 2 + tile + 1)
                    sp.sem_inc(passed, 1)
                    nc.sync.dma_start(c.y_rows.rearrange("(s p) d -> p s d", p=P)[:, bass.ds(tile, 1), :], y[:, q:q + 1, :]).then_inc(stored[q], 16)

                for q in range(R):
                    sp.sem_inc(stored[q], 16)
                row = first_rows(0, R)
                for q in range(R):
                    load(row[q], q)
                with sp.Fori(0, rounds - 1) as turn:
                    row = first_rows((turn + 1) * R, R)
                    for q in range(R):
                        sp.wait_ge(turned, turn * R + q + 1)
                        sp.sem_inc(passed, 1)
                        load(row[q], q)
                        store(turn * R + q, q)
                for q in range(R):
                    store((rounds - 1) * R + q, q)
                for q in range(R):
                    sp.wait_ge(stored[q], 16 + 16 * rounds)

            @block.tensor
            def _(pe):
                t = nc.tensor
                pe.wait_ge(w_loaded, 16 * 4 * NX)

                def turn_tile(tile, q, turn):
                    pe.wait_ge(loaded[q], 16 * turn + 16)
                    if not (isinstance(tile, int) and tile < 2):
                        pe.wait_ge(xt_made, tile - 1)
                        pe.sem_inc(passed, 1)
                    for ch in range(2):
                        op = t.transpose(c.bank[q % 2][:, ch * P:(ch + 1) * P], xs[:, q, ch * P:(ch + 1) * P], c.ident[:, :])
                    op.then_inc(turned, 1)

                def hidden(tile, q):
                    pe.wait_ge(xt_made, tile + 1)
                    pe.wait_ge(now_made, tile + 1)
                    pe.wait_ge(hid_made, 2 + tile - 1)
                    pe.sem_inc(passed, 1)
                    for k in range(FB):
                        for ch in range(2):
                            op = t.matmul(c.bank[2 + q % 2][:, k * P:(k + 1) * P], now[:, q, ch * FF + k * P:ch * FF + (k + 1) * P], xt[:, q % 2, ch * P:(ch + 1) * P],
                                          start=(ch == 0), stop=(ch == 1))
                    op.then_inc(up, 1)

                def out_of(tile, q, expert):
                    pe.wait_ge(hid_made, 2 + tile + 1)
                    pe.wait_ge(y_made, 2 + tile - 1)
                    pe.sem_inc(passed, 1)
                    for k in range(FB):
                        op = t.matmul(c.bank[4 + q % 2][:, 0:D], hid[:, q % 2, k * P:(k + 1) * P], w2[:, bass.ds(expert * FB + k, 1), :].rearrange("p o d -> p (o d)"),
                                      start=(k == 0), stop=(k == FB - 1))
                    op.then_inc(down, 1)

                def work(turn, final):
                    expert = experts_of(turn * R, R, mybir.EngineType.PE)
                    for q in range(R):
                        tile = turn * R + q
                        if not (final and q >= R - 2):
                            turn_tile(tile + 2, (q + 2) % R, turn + (q + 2) // R)
                        if not (final and q == R - 1):
                            hidden(tile + 1, (q + 1) % R)
                        out_of(tile, q, expert[q])

                turn_tile(0, 0, 0)
                turn_tile(1, 1, 0)
                hidden(0, 0)
                with pe.Fori(0, rounds - 1) as turn:
                    work(turn, False)
                work(rounds - 1, True)

            @block.vector
            def _(dve):
                dve.sem_inc(y_made, 2)
                v = nc.vector
                dve.wait_ge(w_loaded, 16 * 4 * NX)

                def prepare(tile, q, expert):
                    dve.wait_ge(turned, tile + 1)
                    v.tensor_copy(xt[:, q % 2, :], c.bank[q % 2][:, 0:D]).then_inc(xt_made, 1)
                    if not (isinstance(tile, int) and tile < 2):
                        dve.wait_ge(y_made, 2 + tile - 4 + 1)
                        dve.sem_inc(passed, 1)
                    v.tensor_copy(now[:, q, :], up_w[:, bass.ds(expert, 1), :].rearrange("p o n -> p (o n)")).then_inc(now_made, 1)

                def finish(turn, q):
                    tile = turn * R + q
                    dve.wait_ge(stored[q], 16 + 16 * turn)
                    dve.wait_ge(down, tile + 1)
                    v.tensor_tensor(y[:, q, :], c.bank[4 + q % 2][:, 0:D], now[:, q, B1:], ALU.add).then_inc(y_made, 1)

                def work(turn, final):
                    expert = experts_of(turn * R + 2, R - 2 if final else R, mybir.EngineType.DVE)
                    for q in range(R):
                        if not (final and q >= R - 2):
                            prepare(turn * R + q + 2, (q + 2) % R, expert[q])
                        finish(turn, q)

                expert = experts_of(0, 2, mybir.EngineType.DVE)
                for q in range(2):
                    prepare(q, q, expert[q])
                with dve.Fori(0, rounds - 1) as turn:
                    work(turn, False)
                work(rounds - 1, True)

            @block.scalar
            def _(act):
                act.sem_inc(hid_made, 2)
                with act.Fori(0, rounds) as turn:
                    for q in range(R):
                        act.wait_ge(up, turn * R + q + 1)
                        for k in range(FB):
                            op = nc.scalar.activation(hid[:, q % 2, k * P:(k + 1) * P], c.bank[2 + q % 2][:, k * P:(k + 1) * P], ACT.Relu, bias=now[:, q, W1 + k:W1 + k + 1])
                        op.then_inc(hid_made, 1)


def combine(nc, c, out):
    with ExitStack() as ctx:
        def sb(name, shape, dt=F32):
            return ctx.enter_context(nc.sbuf_tensor(f"co_{name}", shape, dt))

        def sem(name):
            return nc.alloc_semaphore(f"co_{name}")

        x = sb("x", [P, 2, T, D])
        y = sb("y", [P, 2, 2 * T, D])
        place = sb("place", [P, 2, 2 * T], I32)
        loaded, gathered, stored = ([sem(f"{s}{p}") for p in range(2)] for s in ("loaded", "gathered", "stored"))
        place_ready, best_added, made, passed = sem("place_ready"), sem("best_added"), sem("made"), sem("passed")
        with nc.Block() as block:
            @block.sync
            def _(sp):
                def load(b, p):
                    nc.sync.dma_start(x[:, p, :, :], tiles_of(c.x3, b)).then_inc(loaded[p], 16)

                def store(b, p):
                    sp.wait_ge(made, b + 1)
                    sp.sem_inc(passed, 1)
                    nc.sync.dma_start(tiles_of(out, b), x[:, p, :, :]).then_inc(stored[p], 16)

                for p in range(2):
                    load(p, p)
                with sp.Fori(0, NB // 2 - 1) as pair:
                    for p in range(2):
                        store(pair * 2 + p, p)
                        sp.wait_ge(stored[p], 16 * pair + 16)
                        sp.sem_inc(passed, 1)
                        load(pair * 2 + p + 2, p)
                for p in range(2):
                    store(NB - 2 + p, p)
                for p in range(2):
                    sp.wait_ge(stored[p], 16 * (NB // 2))

            @block.gpsimd
            def _(pool):
                with batches(pool) as pair:
                    for p in range(2):
                        pool.wait_ge(place_ready, pair * 2 + p + 1)
                        pool.sem_inc(passed, 1)
                        for i in range(2 * T):
                            nc.gpsimd.indirect_dma_start(y[:, p, i, :], None, c.y_rows,
                                                         bass.IndirectOffsetOnAxis(ap=place[:, p, i:i + 1], axis=0)).then_inc(gathered[p], 16)

            @block.vector
            def _(dve):
                v = nc.vector

                def places(b, p):
                    v.tensor_copy(place[:, p, :], c.places[:, bass.ds(b * 2 * T, 2 * T)]).then_inc(place_ready, 1)

                def work(pair, p):
                    b = pair * 2 + p
                    share = c.shares[:, bass.ds(b * 2 * T, 2 * T)]
                    v.tensor_copy(share_now[:, p, :], share).then_inc(share_made, 1)
                    dve.wait_ge(share_made, b + 1)
                    dve.wait_ge(loaded[p], 16 * pair + 16)
                    dve.wait_ge(gathered[p], 16 * 2 * T * (pair + 1))
                    dve.sem_inc(passed, 1)
                    for k in range(2):
                        for i in range(T):
                            op = v.scalar_tensor_tensor(x[:, p, i, :], y[:, p, k * T + i, :], share_now[:, p, k * T + i:k * T + i + 1], x[:, p, i, :], ALU.mult, ALU.add)
                        if k == 0:
                            op.then_inc(best_added, 1)
                            dve.wait_ge(best_added, b + 1)
                            dve.sem_inc(passed, 1)
                    op.then_inc(made, 1)

                share_now = sb("share_now", [P, 2, 2 * T])
                share_made = sem("share_made")
                for p in range(2):
                    places(p, p)
                with dve.Fori(0, NB // 2 - 1) as pair:
                    for p in range(2):
                        work(pair, p)
                        places(pair * 2 + p + 2, p)
                for p in range(2):
                    work(NB // 2 - 1, p)


def program(nc, w, out):
    def dram(name, shape, dt=F32):
        return nc.dram_tensor(name, shape, dt).ap()

    with ExitStack() as ctx:
        def sb(name, shape, dt=F32):
            return ctx.enter_context(nc.sbuf_tensor(name, shape, dt))

        def sem(name):
            return nc.alloc_semaphore(name)

        c = Core()
        c.bank = [ctx.enter_context(nc.psum_tensor(f"bank{b}", [P, 512], F32)) for b in range(8)]
        c.x_in, c.x1, c.x2, c.x3 = w["x"], dram("x1", [NPAD, D]), dram("x2", [NPAD, D]), dram("x3", [NPAD, D])
        c.a_table, c.b_table = dram("a_table", [NPAD, A_ROW]), dram("b_table", [NPAD, B_ROW])
        c.swt = dram("swt", [NT, P, INNER])
        make_constants(nc, c, sb, sem)
        c.dst_score = sb("dst_score", [P, NT * HEADS])
        with nc.cleanup_on_exit():
            make_schedule(nc, c, w["src"], w["dst"], dram)
        with nc.cleanup_on_exit():
            gat_project(nc, c, w)
        with nc.sbuf_tensor("a_sums", [P, NT * A_ACC], F32) as sums:
            with nc.cleanup_on_exit():
                edge_stage(nc, c, "ea", HEADS, 0.2, c.a_table, A_ROW, A_ACC, HEADS * HC, -BIG, sums)
            with nc.cleanup_on_exit():
                gat_finish(nc, c, w, sums)
        with nc.sbuf_tensor("w_comb", [P, INNER // P, D], F32) as w_comb:
            with nc.sbuf_tensor("pooled", [P, INNER // P, D + 1], F32) as pooled:
                with nc.cleanup_on_exit():
                    slice_tokens(nc, c, w, pooled)
                with nc.cleanup_on_exit():
                    token_attention(nc, c, w, pooled, w_comb)
            with nc.cleanup_on_exit():
                hyp_project(nc, c, w, w_comb)
        with nc.sbuf_tensor("b_sums", [P, NT * B_ACC], F32) as sums:
            with nc.cleanup_on_exit():
                edge_stage(nc, c, "eb", 1, None, c.b_table, B_ROW, B_ACC, D + 1, -1e9, sums)
            with nc.cleanup_on_exit():
                hyp_finish(nc, c, w, sums)
        c.places = sb("places", [P, NT * 2], I32)
        c.places_f, c.shares = sb("places_f", [P, NT * 2]), sb("shares", [P, NT * 2])
        c.next_row = sb("next_row", [P, NX])
        c.slot_row, c.slot_expert = (sb(name, [1, SLOTS], I32) for name in ("slot_row", "slot_expert"))
        c.routed, c.y_rows = dram("routed", [NX * REG, D]), dram("y_rows", [SLOTS * P, D])
        with nc.cleanup_on_exit():
            route(nc, c, w)
        with nc.cleanup_on_exit():
            plan_tiles(nc, c)
        with nc.cleanup_on_exit():
            experts(nc, c, w)
        with nc.cleanup_on_exit():
            combine(nc, c, out)


_WEIGHTS = ["L0_gnn_W", "L0_gnn_att_src", "L0_gnn_att_dst", "L0_gnn_bias", "L0_gnn_Wp", "L0_gnn_bp",
            "L0_ffn_W_fx", "L0_ffn_b_fx", "L0_ffn_W_x", "L0_ffn_b_x", "L0_ffn_W_slice", "L0_ffn_b_slice",
            "L0_ffn_W_q", "L0_ffn_W_k", "L0_ffn_W_v", "L0_ffn_W_out", "L0_ffn_b_out", "L0_ffn_temperature",
            "L1_gnn_W", "L1_gnn_b", "L1_gnn_mag_w", "L1_gnn_mag_b", "L1_gnn_attn_w",
            "L1_ffn_Wg", "L1_ffn_bg", "L1_ffn_bias", "L1_ffn_W1", "L1_ffn_b1", "L1_ffn_W2", "L1_ffn_b2"]


def kernel(**inputs):
    import numpy as _np
    import concourse.bacc as _bacc
    from concourse import mybir as _mybir
    from concourse.bass_utils import run_bass_kernel_spmd as _run

    def padded(a, shape, fill):
        a = _np.asarray(a)
        out = _np.full(shape, fill, a.dtype)
        out.reshape(-1)[:a.size] = a.reshape(-1)
        return out

    arrays = {
        "x": padded(inputs["x"], (NPAD, D), 0),
        "src": padded(inputs["src"], (K, P), 0),
        "dst": padded(inputs["dst"], (K, P), NPAD - 1),
    }
    for name in _WEIGHTS:
        arrays[name] = _np.ascontiguousarray(inputs[name])
    nc = _bacc.Bacc("TRN2", target_bir_lowering=False, num_devices=1)
    w = {name: nc.dram_tensor(name, a.shape, _mybir.dt.from_np(a.dtype), kind="ExternalInput").ap() for name, a in arrays.items()}
    out = nc.dram_tensor("out", (NPAD, D), F32, kind="ExternalOutput").ap()
    program(nc, w, out)
    r = _run(nc, [arrays], core_ids=[0])
    return r.results[0]["out"][:N]
```

```python
from contextlib import ExitStack

import numpy as np
import concourse.bass as bass
from concourse import mybir

F32 = mybir.dt.float32
BF16 = mybir.dt.bfloat16
I32 = mybir.dt.int32
ALU = mybir.AluOpType
ACT = mybir.ActivationFunctionType
AX = mybir.AxisListType

P = 128
N = 12500
D = 256
E = 200000
NT = -(-N // P)
NPAD = NT * P
ET = -(-E // P)
G = 32
NG = 2 * (-(-(ET + NT - 1) // (2 * G)))
K = NG * G
KC = K // P
EPAD = K * P
T = 7
NB = NT // T
assert NB * T == NT and NB % 2 == 0 and KC * P == K
BIG = float(2 ** 100)
EPS = 1e-5
HEADS, HC = 4, 32
A_ROW = HEADS * HC + HEADS
A_ACC = A_ROW + HEADS
B_ROW = D + 2
B_ACC = D + 1
FH, FG = 8, 64
INNER = FH * FG
NX, FF = 8, 512
FB = FF // P
W1, B1 = 2 * FF, 2 * FF + FB
UPW = B1 + D
REG = (NT + 1) * P
SLOTS = -(-(2 * NT + NX) // 4) * 4


class Core:
    pass


def batches(eng):
    return eng.Fori(0, NB // 2)


def groups(eng):
    return eng.Fori(0, NG // 2)


def prime(eng, *events):
    for event in events:
        eng.sem_inc(event, 1)


def make_constants(nc, c, sb, sem):
    c.ident = sb("ident", [P, P])
    c.ramp_row = sb("ramp_row", [P, P])
    c.ramp_col = sb("ramp_col", [P, 1])
    c.minus_ramp = sb("minus_ramp", [P, 1])
    c.ones = sb("ones", [P, P])
    c.ones_bf = sb("ones_bf", [P, P], BF16)
    c.valid = sb("valid", [P, NT])
    c.eps = sb("eps", [P, 1])
    ints = sb("ramp_ints", [P, P + 1 + NT], I32)
    ramps_made, ramps_copied, constants_made = sem("ramps_made"), sem("ramps_copied"), sem("constants_made")
    with nc.Block() as block:
        @block.gpsimd
        def _(pool):
            nc.gpsimd.iota(ints[:, 0:P], [[1, P]], base=0, channel_multiplier=0)
            nc.gpsimd.iota(ints[:, P:P + 1], [[1, 1]], base=0, channel_multiplier=1)
            nc.gpsimd.iota(ints[:, P + 1:], [[P, NT]], base=0, channel_multiplier=1).then_inc(ramps_made, 1)

        @block.vector
        def _(dve):
            nc.vector.memset(c.ones[:, :], 1.0)
            nc.vector.memset(c.eps[:, :], EPS)
            nc.vector.memset(c.ones_bf[:, :], 1.0)
            dve.wait_ge(ramps_made, 1)
            nc.vector.tensor_copy(c.ramp_row[:, :], ints[:, 0:P])
            nc.vector.tensor_copy(c.ramp_col[:, :], ints[:, P:P + 1])
            nc.vector.tensor_copy(c.valid[:, :], ints[:, P + 1:]).then_inc(ramps_copied, 1)
            dve.wait_ge(ramps_copied, 1)
            nc.vector.tensor_scalar(c.minus_ramp[:, :], c.ramp_col[:, :], -1.0, None, ALU.mult)
            nc.vector.tensor_scalar(c.ident[:, :], c.ramp_row[:, :], c.ramp_col[:, 0:1], None, ALU.is_equal)
            nc.vector.tensor_scalar(c.valid[:, :], c.valid[:, :], float(N), None, ALU.is_lt).then_inc(constants_made, 1)
            dve.wait_ge(constants_made, 1)


def make_schedule(nc, c, src, dst, dram):
    flat = dram("dst_flat", [1, EPAD + 2], F32)
    c.keep_prev = dram("keep_prev", [K, P], F32)
    c.keep_next = dram("keep_next", [K, P], F32)
    c.local_rows = dram("local_rows", [1, EPAD], BF16)
    c.step_rows = dram("step_rows", [4, K], F32)
    c.step_tiles = dram("step_tiles", [1, K], I32)
    c.edge_src = dram("edge_src", [NG, P, G], I32)
    c.edge_place = dram("edge_place", [NG, P, G], F32)
    small, tiles = c.step_rows, c.step_tiles
    with ExitStack() as ctx:
        def sb(name, shape, dt=F32):
            return ctx.enter_context(nc.sbuf_tensor(name, shape, dt))

        def sem(name):
            return nc.alloc_semaphore(name)

        dst_in = sb("dst_in", [P, KC, P], I32)
        last = sb("last", [P, KC], I32)
        key = sb("key", [P, KC])
        step = sb("step", [P, KC])
        step_i = sb("step_i", [P, KC], I32)
        diag = sb("diag", [P, KC, P])
        keys = sb("keys", [P, K])
        below = sb("below", [P, K])
        t_f = sb("t_f", [P, KC])
        t_i = sb("t_i", [P, KC], I32)
        n_f = sb("n_f", [P, KC])
        n_i = sb("n_i", [P, KC], I32)
        n_p = sb("n_p", [P, KC])
        rows_i = sb("rows_i", [P, 2, KC, P], I32)
        dst_f = sb("dst_f", [P, KC, P])
        src_f = sb("src_f", [P, KC, P])
        local = sb("local", [P, KC, P])
        local_bf = sb("local_bf", [P, KC, P], BF16)
        near = sb("near", [P, 2, KC, P])
        one_seg = sb("one_seg", [P, KC])
        four = sb("four", [P, 4, KC])
        turned_src = sb("turned_src", [P, K], I32)
        turned_place = sb("turned_place", [P, K])
        margin = sb("margin", [1, 2])
        dst_loaded, ramp, told, dv = sem("dst_loaded"), sem("step_ramp"), sem("step_told"), sem("schedule_vector")
        keys_spread, rows_found, flat_stored, near_loaded = sem("keys_spread"), sem("rows_found"), sem("flat_stored"), sem("near_loaded")
        turned, all_stored, by_edge_stored = sem("turned"), sem("all_stored"), sem("by_edge_stored")
        with nc.Block() as block:
            @block.sync
            def _(sp):
                sp.dma_start(dst_in[:, :, :], dst.rearrange("(j p) e -> p j e", p=P)).then_inc(dst_loaded, 16)
                sp.wait_ge(dv, 7)
                sp.dma_start(flat[0, 1:1 + EPAD].rearrange("(j p e) -> p j e", p=P, e=P), dst_f[:, :, :]).then_inc(flat_stored, 16)
                sp.dma_start(flat[0:1, 0:1], margin[:, 0:1]).then_inc(flat_stored, 16)
                sp.dma_start(flat[0:1, EPAD + 1:EPAD + 2], margin[:, 1:2]).then_inc(flat_stored, 16)
                sp.wait_ge(flat_stored, 48)
                sp.dma_start(near[:, 0, :, :], flat[0, 0:EPAD].rearrange("(j p e) -> p j e", p=P, e=P)).then_inc(near_loaded, 16)
                sp.dma_start(near[:, 1, :, :], flat[0, 2:2 + EPAD].rearrange("(j p e) -> p j e", p=P, e=P)).then_inc(near_loaded, 16)
                sp.wait_ge(dv, 12)
                sp.dma_start(c.keep_prev.rearrange("(j p) e -> p j e", p=P), near[:, 0, :, :]).then_inc(all_stored, 16)
                sp.dma_start(c.keep_next.rearrange("(j p) e -> p j e", p=P), near[:, 1, :, :]).then_inc(all_stored, 16)
                sp.dma_start(c.local_rows[0, :].rearrange("(j p e) -> p j e", p=P, e=P), local_bf[:, :, :]).then_inc(all_stored, 16)
                sp.dma_start(tiles[0, :].rearrange("(j p one) -> p j one", p=P, one=1), n_i[:, :].rearrange("p (j one) -> p j one", one=1), allow_slow_non_contiguous=True).then_inc(all_stored, 16)
                for r in range(4):
                    sp.dma_start(small[r, :].rearrange("(j p one) -> p j one", p=P, one=1), four[:, r, :].rearrange("p (j one) -> p j one", one=1), allow_slow_non_contiguous=True).then_inc(all_stored, 16)
                sp.wait_ge(all_stored, 16 * 8)
                sp.wait_ge(dv, 13)
                sp.dma_start(c.edge_src.rearrange("g p s -> p g s"), turned_src[:, :].rearrange("p (g s) -> p g s", s=G)).then_inc(by_edge_stored, 16)
                sp.dma_start(c.edge_place.rearrange("g p s -> p g s"), turned_place[:, :].rearrange("p (g s) -> p g s", s=G)).then_inc(by_edge_stored, 16)
                sp.wait_ge(by_edge_stored, 32)

            @block.gpsimd
            def _(pool):
                nc.gpsimd.iota(step_i[:, :], [[P, KC]], base=0, channel_multiplier=1).then_inc(ramp, 1)
                pool.wait_ge(dv, 5)
                for j in range(KC):
                    for which, rows in ((0, src), (1, dst)):
                        nc.gpsimd.indirect_dma_start(rows_i[:, which, j, :], None, rows,
                                                     bass.IndirectOffsetOnAxis(ap=t_i[:, j:j + 1], axis=0)).then_inc(rows_found, 16)

            @block.tensor
            def _(pe):
                pe.wait_ge(dv, 3)
                for j in range(KC):
                    last_mm = nc.tensor.matmul(c.bank[j // 4][:, (j % 4) * P:(j % 4 + 1) * P], c.ones[:, :], diag[:, j, :], start=True, stop=True)
                last_mm.then_inc(keys_spread, 1)
                pe.wait_ge(dv, 9)
                for j in range(KC):
                    nc.tensor.transpose(c.bank[j // 4][:, (j % 4) * P:(j % 4 + 1) * P], local[:, j, :], c.ident[:, :])
                    last_mm = nc.tensor.transpose(c.bank[4 + j // 4][:, (j % 4) * P:(j % 4 + 1) * P], src_f[:, j, :], c.ident[:, :])
                last_mm.then_inc(turned, 1)

            @block.vector
            def _(dve):
                v = nc.vector
                v.memset(margin[:, 0:1], -5.0)
                v.memset(margin[:, 1:2], -7.0)
                dve.wait_ge(ramp, 1)
                v.tensor_copy(step[:, :], step_i[:, :])
                dve.wait_ge(dst_loaded, 16)
                v.tensor_scalar(last[:, :], dst_in[:, :, P - 1], 7, None, ALU.arith_shift_right).then_inc(dv, 1)
                dve.wait_ge(dv, 1)
                v.tensor_tensor(key[:, :], last[:, :], step[:, :], ALU.add).then_inc(dv, 1)
                dve.wait_ge(dv, 2)
                for j in range(KC):
                    op = v.tensor_scalar(diag[:, j, :], c.ident[:, :], key[:, j:j + 1], None, ALU.mult)
                op.then_inc(dv, 1)
                dve.wait_ge(keys_spread, 1)
                for b in range(-(-KC // 4)):
                    w = min(512, K - b * 512)
                    op = v.tensor_copy(keys[:, b * 512:b * 512 + w], c.bank[b][:, 0:w])
                op.then_inc(dv, 1)
                dve.wait_ge(dv, 4)
                for j in range(KC):
                    v.tensor_scalar(below[:, :], keys[:, :], step[:, j:j + 1], 0.0, ALU.is_lt, ALU.add, accum_out=t_f[:, j:j + 1]).then_inc(told, 1)
                    dve.wait_ge(told, j + 1)
                v.tensor_copy(t_i[:, :], t_f[:, :]).then_inc(dv, 1)
                v.tensor_tensor(n_f[:, :], step[:, :], t_f[:, :], ALU.subtract).then_inc(dv, 1)
                dve.wait_ge(dv, 6)
                v.tensor_copy(n_i[:, :], n_f[:, :])
                v.tensor_scalar(n_p[:, :], n_f[:, :], float(P), None, ALU.mult)
                dve.wait_ge(rows_found, 32 * KC)
                v.tensor_copy(dst_f[:, :, :], rows_i[:, 1, :, :]).then_inc(dv, 1)
                v.tensor_copy(src_f[:, :, :], rows_i[:, 0, :, :])
                dve.wait_ge(dv, 7)
                for j in range(KC):
                    op = v.tensor_scalar(local[:, j, :], dst_f[:, j, :], n_p[:, j:j + 1], -1.0, ALU.subtract, ALU.max)
                op.then_inc(dv, 1)
                dve.wait_ge(dv, 8)
                v.tensor_scalar(local[:, :, :], local[:, :, :], float(P), None, ALU.min).then_inc(dv, 1)
                dve.wait_ge(dv, 9)
                v.tensor_copy(local_bf[:, :, :], local[:, :, :])
                v.tensor_tensor(one_seg[:, :], dst_f[:, :, 0], dst_f[:, :, P - 1], ALU.is_equal)
                v.tensor_copy(four[:, 3, :], local[:, :, 0])
                dve.wait_ge(near_loaded, 32)
                for w in range(2):
                    op = v.tensor_tensor(near[:, w, :, :], near[:, w, :, :], dst_f[:, :, :], ALU.is_equal)
                op.then_inc(dv, 1)
                dve.wait_ge(dv, 10)
                v.tensor_copy(four[:, 2, :], near[:, 0, :, 0])
                v.tensor_tensor(four[:, 0, :], near[:, 0, :, 0], one_seg[:, :], ALU.mult)
                v.tensor_tensor(four[:, 1, :], near[:, 1, :, P - 1], one_seg[:, :], ALU.mult).then_inc(dv, 1)
                dve.wait_ge(dv, 11)
                v.tensor_scalar(near[:, :, :, :], near[:, :, :, :], 1.0, BIG, ALU.subtract, ALU.mult)
                v.tensor_scalar(four[:, 0:2, :], four[:, 0:2, :], 1.0, BIG, ALU.subtract, ALU.mult).then_inc(dv, 1)
                dve.wait_ge(turned, 1)
                for b in range(-(-KC // 4)):
                    w = min(512, K - b * 512)
                    v.tensor_copy(turned_place[:, b * 512:b * 512 + w], c.bank[b][:, 0:w])
                    op = v.tensor_copy(turned_src[:, b * 512:b * 512 + w], c.bank[4 + b][:, 0:w])
                op.then_inc(dv, 1)
                dve.wait_ge(dv, 13)


class Front:

    def __init__(self, nc, ctx, tag, deep=1):
        def sb(name, shape, dt=F32):
            return ctx.enter_context(nc.sbuf_tensor(f"{name}_{tag}", shape, dt))

        def sem(name):
            return nc.alloc_semaphore(f"{name}_{tag}")

        self.x = sb("x", [P, 2, T, D])
        self.stats = sb("stats", [P, 2, T, 6])
        self.mv = sb("mv", [P, 2, T, 2])
        self.sd = sb("sd", [P, 2, T])
        self.rstd = sb("rstd", [P, 2, T])
        self.shift = sb("shift", [P, 2, T])
        self.deep = deep
        self.xn = sb("xn", [P, deep, T, D + 1])
        self.xt = sb("xt", [P, T, 2, P])
        self.loaded = [sem("x_loaded0"), sem("x_loaded1")]
        self.passed = sem("passed")
        self.stats_made, self.mv_made, self.sd_made = sem("stats_made"), sem("mv_made"), sem("sd_made")
        self.rstd_made, self.shift_made, self.xn_made = sem("rstd_made"), sem("shift_made"), sem("xn_made")
        self.turned, self.xt_made = sem("turned"), sem("xt_made")

    def load(self, sp, nc, x_dram, b, p):
        nc.sync.dma_start(self.x[:, p, :, :], x_dram.rearrange("(n p) d -> p n d", p=P)[:, bass.ds(b * T, T), :]).then_inc(self.loaded[p], 16)

    def sync(self, sp, nc, x_dram, store):
        for p in range(2):
            self.load(sp, nc, x_dram, p, p)
        with sp.Fori(0, NB // 2 - 1) as pair:
            for p in range(2):
                sp.wait_ge(self.xn_made, (pair * 2 + p + 1) * T)
                sp.sem_inc(self.passed, 1)
                self.load(sp, nc, x_dram, pair * 2 + p + 2, p)
                store(pair * 2 + p, p)
        for p in range(2):
            store(NB - 2 + p, p)

    def vector(self, dve, nc, b, pair, p, update=None):
        self.moments(dve, nc, b, pair, p, update)
        self.scales(dve, nc, b, p)

    def moments(self, dve, nc, b, pair, p, update=None):
        dve.wait_ge(self.loaded[p], 16 * pair + 16)
        if update:
            update()
        for i in range(T):
            op = nc.vector.bn_stats(self.stats[:, p, i, :], self.x[:, p, i, :])
        op.then_inc(self.stats_made, 1)
        dve.wait_ge(self.stats_made, b + 1)
        dve.sem_inc(self.passed, 1)
        for i in range(T):
            op = nc.vector.bn_aggr(self.mv[:, p, i, :], self.stats[:, p, i, :])
        op.then_inc(self.mv_made, 1)

    def scales(self, dve, nc, b, p):
        dve.wait_ge(self.sd_made, b + 1)
        nc.vector.reciprocal(self.rstd[:, p, :], self.sd[:, p, :]).then_inc(self.rstd_made, 1)
        dve.wait_ge(self.rstd_made, b + 1)
        nc.vector.scalar_tensor_tensor(self.shift[:, p, :], self.mv[:, p, :, 0], -1.0, self.rstd[:, p, :], ALU.mult, ALU.mult).then_inc(self.shift_made, 1)

    def scalar(self, act, nc, c, b, p, used, also=None, more=0, free=None):
        act.wait_ge(self.mv_made, b + 1)
        nc.scalar.activation(self.sd[:, p, :], self.mv[:, p, :, 1], ACT.Sqrt, bias=c.eps[:, 0:1]).then_inc(self.sd_made, 1)
        act.wait_ge(self.shift_made, b + 1)
        act.wait_ge(used, 1 + b * T)
        if free:
            free()
        for i in range(T + 1 + more):
            if i < T:
                nc.scalar.activation(self.xn[:, p % self.deep, i, 0:D], self.x[:, p, i, :], ACT.Identity,
                                     bias=self.shift[:, p, i:i + 1], scale=self.rstd[:, p, i:i + 1]).then_inc(self.xn_made, 1)
            if 1 <= i <= T:
                act.wait_ge(self.turned, b * T + i)
                nc.scalar.copy(self.xt[:, i - 1, :, :].rearrange("p c n -> p (c n)"), c.bank[(i - 1) % 2][:, 0:D]).then_inc(self.xt_made, 1)
            if also:
                also(i)

    def tensor(self, pe, nc, c, b, p, i):
        pe.wait_ge(self.xn_made, b * T + i + 1)
        pe.wait_ge(self.xt_made, 1 + b * T + max(i - 1, 0))
        for h in range(2):
            op = nc.tensor.transpose(c.bank[i % 2][:, h * P:(h + 1) * P], self.xn[:, p % self.deep, i, h * P:(h + 1) * P], c.ident[:, :])
        op.then_inc(self.turned, 1)


def gat_project(nc, c, w):
    with ExitStack() as ctx:
        def sb(name, shape, dt=F32):
            return ctx.enter_context(nc.sbuf_tensor(name, shape, dt))

        def sem(name):
            return nc.alloc_semaphore(name)

        HW = HEADS * HC
        w_ext = sb("w_ext", [P, 2, HW + 2 * HEADS])
        w_t = sb("w_t", [P, 2, P])
        att = sb("att", [P, 2])
        att_block = sb("att_block", [P, 2 * HEADS])
        head_of = sb("head_of", [P, HEADS])
        head_lo = sb("head_lo", [P, HEADS])
        rows = sb("rows", [P, 2, T, A_ROW])
        w_loaded, w_turned, block_made, w_copied, w_folded, w_ready = (sem(s) for s in ("gp_w_loaded", "gp_w_turned", "gp_block_made", "gp_w_copied", "gp_w_folded", "gp_w_ready"))
        projected, rows_copied, rows_stored0, rows_stored1 = sem("gp_projected"), sem("gp_rows_copied"), sem("gp_rows_stored0"), sem("gp_rows_stored1")
        rows_stored = [rows_stored0, rows_stored1]
        f = Front(nc, ctx, "gp")
        with nc.Block() as block:
            @block.sync
            def _(sp):
                sp.dma_start(w_ext[:, :, 0:HW], w["L0_gnn_W"].rearrange("(c p) n -> p c n", p=P)).then_inc(w_loaded, 16)
                sp.dma_start(att[:, 0:1], w["L0_gnn_att_src"].rearrange("h (c one) -> (h c) one", one=1)).then_inc(w_loaded, 16)
                sp.dma_start(att[:, 1:2], w["L0_gnn_att_dst"].rearrange("h (c one) -> (h c) one", one=1)).then_inc(w_loaded, 16)
                for p in range(2):
                    sp.sem_inc(rows_stored[p], 16)

                def store(b, p):
                    sp.wait_ge(rows_copied, 1 + (b + 1) * T)
                    sp.sem_inc(f.passed, 1)
                    nc.sync.dma_start(c.a_table.rearrange("(n p) d -> p n d", p=P)[:, bass.ds(b * T, T), :], rows[:, p, :, :]).then_inc(rows_stored[p], 16)

                f.sync(sp, nc, c.x_in, store)
                for p in range(2):
                    sp.wait_ge(rows_stored[p], 16 + 16 * (NB // 2))

            @block.vector
            def _(dve):
                prime(dve, rows_copied)
                v = nc.vector
                v.tensor_scalar(head_of[:, :], c.ramp_row[:, 0:HEADS], float(HC), None, ALU.mult).then_inc(block_made, 1)
                dve.wait_ge(block_made, 1)
                v.tensor_scalar(head_lo[:, :], head_of[:, :], c.ramp_col[:, 0:1], None, ALU.is_le)
                v.tensor_scalar(head_of[:, :], head_of[:, :], float(HC), c.ramp_col[:, 0:1], ALU.add, ALU.is_gt).then_inc(block_made, 1)
                dve.wait_ge(block_made, 2)
                v.tensor_tensor(head_of[:, :], head_of[:, :], head_lo[:, :], ALU.mult).then_inc(block_made, 1)
                dve.wait_ge(block_made, 3)
                dve.wait_ge(w_loaded, 48)
                for s in range(2):
                    op = v.tensor_scalar(att_block[:, s * HEADS:(s + 1) * HEADS], head_of[:, :], att[:, s:s + 1], None, ALU.mult)
                op.then_inc(block_made, 1)
                dve.wait_ge(w_turned, 1)
                v.tensor_copy(w_t[:, :, :].rearrange("p c n -> p (c n)"), c.bank[2][:, 0:2 * P]).then_inc(w_copied, 1)
                dve.wait_ge(w_folded, 1)
                v.tensor_copy(w_ext[:, :, HW:], c.bank[3][:, 0:4 * HEADS].rearrange("p (c n) -> p c n", c=2)).then_inc(w_ready, 1)

                def work(b, pair, p, more):
                    f.scales(dve, nc, b, p)
                    if more:
                        f.moments(dve, nc, b + 1, pair + p, 1 - p)
                    dve.wait_ge(rows_stored[p], 16 * pair + 16)
                    for i in range(T):
                        dve.wait_ge(projected, 1 + b * T + i + 1)
                        v.tensor_copy(rows[:, p, i, :], c.bank[2 + i % 2][:, 0:A_ROW])
                        op = v.tensor_copy(c.dst_score[:, bass.ds((b * T + i) * HEADS, HEADS)], c.bank[2 + i % 2][:, A_ROW:A_ROW + HEADS])
                        op.then_inc(rows_copied, 1)

                f.moments(dve, nc, 0, 0, 0)
                with dve.Fori(0, NB // 2 - 1) as pair:
                    for p in range(2):
                        work(pair * 2 + p, pair, p, True)
                for p in range(2):
                    work(NB - 2 + p, NB // 2 - 1, p, p == 0)

            @block.scalar
            def _(act):
                prime(act, f.xt_made)
                with batches(act) as pair:
                    for p in range(2):
                        b = pair * 2 + p
                        f.scalar(act, nc, c, b, p, projected)

            @block.tensor
            def _(pe):
                prime(pe, projected)
                pe.wait_ge(w_loaded, 48)
                for ch in range(2):
                    op = nc.tensor.transpose(c.bank[2][:, ch * P:(ch + 1) * P], w_ext[:, ch, 0:HW], c.ident[:, :])
                op.then_inc(w_turned, 1)
                pe.wait_ge(w_copied, 1)
                pe.wait_ge(block_made, 4)
                for ch in range(2):
                    op = nc.tensor.matmul(c.bank[3][:, ch * 2 * HEADS:(ch + 1) * 2 * HEADS], w_t[:, ch, :], att_block[:, :], start=True, stop=True)
                op.then_inc(w_folded, 1)
                pe.wait_ge(w_ready, 1)
                with batches(pe) as pair:
                    for p in range(2):
                        b = pair * 2 + p
                        for i in range(T + 1):
                            if i < T:
                                f.tensor(pe, nc, c, b, p, i)
                            if i >= 1:
                                k = i - 1
                                pe.wait_ge(f.xt_made, 1 + b * T + i)
                                pe.wait_ge(rows_copied, 1 + b * T + max(k - 1, 0))
                                for ch in range(2):
                                    op = nc.tensor.matmul(c.bank[2 + k % 2][:, 0:HW + 2 * HEADS], f.xt[:, k, ch, :], w_ext[:, ch, :], start=(ch == 0), stop=(ch == 1))
                                op.then_inc(projected, 1)


def edge_stage(nc, c, tag, heads, leaky, table, row, width, score_at, floor, acc):
    H, Q = heads, 4
    HS = H * G
    TL = 16
    multi = H > 1
    with ExitStack() as ctx:
        def sb(name, shape, dt=F32):
            return ctx.enter_context(nc.sbuf_tensor(f"{tag}_{name}", shape, dt))

        def sem(name):
            return nc.alloc_semaphore(f"{tag}_{name}")

        rows = sb("rows", [P, 2, G, row])
        src_now = sb("src_now", [P, 2, G], I32)
        keep_prev = sb("keep_prev", [HS, 2, P])
        keep_next = sb("keep_next", [HS, 2, P])
        place = sb("place", [P, 2, G])
        step_rows = sb("step_rows", [1, 2, 4, G])
        tile_now = sb("tile_now", [1, 2, G], I32)
        place_row = sb("place_row", [1, 2, G * P], BF16)
        away = sb("away", [P, 2, Q * P])
        node_of = sb("node_of", [P, 2, Q * P], BF16)
        dst_parts = sb("dst_parts", [P, NT * 3 * H], BF16)
        dst_rest = sb("dst_rest", [P, NT * H])
        dst_now = sb("dst_now", [P, HS])
        z = sb("z", [P, HS])
        zt = sb("zt", [HS, P])
        zf = zt if floor is None else sb("zf", [HS, P])
        scan0 = sb("scan0", [HS, P])
        fwd = sb("fwd", [HS, P])
        scan1 = sb("scan1", [HS, P])
        top = sb("top", [HS, P])
        diff = sb("diff", [HS, P])
        ex = sb("ex", [HS, P])
        fm = sb("fm", [HS, P])
        pen_f = sb("pen_f", [1, H, G + 1])
        pen_b = sb("pen_b", [1, H, G + 1])
        in_f = sb("in_f", [1, H, G + 1])
        in_b = sb("in_b", [1, H, G + 1])
        out_f = sb("out_f", [1, H, G + 1])
        out_b = sb("out_b", [1, H, G + 1])
        start_f = sb("start_f", [1, HS]) if multi else out_f[:, 0, 0:G]
        start_b = sb("start_b", [1, HS]) if multi else out_b[:, 0, 1:]
        drop = sb("drop", [1, H])
        first = sb("first", [1, P])
        dropped_by = sb("dropped_by", [P, H])
        scale = sb("scale", [P, H])
        weight = sb("weight", [P, 2 * H, G])
        hot = sb("hot", [P, 2, Q, P])
        msg = sb("msg", [P, 2, Q, width]) if multi else None
        gathered = [sem("gathered0"), sem("gathered1")]
        kept = [sem("kept0"), sem("kept1")]
        placed = [sem("placed0"), sem("placed1")]
        src_staged = [sem("src_staged0"), sem("src_staged1")]
        passed, passed_sp, passed_pe = sem("passed"), sem("passed_sp"), sem("passed_pe")
        place_spread, node_of_made, scored = sem("place_spread"), sem("node_of_made"), sem("scored")
        z_made, z_turned, zt_made, scan0_made, row_f, start_f_made, col_f = (sem(s) for s in (
            "z_made", "z_turned", "zt_made", "scan0_made", "row_f", "start_f_made", "col_f"))
        fwd_made, scan1_made, row_b, start_b_made, col_b, dropped_spread, top_made, diff_made = (sem(s) for s in (
            "fwd_made", "scan1_made", "row_b", "start_b_made", "col_b", "dropped_spread", "top_made", "diff_made"))
        ex_made, fm_made, weight_turned, weight_made, dropped, scale_made = (sem(s) for s in (
            "ex_made", "fm_made", "weight_turned", "weight_made", "dropped", "scale_made"))
        in_f_made, out_f_made, in_b_made, out_b_made, diff0, rescaled = (sem(s) for s in (
            "in_f_made", "out_f_made", "in_b_made", "out_b_made", "diff0", "rescaled"))
        hot_made, msg_made, msg_w_made, summed, added = (sem(s) for s in ("hot_made", "msg_made", "msg_w_made", "summed", "added"))
        set_up, away_made, parts_made, dst_summed = (sem(s) for s in ("set_up", "away_made", "parts_made", "dst_summed"))

        spread_bank = [c.bank[0], c.bank[1]]
        s_bank, t_bank = c.bank[2], c.bank[3]
        ring = c.bank[4:8]
        w_cols = t_bank[:, 0:2 * HS]


        def tiles_now(engine, p, k, count):
            return nc.values_load_multi_w_load_instructions(tile_now[0:1, p, k:k + count], engines=[engine], min_val=0, max_val=NT - 1,
                                                              skip_runtime_bounds_check_because="a step's node tile is some edge's, below NT by construction")[1]

        with nc.Block() as block:
            @block.sync
            def _(sp):
                def load(g, p):
                    for h in range(H):
                        nc.sync.dma_start(keep_prev[h * G:(h + 1) * G, p, :], c.keep_prev[bass.ds(g * G, G), :]).then_inc(kept[p], 16)
                        nc.sync.dma_start(keep_next[h * G:(h + 1) * G, p, :], c.keep_next[bass.ds(g * G, G), :]).then_inc(kept[p], 16)
                    nc.sync.dma_start(place_row[:, p, :], c.local_rows[:, bass.ds(g * G * P, G * P)]).then_inc(placed[p], 16)
                    nc.sync.dma_start(place[:, p, :], c.edge_place[bass.ds(g, 1), :, :].rearrange("g p s -> (g p) s")).then_inc(placed[p], 16)
                    nc.sync.dma_start(tile_now[:, p, :], c.step_tiles[:, bass.ds(g * G, G)]).then_inc(placed[p], 16)
                    nc.sync.dma_start(step_rows[:, p, :, :], c.step_rows[:, bass.ds(g * G, G)].rearrange("(o r) k -> o r k", o=1)).then_inc(placed[p], 16)

                def load_sources(g, p):
                    nc.sync.dma_start(src_now[:, p, :], c.edge_src[bass.ds(g, 1), :, :].rearrange("g p s -> (g p) s")).then_inc(src_staged[p], 16)

                def next_loads(pair, p, sources):
                    g = pair * 2 + p
                    if sources:
                        sp.wait_ge(gathered[1 - p], 16 * G * (pair + 1 + p))
                        sp.sem_inc(passed_sp, 1)
                        load_sources(g + 3, 1 - p)
                    sp.wait_ge(added, 1 + (g + 1) * G)
                    sp.sem_inc(passed_sp, 1)
                    load(g + 2, p)

                for p in range(2):
                    load_sources(p, p)
                for p in range(2):
                    load(p, p)
                sp.wait_ge(gathered[0], 16 * G)
                load_sources(2, 0)
                with sp.Fori(0, NG // 2 - 2) as pair:
                    for p in range(2):
                        next_loads(pair, p, True)
                for p in range(2):
                    next_loads(NG // 2 - 2, p, p == 0)

            @block.gpsimd
            def _(pool):
                def gather(p, n, used=None):
                    pool.wait_ge(src_staged[p], 16 * n + 16)
                    pool.sem_inc(passed, 1)
                    for s in range(G):
                        if used is not None and s % Q == 0:
                            pool.wait_ge(summed, 1 + used + s + Q)
                            pool.sem_inc(passed, 1)
                        nc.gpsimd.indirect_dma_start(rows[:, p, s, :], None, table,
                                                     bass.IndirectOffsetOnAxis(ap=src_now[:, p, s:s + 1], axis=0)).then_inc(gathered[p], 16)

                for p in range(2):
                    gather(p, 0)
                with pool.Fori(0, NG // 2 - 1) as pair:
                    for p in range(2):
                        gather(p, pair + 1, (pair * 2 + p) * G)

            @block.vector
            def _(dve):
                prime(dve, z_made, added, rescaled)
                v = nc.vector
                v.memset(pen_f[:, :, 0:1], -BIG)
                v.memset(pen_b[:, :, G:G + 1], -BIG)
                v.memset(in_b[:, :, G:G + 1], -BIG)
                v.memset(out_f[:, :, :], 0.0)
                v.memset(acc[:, :], 0.0).then_inc(set_up, 1)
                dve.wait_ge(set_up, 1)
                rest, parts = c.dst_score[:, 0:NT * H], dst_parts[:, :].rearrange("p (n j h) -> p j n h", j=3, h=H)
                for j in range(3):
                    v.tensor_copy(parts[:, j, :, :], rest.rearrange("p (n h) -> p n h", h=H)).then_inc(parts_made, 1)
                    dve.wait_ge(parts_made, 2 * j + 1)
                    if j < 2:
                        v.tensor_tensor(dst_rest[:, :].rearrange("p (n h) -> p n h", h=H), rest.rearrange("p (n h) -> p n h", h=H), parts[:, j, :, :], ALU.subtract).then_inc(parts_made, 1)
                        dve.wait_ge(parts_made, 2 * j + 2)
                        rest = dst_rest[:, :]
                with groups(dve) as pair:
                    for p in range(2):
                        g = pair * 2 + p

                        def plain_hot(q, s):
                            return v.tensor_scalar(hot[:, q % 2, s, :], c.ramp_row[:, :], place[:, p, q * Q + s:q * Q + s + 1], None, ALU.is_equal)

                        def early_hot(q, lo, hi):
                            if multi:
                                for s in range(lo, hi):
                                    op = plain_hot(q, s)
                                if hi == Q:
                                    op.then_inc(hot_made, 1)

                        dve.wait_ge(scored, (g + 1) * (G // Q))
                        v.tensor_reduce(dst_now[:, :].rearrange("e (s h) -> e s h", h=H), s_bank[:, 0:3 * HS].rearrange("e (s j h) -> e s h j", j=3, h=H), AX.X, ALU.add).then_inc(dst_summed, 1)
                        dve.wait_ge(dst_summed, g + 1)
                        dve.wait_ge(gathered[p], (pair + 1) * 16 * G)
                        dve.wait_ge(z_turned, 1 + g)
                        v.tensor_tensor(z[:, :].rearrange("e (h s) -> e s h", h=H), rows[:, p, :, score_at:score_at + H],
                                        dst_now[:, :].rearrange("e (s h) -> e s h", h=H), ALU.add).then_inc(z_made, 1)
                        if leaky:
                            dve.wait_ge(z_made, 1 + 2 * g + 1)
                            v.scalar_tensor_tensor(z[:, :], z[:, :], leaky, z[:, :], ALU.mult, ALU.max).then_inc(z_made, 1)
                        dve.wait_ge(placed[p], 64 * (pair + 1))
                        v.tensor_copy(pen_f[:, :, 1:], step_rows[:, p, 0:1, :].broadcast_to([1, H, G]))
                        v.tensor_copy(pen_b[:, :, 0:G], step_rows[:, p, 1:2, :].broadcast_to([1, H, G]))
                        v.tensor_copy(in_f[:, :, 0:1], out_f[:, :, G:G + 1])
                        v.tensor_scalar(first[:, :], c.ramp_row[0:1, :], step_rows[:, p, 3, 0:1], None, ALU.is_equal)
                        dve.wait_ge(z_turned, 1 + g + 1)
                        if floor is not None:
                            v.tensor_scalar(zf[:, :], t_bank[0:HS, 0:P], floor, None, ALU.max)
                        v.tensor_copy(zt[:, :], t_bank[0:HS, 0:P]).then_inc(zt_made, 1)
                        dve.wait_ge(zt_made, g + 1)
                        dve.wait_ge(kept[p], (pair + 1) * 32 * H)
                        v.tensor_tensor_scan(scan0[:, :], keep_prev[:, p, :], zf[:, :], -BIG, ALU.add, ALU.max).then_inc(scan0_made, 1)
                        early_hot(0, 0, 2)
                        dve.wait_ge(row_f, g + 1)
                        v.tensor_copy(in_f[:, :, 1:], t_bank[0:1, P:P + HS].rearrange("o (h s) -> o h s", h=H)).then_inc(in_f_made, 1)
                        dve.wait_ge(in_f_made, g + 1)
                        v.tensor_tensor_scan(out_f[:, :, :].rearrange("o h s -> o (h s)"), pen_f[:, :, :].rearrange("o h s -> o (h s)"),
                                             in_f[:, :, :].rearrange("o h s -> o (h s)"), -BIG, ALU.add, ALU.max).then_inc(out_f_made, 1)
                        if multi:
                            dve.wait_ge(out_f_made, g + 1)
                            v.tensor_copy(start_f[:, :].rearrange("o (h s) -> o h s", h=H), out_f[:, :, 0:G]).then_inc(start_f_made, 1)
                        early_hot(0, 2, Q)
                        dve.wait_ge(col_f, g + 1)
                        v.tensor_tensor_scan(fwd[:, :], keep_prev[:, p, :], zf[:, :], t_bank[0:HS, 2 * P:2 * P + 1], ALU.add, ALU.max).then_inc(fwd_made, 1)
                        dve.wait_ge(fwd_made, g + 1)
                        v.tensor_tensor_scan(scan1[:, ::-1], keep_next[:, p, ::-1], fwd[:, ::-1], -BIG, ALU.add, ALU.max).then_inc(scan1_made, 1)
                        early_hot(1, 0, 2)
                        dve.wait_ge(row_b, g + 1)
                        v.tensor_copy(in_b[:, :, 0:G], t_bank[0:1, P:P + HS].rearrange("o (h s) -> o h s", h=H)).then_inc(in_b_made, 1)
                        dve.wait_ge(in_b_made, g + 1)
                        v.tensor_tensor_scan(out_b[:, :, :].rearrange("o h s -> o (h s)")[:, ::-1], pen_b[:, :, :].rearrange("o h s -> o (h s)")[:, ::-1],
                                             in_b[:, :, :].rearrange("o h s -> o (h s)")[:, ::-1], -BIG, ALU.add, ALU.max).then_inc(out_b_made, 1)
                        dve.wait_ge(out_b_made, g + 1)
                        v.tensor_tensor(drop[:, :], out_f[:, :, 0], out_b[:, :, 0], ALU.subtract).then_inc(diff0, 1)
                        if multi:
                            v.tensor_copy(start_b[:, :].rearrange("o (h s) -> o h s", h=H), out_b[:, :, 1:]).then_inc(start_b_made, 1)
                        dve.wait_ge(diff0, g + 1)
                        v.tensor_scalar(drop[:, :], drop[:, :], step_rows[:, p, 2, 0:1], None, ALU.mult).then_inc(dropped, 1)
                        early_hot(1, 2, Q)
                        dve.wait_ge(col_b, g + 1)
                        v.tensor_copy(dropped_by[:, :], t_bank[:, 2 * P + 4:2 * P + 4 + H]).then_inc(dropped_spread, 1)
                        v.tensor_tensor_scan(top[:, ::-1], keep_next[:, p, ::-1], fwd[:, ::-1], t_bank[0:HS, 2 * P + 2:2 * P + 3], ALU.add, ALU.max).then_inc(top_made, 1)
                        dve.wait_ge(top_made, g + 1)
                        v.tensor_tensor(diff[:, :], zt[:, :], top[:, :], ALU.subtract).then_inc(diff_made, 1)
                        if multi:
                            v.scalar_tensor_tensor(fm[:, :], keep_prev[:, p, :], -1.0 / BIG, top[:, :], ALU.mult, ALU.mult).then_inc(fm_made, 1)
                        n = tiles_now(mybir.EngineType.DVE, p, 0, 1)[0]
                        dve.wait_ge(scale_made, g + 1)
                        dve.wait_ge(added, 1 + g * G)
                        if multi:
                            cols = acc[:, bass.ds(n * width, HEADS * HC)].rearrange("p (h c) -> p h c", h=H)
                            v.tensor_tensor(cols, cols, scale[:, :].rearrange("p (h o) -> p h o", o=1).broadcast_to([P, H, HC]), ALU.mult)
                            v.tensor_tensor(acc[:, bass.ds(n * width + HEADS * HC, H)], acc[:, bass.ds(n * width + HEADS * HC, H)], scale[:, :], ALU.mult)
                            v.tensor_tensor(acc[:, bass.ds(n * width + A_ROW, H)], acc[:, bass.ds(n * width + A_ROW, H)],
                                            dropped_by[:, :], ALU.subtract).then_inc(rescaled, 1)
                        else:
                            v.tensor_scalar(acc[:, bass.ds(n * width, width)], acc[:, bass.ds(n * width, width)], scale[:, 0:1], None, ALU.mult).then_inc(rescaled, 1)
                        dve.wait_ge(weight_made, g + 1)

                        def prepare(q, s):
                            k = q * Q + s
                            if multi:
                                if q >= 2:
                                    one_hot = plain_hot(q, s)
                                message = v.tensor_tensor(msg[:, q % 2, s, 0:HEADS * HC].rearrange("p (h c) -> p h c", h=H),
                                                          rows[:, p, k, 0:HEADS * HC].rearrange("p (h c) -> p h c", h=H),
                                                          weight[:, 0:H, k:k + 1].broadcast_to([P, H, HC]), ALU.mult)
                            else:
                                one_hot = v.tensor_scalar(hot[:, q % 2, s, :], c.ramp_row[:, :], place[:, p, k:k + 1], weight[:, 0, k:k + 1], ALU.is_equal, ALU.mult)
                            if s == Q - 1:
                                if not multi or q >= 2:
                                    one_hot.then_inc(hot_made, 1)
                                if multi:
                                    message.then_inc(msg_made, 1)

                        for q in range(2):
                            for s in range(Q):
                                prepare(q, s)
                        for q in range(G // Q):
                            if q * Q % TL == 0:
                                node_tile = tiles_now(mybir.EngineType.DVE, p, q * Q, TL)
                            for s in range(Q):
                                k = q * Q + s
                                n = node_tile[k % TL]
                                dve.wait_ge(added, 1 + g * G + k) if k else dve.wait_ge(rescaled, 1 + g + 1)
                                dve.wait_ge(summed, 1 + g * G + k + 1)
                                v.tensor_tensor(acc[:, bass.ds(n * width, width)], acc[:, bass.ds(n * width, width)], ring[s][:, 0:width], ALU.add).then_inc(added, 1)
                                if q + 2 < G // Q:
                                    prepare(q + 2, s)

            @block.scalar
            def _(act):
                prime(act, node_of_made)

                def node_one_hots(g, q):
                    act.wait_ge(place_spread, g * (G // Q) + q + 1)
                    nc.scalar.activation(away[:, q % 2, :], spread_bank[q % 2][:, :], ACT.Abs, bias=c.minus_ramp[:, 0:1]).then_inc(away_made, 1)
                    act.wait_ge(away_made, g * (G // Q) + q + 1)
                    nc.scalar.activation(node_of[:, q % 2, :], away[:, q % 2, :], ACT.Relu, bias=c.ones[:, 0:1], scale=-1.0).then_inc(node_of_made, 1)

                def group(g, p, more):
                    act.wait_ge(dropped_spread, g + 1)
                    act.wait_ge(rescaled, 1 + g)
                    nc.scalar.activation(scale[:, :], dropped_by[:, :], ACT.Exp).then_inc(scale_made, 1)
                    act.wait_ge(diff_made, g + 1)
                    act.wait_ge(weight_turned, 1 + g)
                    nc.scalar.activation(ex[:, :], diff[:, :], ACT.Exp).then_inc(ex_made, 1)
                    act.wait_ge(weight_turned, 1 + g + 1)
                    act.wait_ge(summed, 1 + g * G)
                    nc.scalar.copy(weight[:, 0:(2 * H if multi else H), :].rearrange("e h s -> e (h s)"), w_cols[:, 0:(2 * HS if multi else HS)]).then_inc(weight_made, 1)
                    act.wait_ge(weight_made, g + 1)
                    for q in range(-1, G // Q):
                        if multi and q + 1 < G // Q:
                            act.wait_ge(summed, 1 + g * G + max(Q * q, 0))
                            nc.scalar.copy(msg[:, (q + 1) % 2, :, HEADS * HC:].rearrange("p s h -> p h s"), weight[:, :, (q + 1) * Q:(q + 2) * Q]).then_inc(msg_w_made, 1)
                        if more and q >= 0:
                            node_one_hots(g + 1, q)

                for q in range(G // Q):
                    node_one_hots(0, q)
                with act.Fori(0, NG // 2 - 1) as pair:
                    for p in range(2):
                        group(pair * 2 + p, p, True)
                for p in range(2):
                    group(NG - 2 + p, p, p == 0)

            @block.tensor
            def _(pe):
                prime(pe, z_turned, summed, weight_turned)

                def spread(g, q, p):
                    pe.wait_ge(node_of_made, 1 + g * (G // Q) + max(q - 1, 0))
                    nc.tensor.matmul(spread_bank[q % 2][:, :], c.ones_bf[0:1, :], place_row[:, p, q * Q * P:(q + 1) * Q * P], start=True, stop=True).then_inc(place_spread, 1)

                def score(g, q, s, p, n):
                    k = q * Q + s
                    if s == 0:
                        pe.wait_ge(node_of_made, 1 + g * (G // Q) + q + 1)
                    op = nc.tensor.matmul(s_bank[:, k * 3 * H:(k + 1) * 3 * H], node_of[:, q % 2, s * P:(s + 1) * P],
                                          dst_parts[:, bass.ds(n * 3 * H, 3 * H)], start=True, stop=True)
                    if s == Q - 1:
                        op.then_inc(scored, 1)

                def group(g, p, more, next_placed):
                    pe.wait_ge(z_made, 1 + (2 if leaky else 1) * (g + 1))
                    pe.wait_ge(rescaled, 1 + g)
                    nc.tensor.transpose(t_bank[0:HS, 0:P], z[:, :], c.ident[:, :]).then_inc(z_turned, 1)
                    pe.wait_ge(scan0_made, g + 1)
                    pe.sem_inc(passed_pe, 1)
                    nc.tensor.transpose(t_bank[0:1, P:P + HS], scan0[:, P - 1:P], c.ident[0:HS, 0:HS]).then_inc(row_f, 1)
                    pe.wait_ge(start_f_made if multi else out_f_made, g + 1)
                    pe.sem_inc(passed_pe, 1)
                    nc.tensor.matmul(t_bank[0:HS, 2 * P:2 * P + 1], start_f[:, :] if multi else start_f, c.ones[0:1, 0:1], start=True, stop=True).then_inc(col_f, 1)
                    pe.wait_ge(scan1_made, g + 1)
                    pe.sem_inc(passed_pe, 1)
                    nc.tensor.transpose(t_bank[0:1, P:P + HS], scan1[:, 0:1], c.ident[0:HS, 0:HS]).then_inc(row_b, 1)
                    if multi:
                        pe.wait_ge(start_b_made, g + 1)
                    pe.wait_ge(dropped, g + 1)
                    pe.sem_inc(passed_pe, 1)
                    nc.tensor.matmul(t_bank[0:HS, 2 * P + 2:2 * P + 3], start_b[:, :] if multi else start_b, c.ones[0:1, 0:1], start=True, stop=True)
                    nc.tensor.matmul(t_bank[:, 2 * P + 4:2 * P + 4 + H], first[:, :], drop[:, :], start=True, stop=True).then_inc(col_b, 1)
                    pe.wait_ge(ex_made, g + 1)
                    pe.sem_inc(passed_pe, 1)
                    op = nc.tensor.transpose(w_cols[:, 0:HS], ex[:, :], c.ident[0:HS, 0:HS])
                    if multi:
                        pe.wait_ge(fm_made, g + 1)
                        pe.sem_inc(passed_pe, 1)
                        op = nc.tensor.transpose(w_cols[:, HS:2 * HS], fm[:, :], c.ident[0:HS, 0:HS])
                    op.then_inc(weight_turned, 1)
                    if more:
                        pe.wait_ge(placed[1 - p], next_placed)
                        pe.sem_inc(passed_pe, 1)
                    for k in range(G):
                        if k % Q == 0:
                            pe.wait_ge(hot_made, g * (G // Q) + k // Q + 1)
                            if multi:
                                pe.wait_ge(msg_made, g * (G // Q) + k // Q + 1)
                                pe.wait_ge(msg_w_made, g * (G // Q) + k // Q + 1)
                        if k >= Q:
                            pe.wait_ge(added, 1 + g * G + k - Q + 1)
                        else:
                            pe.wait_ge(added, 1 + g * G)
                        rhs = msg[:, k // Q % 2, k % Q, :] if multi else rows[:, p, k, 0:width]
                        nc.tensor.matmul(ring[k % Q][:, 0:width], hot[:, k // Q % 2, k % Q, :], rhs, start=True, stop=True).then_inc(summed, 1)
                        if more:
                            if k % Q == 0:
                                spread(g + 1, k // Q, 1 - p)
                                if k and (k - Q) % TL == 0:
                                    node_tile = tiles_now(mybir.EngineType.PE, 1 - p, k - Q, TL)
                            if k >= Q:
                                score(g + 1, k // Q - 1, k % Q, 1 - p, node_tile[(k - Q) % TL])
                    if more:
                        for s in range(Q):
                            score(g + 1, G // Q - 1, s, 1 - p, node_tile[TL - Q + s])

                pe.wait_ge(placed[0], 64)
                pe.wait_ge(parts_made, 5)
                for q in range(G // Q):
                    spread(0, q, 0)
                    node_tile = tiles_now(mybir.EngineType.PE, 0, q * Q, Q)
                    for s in range(Q):
                        score(0, q, s, 0, node_tile[s])
                with pe.Fori(0, NG // 2 - 1) as pair:
                    group(pair * 2, 0, True, 64 * (pair + 1))
                    group(pair * 2 + 1, 1, True, 64 * (pair + 2))
                group(NG - 2, 0, True, 32 * NG)
                group(NG - 1, 1, False, None)


def spread_row(w_row, n):
    return w_row.rearrange("(one n) -> one n", one=1).broadcast_to([P, n])


def tiles_of(dram_ap, b):
    return dram_ap.rearrange("(n p) d -> p n d", p=P)[:, bass.ds(b * T, T), :]


def gat_finish(nc, c, w, acc):
    with ExitStack() as ctx:
        def sb(name, shape, dt=F32):
            return ctx.enter_context(nc.sbuf_tensor(f"gf_{name}", shape, dt))

        def sem(name):
            return nc.alloc_semaphore(f"gf_{name}")

        HW = HEADS * HC
        x = sb("x", [P, 2, T, D])
        h = sb("h", [P, 2, T, A_ROW])
        x_new = sb("x_new", [P, 2, T, D])
        wp = sb("wp", [P, D])
        bias = sb("bias", [HW, 1])
        bias_wide = sb("bias_wide", [HW, P])
        bp = sb("bp", [P, D])
        own = sb("own", [P, T, HEADS])
        top = sb("top", [P, T, HEADS])
        both = sb("both", [P, T, HEADS])
        gap = sb("gap", [P, 2, T, HEADS])
        factor = sb("factor", [P, 2, T, HEADS])
        den = sb("den", [P, T, HEADS])
        part = sb("part", [P, T, HW])
        o = sb("o", [P, T, HW])
        ot = sb("ot", [P, T, HW])
        loaded = [sem("loaded0"), sem("loaded1")]
        bias_spread, bias_projected, offset_made, x_offset = (sem(s) for s in ("bias_spread", "bias_projected", "offset_made", "x_offset"))
        stored = [sem("stored0"), sem("stored1")]
        w_loaded, dv, gap_made, factor_made, o_made, turned, ot_made, projected, added = (sem(s) for s in (
            "w_loaded", "dv", "gap_made", "factor_made", "o_made", "turned", "ot_made", "projected", "added"))
        V = 7
        passed = nc.alloc_semaphore("passed")
        with nc.Block() as block:
            @block.sync
            def _(sp):
                sp.dma_start(wp[:, :], w["L0_gnn_Wp"]).then_inc(w_loaded, 16)
                sp.dma_start(bias[:, :], w["L0_gnn_bias"].rearrange("(k one) -> k one", one=1)).then_inc(w_loaded, 16)
                sp.dma_start(bp[:, :], spread_row(w["L0_gnn_bp"], D)).then_inc(w_loaded, 16)
                for p in range(2):
                    sp.sem_inc(stored[p], 16)

                def load(b, p):
                    nc.sync.dma_start(x[:, p, :, :], tiles_of(c.x_in, b)).then_inc(loaded[p], 16)
                    nc.sync.dma_start(h[:, p, :, :], tiles_of(c.a_table, b)).then_inc(loaded[p], 16)

                def store(b, p):
                    sp.wait_ge(added, 1 + (b + 1) * T)
                    sp.sem_inc(passed, 1)
                    nc.sync.dma_start(tiles_of(c.x1, b), x_new[:, p, :, :]).then_inc(stored[p], 16)

                for p in range(2):
                    load(p, p)
                with sp.Fori(0, NB // 2 - 1) as pair:
                    for p in range(2):
                        b = pair * 2 + p
                        store(b, p)
                        load(b + 2, p)
                for p in range(2):
                    store(NB - 2 + p, p)
                for p in range(2):
                    sp.wait_ge(stored[p], 16 + 16 * (NB // 2))

            @block.gpsimd
            def _(pool):
                pool.wait_ge(offset_made, 1)
                with batches(pool) as pair:
                    for p in range(2):
                        pool.wait_ge(loaded[p], 32 * pair + 32)
                        pool.sem_inc(passed, 1)
                        nc.gpsimd.tensor_tensor(x[:, p, :, :], x[:, p, :, :], bp[:, :].rearrange("p (o d) -> p o d", o=1).broadcast_to([P, T, D]), ALU.add).then_inc(x_offset, 1)

            @block.vector
            def _(dve):
                prime(dve, added)
                v = nc.vector
                dve.wait_ge(w_loaded, 48)
                v.tensor_scalar(bias_wide[:, :], c.ones[0:HW, :], bias[:, 0:1], None, ALU.mult).then_inc(bias_spread, 1)
                dve.wait_ge(bias_projected, 1)
                v.tensor_tensor(bp[:, :], bp[:, :], c.bank[4][:, 0:D], ALU.add).then_inc(offset_made, 1)
                with batches(dve) as pair:
                    for p in range(2):
                        b = pair * 2 + p
                        sums = acc[:, bass.ds(b * T * A_ACC, T * A_ACC)].rearrange("p (t k) -> p t k", t=T)
                        score = c.dst_score[:, bass.ds(b * T * HEADS, T * HEADS)].rearrange("p (t k) -> p t k", t=T)
                        dve.wait_ge(loaded[p], 32 * pair + 32)

                        def chain(op, n):
                            op.then_inc(dv, 1)
                            dve.wait_ge(dv, b * V + n)

                        v.tensor_tensor(own[:, :, :], h[:, p, :, HW:A_ROW], score, ALU.add)
                        chain(v.tensor_scalar(top[:, :, :], sums[:, :, HW:A_ROW], 0.0, -BIG, ALU.is_equal, ALU.mult), 1)
                        v.scalar_tensor_tensor(own[:, :, :], own[:, :, :], 0.2, own[:, :, :], ALU.mult, ALU.max)
                        chain(v.tensor_tensor(top[:, :, :], top[:, :, :], sums[:, :, A_ROW:A_ACC], ALU.add), 2)
                        chain(v.tensor_tensor(both[:, :, :], top[:, :, :], own[:, :, :], ALU.max), 3)
                        v.tensor_tensor(gap[:, 0, :, :], top[:, :, :], both[:, :, :], ALU.subtract)
                        v.tensor_tensor(gap[:, 1, :, :], own[:, :, :], both[:, :, :], ALU.subtract).then_inc(gap_made, 1)
                        dve.wait_ge(factor_made, b + 1)
                        o4 = o[:, :, :].rearrange("p t (h c) -> p t h c", h=HEADS)
                        part4 = part[:, :, :].rearrange("p t (h c) -> p t h c", h=HEADS)

                        def wide(ap, i):
                            return ap[:, i, :].rearrange("p (h one) -> p h one", one=1).broadcast_to([P, HEADS, HC])

                        dve.wait_ge(turned, 1 + b * T)
                        for i in range(T):
                            v.tensor_tensor(o4[:, i, :, :], sums[:, i, 0:HW].rearrange("p (h c) -> p h c", h=HEADS), wide(factor[:, 0], i), ALU.mult)
                            v.tensor_tensor(part4[:, i, :, :], h[:, p, i, 0:HW].rearrange("p (h c) -> p h c", h=HEADS), wide(factor[:, 1], i), ALU.mult)
                        chain(v.tensor_tensor(den[:, :, :], sums[:, :, HW:A_ROW], factor[:, 0, :, :], ALU.mult), 4)
                        chain(v.tensor_tensor(den[:, :, :], den[:, :, :], factor[:, 1, :, :], ALU.add), 5)
                        v.tensor_tensor(o[:, :, :], o[:, :, :], part[:, :, :], ALU.add)
                        chain(v.tensor_scalar(den[:, :, :], den[:, :, :], 1e-16, None, ALU.add), 6)
                        chain(v.reciprocal(den[:, :, :], den[:, :, :]), 7)
                        for i in range(T):
                            v.tensor_tensor(o4[:, i, :, :], o4[:, i, :, :], wide(den, i), ALU.mult).then_inc(o_made, 1)
                        dve.wait_ge(stored[p], 16 * pair + 16)
                        dve.wait_ge(x_offset, b + 1)
                        for i in range(T):
                            dve.wait_ge(projected, 1 + b * T + i + 1)
                            op = v.tensor_tensor(x_new[:, p, i, :], c.bank[2 + i % 2][:, 0:D], x[:, p, i, :], ALU.add)
                            op.then_inc(added, 1)

            @block.scalar
            def _(act):
                prime(act, ot_made)
                with batches(act) as pair:
                    for p in range(2):
                        b = pair * 2 + p
                        act.wait_ge(gap_made, b + 1)
                        nc.scalar.activation(factor[:, :, :, :], gap[:, :, :, :], ACT.Exp).then_inc(factor_made, 1)
                        act.wait_ge(projected, 1 + b * T)
                        for i in range(T):
                            act.wait_ge(turned, 1 + b * T + i + 1)
                            nc.scalar.copy(ot[:, i, :], c.bank[i % 2][:, 0:HW]).then_inc(ot_made, 1)

            @block.tensor
            def _(pe):
                prime(pe, turned, projected)
                pe.wait_ge(w_loaded, 48)
                pe.wait_ge(bias_spread, 1)
                nc.tensor.matmul(c.bank[4][:, 0:D], bias_wide[:, :], wp[:, :], start=True, stop=True).then_inc(bias_projected, 1)
                with batches(pe) as pair:
                    for p in range(2):
                        b = pair * 2 + p
                        for i in range(T + 1):
                            if i < T:
                                pe.wait_ge(o_made, b * T + i + 1)
                                pe.wait_ge(ot_made, 1 + b * T + max(i - 1, 0))
                                nc.tensor.transpose(c.bank[i % 2][:, 0:HW], o[:, i, :], c.ident[:, :]).then_inc(turned, 1)
                            if i >= 1:
                                k = i - 1
                                pe.wait_ge(ot_made, 1 + b * T + i)
                                pe.wait_ge(added, 1 + b * T + max(k - 1, 0))
                                nc.tensor.matmul(c.bank[2 + k % 2][:, 0:D], ot[:, k, :], wp[:, :], start=True, stop=True).then_inc(projected, 1)


def slice_tokens(nc, c, w, pooled_out):
    with ExitStack() as ctx:
        def sb(name, shape, dt=F32):
            return ctx.enter_context(nc.sbuf_tensor(f"st_{name}", shape, dt))

        def sem(name):
            return nc.alloc_semaphore(f"st_{name}")

        NBK = INNER // P
        f = Front(nc, ctx, "st")
        wx = sb("wx", [P, 2, INNER])
        wx_t = sb("wx_t", [P, NBK, D])
        pair_slice = sb("pair_slice", [P, P])
        bx = sb("bx", [P, NBK])
        rows = sb("rows", [1, 4, INNER])
        temp = sb("temp", [1, FH])
        wc = sb("wc", [P, 2, INNER])
        inv_temp = sb("inv_temp", [P, INNER])
        brow = sb("brow", [P, INNER])
        lg = sb("lg", [P, 2, INNER])
        mx = sb("mx", [P, 2, FH])
        e = sb("e", [P, 2, INNER])
        total = sb("total", [P, 2, FH])
        inv = sb("inv", [P, 2, FH])
        sw = sb("sw", [P, 2, INNER])
        swt = sb("swt", [P, 2, T, INNER])
        zeros = sb("zeros", [P, P])
        zero_rows = sb("zero_rows", [P, D + 1])
        stored = [sem("stored0"), sem("stored1")]
        w_loaded, dv, pe_prep, logits, lg_made, mx_made, sub_made, e_made, total_made, inv_made, inv_masked, sw_made, pooled, sw_turned, swt_made = (sem(s) for s in (
            "w_loaded", "dv", "pe_prep", "logits", "lg_made", "mx_made", "sub_made", "e_made", "total_made", "inv_made", "inv_masked", "sw_made", "pooled", "sw_turned", "swt_made"))
        with nc.Block() as block:
            @block.sync
            def _(sp):
                sp.wait_ge(dv, 1)
                sp.dma_start(wx[:, :, :], w["L0_ffn_W_x"].rearrange("(c p) n -> p c n", p=P)).then_inc(w_loaded, 16)
                for h in range(2):
                    sp.dma_start(pair_slice[h * FG:(h + 1) * FG, h * FG:(h + 1) * FG], w["L0_ffn_W_slice"]).then_inc(w_loaded, 16)
                sp.dma_start(bx[:, :], w["L0_ffn_b_x"].rearrange("(k p) -> p k", p=P), allow_slow_non_contiguous=True).then_inc(w_loaded, 16)
                for h in range(FH):
                    sp.dma_start(rows[:, 1, h * FG:(h + 1) * FG], w["L0_ffn_b_slice"].rearrange("(one n) -> one n", one=1)).then_inc(w_loaded, 16)
                sp.dma_start(temp[:, :], w["L0_ffn_temperature"].rearrange("a h b c -> (a b c) h")).then_inc(w_loaded, 16)
                for p in range(2):
                    sp.sem_inc(stored[p], 16)

                def store(b, p):
                    sp.wait_ge(swt_made, 1 + (b + 1) * T)
                    sp.sem_inc(f.passed, 1)
                    nc.sync.dma_start(c.swt.rearrange("n p k -> p n k")[:, bass.ds(b * T, T), :], swt[:, p, :, :]).then_inc(stored[p], 16)

                f.sync(sp, nc, c.x1, store)
                for p in range(2):
                    sp.wait_ge(stored[p], 16 + 16 * (NB // 2))

            @block.tensor
            def _(pe):
                prime(pe, sw_turned, pooled)
                pe.wait_ge(w_loaded, 16 * 13)
                for k in range(NBK):
                    for ch in range(2):
                        op = nc.tensor.transpose(c.bank[k][:, ch * P:(ch + 1) * P], wx[:, ch, k * P:(k + 1) * P], c.ident[:, :])
                op.then_inc(pe_prep, 1)
                pe.wait_ge(dv, 3)
                for k in range(NBK):
                    for ch in range(2):
                        nc.tensor.matmul(c.bank[ch][:, k * P:(k + 1) * P], wx_t[:, k, ch * P:(ch + 1) * P], pair_slice[:, :], start=True, stop=True)
                    nc.tensor.matmul(c.bank[2][0:1, k * P:(k + 1) * P], bx[:, k:k + 1], pair_slice[:, :], start=True, stop=True)
                nc.tensor.matmul(c.bank[3][:, :], c.ones[0:1, :], rows[:, 0, :], start=True, stop=True).then_inc(pe_prep, 1)
                pe.wait_ge(dv, 6)
                nc.tensor.matmul(c.bank[3][:, :], c.ones[0:1, :], rows[:, 3, :], start=True, stop=True).then_inc(pe_prep, 1)
                for k in range(NBK):
                    nc.tensor.matmul(c.bank[4 + k][:, 0:D + 1], zeros[:, :], zero_rows[:, :], start=True, stop=False, skip_group_check=True)
                pe.wait_ge(dv, 7)
                with batches(pe) as pair:
                    for p in range(2):
                        b = pair * 2 + p
                        for i in range(T + 3):
                            if i < T:
                                f.tensor(pe, nc, c, b, p, i)
                            if 1 <= i <= T:
                                k = i - 1
                                pe.wait_ge(f.xt_made, 1 + b * T + i)
                                pe.wait_ge(lg_made, 1 + b * T + k)
                                for ch in range(2):
                                    op = nc.tensor.matmul(c.bank[2][:, :], f.xt[:, k, ch, :], wc[:, ch, :], start=(ch == 0), stop=(ch == 1))
                                op.then_inc(logits, 1)
                            if i >= 3:
                                k = i - 3
                                pe.wait_ge(sw_made, 1 + b * T + k + 1)
                                for q in range(NBK):
                                    op = nc.tensor.matmul(c.bank[4 + q][:, 0:D + 1], sw[:, k % 2, q * P:(q + 1) * P], f.xn[:, 0, k, :], start=False, stop=True, skip_group_check=True)
                                op.then_inc(pooled, 1)
                                pe.wait_ge(swt_made, 1 + b * T + k)
                                for q in range(NBK):
                                    op = nc.tensor.transpose(c.bank[3][:, q * P:(q + 1) * P], sw[:, k % 2, q * P:(q + 1) * P], c.ident[:, :])
                                op.then_inc(sw_turned, 1)

            @block.vector
            def _(dve):
                prime(dve, lg_made, sw_made)
                v = nc.vector
                v.memset(zeros[:, :], 0.0)
                v.memset(zero_rows[:, :], 0.0)
                v.memset(f.xn[:, 0, :, D:D + 1], 1.0)
                v.memset(pair_slice[:, :], 0.0).then_inc(dv, 1)
                dve.wait_ge(w_loaded, 16 * 13)
                v.tensor_scalar(temp[:, :], temp[:, :], 0.1, 5.0, ALU.max, ALU.min).then_inc(dv, 1)
                dve.wait_ge(dv, 2)
                v.reciprocal(temp[:, :], temp[:, :]).then_inc(mx_made, 1)
                dve.wait_ge(mx_made, 1)
                v.tensor_copy(rows[:, 0, :].rearrange("o (h g) -> o h g", h=FH), temp[:, :].rearrange("o (h g) -> o h g", g=1).broadcast_to([1, FH, FG]))
                dve.wait_ge(pe_prep, 1)
                for k in range(NBK):
                    op = v.tensor_copy(wx_t[:, k, :], c.bank[k][:, 0:D])
                op.then_inc(dv, 1)
                dve.wait_ge(pe_prep, 2)
                v.tensor_copy(inv_temp[:, :], c.bank[3][:, :])
                v.tensor_tensor(rows[:, 2, :], c.bank[2][0:1, :], rows[:, 1, :], ALU.add).then_inc(dv, 1)
                dve.wait_ge(dv, 4)
                for ch in range(2):
                    v.tensor_tensor(wc[:, ch, :], c.bank[ch][:, :], inv_temp[:, :], ALU.mult)
                v.tensor_tensor(rows[:, 3, :], rows[:, 2, :], rows[:, 0, :], ALU.mult).then_inc(dv, 1)
                dve.wait_ge(dv, 5)
                dve.sem_inc(dv, 1)
                dve.wait_ge(pe_prep, 3)
                v.tensor_copy(brow[:, :], c.bank[3][:, :]).then_inc(dv, 1)
                dve.wait_ge(dv, 7)
                with batches(dve) as pair:
                    for p in range(2):
                        b = pair * 2 + p
                        f.vector(dve, nc, b, pair, p)
                        for i in range(T + 1):
                            new, old = i < T, i >= 1
                            if new:
                                s, n = i % 2, b * T + i
                                heads = lg[:, s, :].rearrange("p (h g) -> p h g", h=FH)
                                dve.wait_ge(e_made, 1 + b * T + max(i - 1, 0))
                                dve.wait_ge(logits, n + 1)
                                v.tensor_tensor(lg[:, s, :], c.bank[2][:, :], brow[:, :], ALU.add).then_inc(lg_made, 1)
                            if old:
                                so, no = (i - 1) % 2, b * T + i - 1
                                e_heads = e[:, so, :].rearrange("p (h g) -> p h g", h=FH)
                                dve.wait_ge(e_made, 1 + no + 1)
                                v.tensor_reduce(total[:, so, :], e_heads, AX.X, ALU.add).then_inc(total_made, 1)
                            if new:
                                dve.wait_ge(lg_made, 1 + n + 1)
                                v.tensor_reduce(mx[:, s, :], heads, AX.X, ALU.max).then_inc(mx_made, 1)
                            if old:
                                dve.wait_ge(total_made, no + 1)
                                v.reciprocal(inv[:, so, :], total[:, so, :]).then_inc(inv_made, 1)
                            if new:
                                dve.wait_ge(mx_made, n + 2)
                                v.tensor_tensor(heads, heads, mx[:, s, :].rearrange("p (h g) -> p h g", g=1).broadcast_to([P, FH, FG]), ALU.subtract).then_inc(sub_made, 1)
                            if old:
                                dve.wait_ge(inv_made, no + 1)
                                v.tensor_scalar(inv[:, so, :], inv[:, so, :], c.valid[:, bass.ds(no, 1)], None, ALU.mult).then_inc(inv_masked, 1)
                                dve.wait_ge(inv_masked, no + 1)
                                dve.wait_ge(sw_turned, 1 + b * T + max(i - 2, 0))
                                v.tensor_tensor(sw[:, so, :].rearrange("p (h g) -> p h g", h=FH), e_heads,
                                                inv[:, so, :].rearrange("p (h g) -> p h g", g=1).broadcast_to([P, FH, FG]), ALU.mult).then_inc(sw_made, 1)

            @block.scalar
            def _(act):
                prime(act, swt_made, e_made, f.xt_made)
                with batches(act) as pair:
                    for p in range(2):
                        b = pair * 2 + p

                        def also(i):
                            if 2 <= i < T + 2:
                                k = i - 2
                                act.wait_ge(sub_made, b * T + k + 1)
                                act.wait_ge(sw_made, 1 + b * T + max(k - 1, 0))
                                nc.scalar.activation(e[:, k % 2, :], lg[:, k % 2, :], ACT.Exp).then_inc(e_made, 1)
                            if i == 0:
                                act.wait_ge(stored[p], 16 * pair + 16)
                            if i >= 4:
                                k = i - 4
                                act.wait_ge(sw_turned, 1 + b * T + k + 1)
                                nc.scalar.copy(swt[:, p, k, :], c.bank[3][:, :]).then_inc(swt_made, 1)

                        f.scalar(act, nc, c, b, p, pooled, also, 3)

        copied = sem("pooled_copied")
        with nc.Block() as block:
            @block.vector
            def _(dve):
                for k in range(NBK):
                    op = nc.vector.tensor_copy(pooled_out[:, k, :], c.bank[4 + k][:, 0:D + 1])
                op.then_inc(copied, 1)
                dve.wait_ge(copied, 1)


def token_attention(nc, c, w, pooled_in, w_comb):
    with ExitStack() as ctx:
        def sb(name, shape, dt=F32):
            return ctx.enter_context(nc.sbuf_tensor(f"ta_{name}", shape, dt))

        def sem(name):
            return nc.alloc_semaphore(f"ta_{name}")

        NBK = INNER // P
        wfx = sb("wfx", [P, 2, INNER])
        wout = sb("wout", [P, NBK, D])
        bfx = sb("bfx", [P, INNER])
        qkv = sb("qkv", [P, 3, P])
        mask = sb("mask", [P, P])
        hide = sb("hide", [P, P])
        half_row = sb("half_row", [P, P])
        half_col = sb("half_col", [P, 1])
        pt = sb("pt", [P, 2, P])
        tok = sb("tok", [P, P])
        tok_t = sb("tok_t", [P, P])
        qkv_out = sb("qkv_out", [P, 3, P])
        s = sb("s", [P, P])
        mx = sb("mx", [P, 1])
        e = sb("e", [P, P])
        total = sb("total", [P, 1])
        e_t = sb("e_t", [P, P])
        out_t = sb("out_t", [P, P])
        den = sb("den", [P, 1])
        w_loaded, dv, pv, av = sem("w_loaded"), sem("vector_step"), sem("tensor_step"), sem("block_projected")
        exp_made, inv_made, comb_made = sem("exp_made"), sem("inv_made"), sem("comb_made")
        V, PV = 15, 7
        scale = float(FG) ** -0.5
        with nc.Block() as block:
            @block.sync
            def _(sp):
                sp.dma_start(wfx[:, :, :], w["L0_ffn_W_fx"].rearrange("(c p) n -> p c n", p=P)).then_inc(w_loaded, 16)
                sp.dma_start(wout[:, :, :], w["L0_ffn_W_out"].rearrange("(k p) n -> p k n", p=P)).then_inc(w_loaded, 16)
                sp.dma_start(bfx[:, :], spread_row(w["L0_ffn_b_fx"], INNER)).then_inc(w_loaded, 16)
                sp.wait_ge(dv, 1)
                for n, name in enumerate(("L0_ffn_W_q", "L0_ffn_W_k", "L0_ffn_W_v")):
                    for h in range(2):
                        sp.dma_start(qkv[h * FG:(h + 1) * FG, n, h * FG:(h + 1) * FG], w[name]).then_inc(w_loaded, 16)

            @block.tensor
            def _(pe):
                pe.wait_ge(w_loaded, 16 * 9)
                t = nc.tensor
                for k in range(NBK):
                    d0 = 4 + V * k
                    pe.wait_ge(dv, d0)
                    for ch in range(2):
                        op = t.transpose(c.bank[0][:, ch * P:(ch + 1) * P], pooled_in[:, k, ch * P:(ch + 1) * P], c.ident[:, :])
                    op.then_inc(pv, 1)
                    pe.wait_ge(dv, d0 + 1)
                    for ch in range(2):
                        op = t.matmul(c.bank[1][:, 0:P], pt[:, ch, :], wfx[:, ch, k * P:(k + 1) * P], start=(ch == 0), stop=(ch == 1))
                    op.then_inc(pv, 1)
                    pe.wait_ge(dv, d0 + 6)
                    t.transpose(c.bank[2][:, 0:P], tok[:, :], c.ident[:, :]).then_inc(pv, 1)
                    pe.wait_ge(dv, d0 + 7)
                    t.matmul(c.bank[3][:, 0:P], qkv[:, 0, :], tok_t[:, :], start=True, stop=True)
                    t.matmul(c.bank[3][:, P:2 * P], qkv[:, 1, :], tok_t[:, :], start=True, stop=True)
                    t.matmul(c.bank[3][:, 2 * P:3 * P], tok_t[:, :], qkv[:, 2, :], start=True, stop=True).then_inc(pv, 1)
                    pe.wait_ge(dv, d0 + 8)
                    t.matmul(c.bank[4][:, 0:P], qkv_out[:, 0, :], qkv_out[:, 1, :], start=True, stop=True).then_inc(pv, 1)
                    pe.wait_ge(dv, d0 + 13)
                    t.transpose(c.bank[5][:, 0:P], e[:, :], c.ident[:, :]).then_inc(pv, 1)
                    pe.wait_ge(dv, d0 + 14)
                    t.matmul(c.bank[6][:, 0:P], qkv_out[:, 2, :], e_t[:, :], start=True, stop=True).then_inc(pv, 1)
                    pe.wait_ge(dv, d0 + 15)
                    t.matmul(c.bank[7][:, 0:D], out_t[:, :], wout[:, k, :], start=True, stop=True).then_inc(av, 1)

            @block.scalar
            def _(act):
                for k in range(NBK):
                    d0 = 4 + V * k
                    act.wait_ge(dv, d0 + 11)
                    nc.scalar.activation(e[:, :], s[:, :], ACT.Exp, scale=scale).then_inc(exp_made, 1)
                    act.wait_ge(av, k + 1)
                    nc.scalar.copy(w_comb[:, k, :], c.bank[7][:, 0:D]).then_inc(comb_made, 1)

            @block.vector
            def _(dve):
                v = nc.vector
                n = [0]

                def chain(op):
                    op.then_inc(dv, 1)
                    n[0] += 1
                    dve.wait_ge(dv, n[0])

                chain(v.memset(qkv[:, :, :], 0.0))
                v.tensor_scalar(half_col[:, :], c.ramp_col[:, :], float(FG), None, ALU.is_ge)
                chain(v.tensor_scalar(half_row[:, :], c.ramp_row[:, :], float(FG), None, ALU.is_ge))
                chain(v.tensor_scalar(mask[:, :], half_row[:, :], half_col[:, 0:1], None, ALU.is_equal))
                chain(v.tensor_scalar(hide[:, :], mask[:, :], 1.0, BIG, ALU.subtract, ALU.mult))
                dve.wait_ge(w_loaded, 16 * 9)
                for k in range(NBK):
                    norm = pooled_in[:, k, D:D + 1]
                    dve.wait_ge(pv, PV * k + 1)
                    if k:
                        dve.wait_ge(comb_made, k)
                    chain(v.tensor_copy(pt[:, :, :].rearrange("p c n -> p (c n)"), c.bank[0][:, 0:D]))
                    chain(v.tensor_scalar(den[:, :], norm, 1e-5, None, ALU.add))
                    chain(v.reciprocal(den[:, :], den[:, :]))
                    dve.wait_ge(pv, PV * k + 2)
                    chain(v.scalar_tensor_tensor(tok[:, :], bfx[:, k * P:(k + 1) * P], norm, c.bank[1][:, 0:P], ALU.mult, ALU.add))
                    chain(v.tensor_scalar(tok[:, :], tok[:, :], den[:, 0:1], None, ALU.mult))
                    chain(v.tensor_tensor(tok[:, :], tok[:, :], mask[:, :], ALU.mult))
                    dve.wait_ge(pv, PV * k + 3)
                    chain(v.tensor_copy(tok_t[:, :], c.bank[2][:, 0:P]))
                    dve.wait_ge(pv, PV * k + 4)
                    chain(v.tensor_copy(qkv_out[:, :, :].rearrange("p c n -> p (c n)"), c.bank[3][:, 0:3 * P]))
                    dve.wait_ge(pv, PV * k + 5)
                    chain(v.tensor_tensor(s[:, :], c.bank[4][:, 0:P], hide[:, :], ALU.add))
                    chain(v.tensor_reduce(mx[:, :], s[:, :], AX.X, ALU.max))
                    chain(v.tensor_scalar(s[:, :], s[:, :], mx[:, 0:1], None, ALU.subtract))
                    dve.wait_ge(exp_made, k + 1)
                    chain(v.tensor_reduce(total[:, :], e[:, :], AX.X, ALU.add))
                    dve.wait_ge(dv, n[0])
                    v.reciprocal(total[:, :], total[:, :]).then_inc(inv_made, 1)
                    dve.wait_ge(inv_made, k + 1)
                    chain(v.tensor_scalar(e[:, :], e[:, :], total[:, 0:1], None, ALU.mult))
                    dve.wait_ge(pv, PV * k + 6)
                    chain(v.tensor_copy(e_t[:, :], c.bank[5][:, 0:P]))
                    dve.wait_ge(pv, PV * k + 7)
                    chain(v.tensor_copy(out_t[:, :], c.bank[6][:, 0:P]))
                dve.wait_ge(comb_made, NBK)


def hyp_project(nc, c, w, w_comb):
    with ExitStack() as ctx:
        def sb(name, shape, dt=F32):
            return ctx.enter_context(nc.sbuf_tensor(f"hp_{name}", shape, dt))

        def sem(name):
            return nc.alloc_semaphore(f"hp_{name}")

        NBK = INNER // P
        f = Front(nc, ctx, "hp")
        swt = sb("swt", [P, 2, T, INNER])
        b_out = sb("b_out", [P, D])
        wg = sb("wg", [P, 2, D])
        w_ext = sb("w_ext", [P, 2, D + 1])
        b_row = sb("b_row", [P, D])
        att = sb("att", [P, 2, D])
        mag_b = sb("mag_b", [P, 1])
        raw = sb("raw", [P, T, D])
        z = sb("z", [P, T])
        junk = sb("junk", [P, 2, 2, D])
        square = sb("square", [P, T])
        norm = sb("norm", [P, T])
        ez = sb("ez", [P, T])
        factor = sb("factor", [P, T])
        rows = sb("rows", [P, 2, T, B_ROW])
        dots = sb("dots", [P, 2, T])
        act_junk = sb("act_junk", [P, D])
        swt_loaded = [sem("swt_loaded0"), sem("swt_loaded1")]
        x_stored = [sem("x_stored0"), sem("x_stored1")]
        rows_stored = [sem("rows_stored0"), sem("rows_stored1")]
        (w_loaded, mixed, x_mixed, w_turned, w_ready, projected, raw_made, squared, norm_made, ez_made, dv, scored, bias_added) = (sem(s) for s in (
            "w_loaded", "mixed", "x_mixed", "w_turned", "w_ready", "projected", "raw_made", "squared", "norm_made", "ez_made", "dv", "scored", "bias_added"))
        dotted, x_biased, passed_sp = sem("dotted"), sem("x_biased"), sem("passed_sp")
        V = 5
        with nc.Block() as block:
            @block.sync
            def _(sp):
                sp.dma_start(b_out[:, :], spread_row(w["L0_ffn_b_out"], D)).then_inc(w_loaded, 16)
                sp.dma_start(b_row[:, :], spread_row(w["L1_gnn_b"], D)).then_inc(w_loaded, 16)
                sp.dma_start(att[:, :, :].rearrange("p a d -> p (a d)"), spread_row(w["L1_gnn_attn_w"].rearrange("o d -> (o d)"), 2 * D)).then_inc(w_loaded, 16)
                sp.dma_start(mag_b[:, :], spread_row(w["L1_gnn_mag_b"], 1)).then_inc(w_loaded, 16)
                sp.dma_start(wg[:, :, :], w["L1_gnn_W"].rearrange("(c p) n -> p c n", p=P)).then_inc(w_loaded, 16)
                sp.dma_start(w_ext[:, :, D:], w["L1_gnn_mag_w"].rearrange("one (c p) -> p c one", p=P), allow_slow_non_contiguous=True).then_inc(w_loaded, 16)
                for p in range(2):
                    sp.sem_inc(rows_stored[p], 16)

                def load(b, p):
                    f.load(sp, nc, c.x1, b, p)
                    nc.sync.dma_start(swt[:, p, :, :], c.swt.rearrange("n p k -> p n k")[:, bass.ds(b * T, T), :]).then_inc(swt_loaded[p], 16)

                def store(b, pair, p):
                    sp.wait_ge(x_mixed, 1 + (b + 1) * T)
                    sp.sem_inc(passed_sp, 1)
                    nc.sync.dma_start(tiles_of(c.x2, b), f.x[:, p, :, :]).then_inc(x_stored[p], 16)
                    sp.wait_ge(scored, b + 1)
                    sp.sem_inc(passed_sp, 1)
                    nc.sync.dma_start(tiles_of(c.b_table, b), rows[:, p, :, :]).then_inc(rows_stored[p], 16)

                for p in range(2):
                    load(p, p)
                with sp.Fori(0, NB // 2 - 1) as pair:
                    for p in range(2):
                        b = pair * 2 + p
                        store(b, pair, p)
                        sp.wait_ge(x_stored[p], 16 * pair + 16)
                        sp.sem_inc(passed_sp, 1)
                        sp.wait_ge(projected, 1 + (b + 1) * T)
                        sp.sem_inc(passed_sp, 1)
                        load(b + 2, p)
                for p in range(2):
                    store(NB - 2 + p, None, p)
                for p in range(2):
                    sp.wait_ge(x_stored[p], 16 * (NB // 2))
                    sp.wait_ge(rows_stored[p], 16 + 16 * (NB // 2))

            @block.gpsimd
            def _(pool):
                pool.wait_ge(w_loaded, 96)
                with batches(pool) as pair:
                    for p in range(2):
                        pool.wait_ge(f.loaded[p], 16 * pair + 16)
                        pool.sem_inc(passed_sp, 1)
                        op = nc.gpsimd.tensor_tensor(f.x[:, p, :, :], f.x[:, p, :, :], b_out[:, :].rearrange("p (o d) -> p o d", o=1).broadcast_to([P, T, D]), ALU.add)
                        op.then_inc(x_biased, 1)

            @block.vector
            def _(dve):
                prime(dve, x_mixed, raw_made, dotted)
                v = nc.vector
                v.memset(dots[:, :, :], 0.0)
                v.memset(rows[:, :, :, :], 1.0)
                dve.wait_ge(w_loaded, 96)
                dve.wait_ge(w_turned, 1)
                op = v.tensor_copy(w_ext[:, :, 0:D], c.bank[4][:, :].rearrange("p (c n) -> p c n", c=2))
                op.then_inc(w_ready, 1)
                with batches(dve) as pair:
                    for p in range(2):
                        b = pair * 2 + p

                        def update():
                            dve.wait_ge(x_biased, b + 1)
                            for i in range(T):
                                dve.wait_ge(mixed, b * T + i + 1)
                                v.tensor_tensor(f.x[:, p, i, :], f.x[:, p, i, :], c.bank[4 + i % 4][:, 0:D], ALU.add).then_inc(x_mixed, 1)
                            dve.wait_ge(x_mixed, 1 + (b + 1) * T)

                        f.vector(dve, nc, b, pair, p, update)

                        def chain(op, n):
                            op.then_inc(dv, 1)
                            dve.wait_ge(dv, b * V + n)

                        def dot(i):
                            dve.wait_ge(raw_made, 1 + b * T + i + 1)
                            dve.wait_ge(dotted, 1 + b * T + max(i - 1, 0))
                            for a in range(2):
                                op = v.tensor_tensor_reduce(junk[:, i % 2, a, :], raw[:, i, :], att[:, a, :], 1.0, 0.0, ALU.mult, ALU.add, dots[:, a, i:i + 1])
                            op.then_inc(dotted, 1)

                        for i in range(T):
                            dve.wait_ge(projected, 1 + b * T + i + 1)
                            v.tensor_tensor(raw[:, i, :], c.bank[2 + i % 2][:, 0:D], b_row[:, :], ALU.add)
                            v.tensor_copy(z[:, i:i + 1], c.bank[2 + i % 2][:, D:D + 1]).then_inc(raw_made, 1)
                            if i:
                                dot(i - 1)
                        dot(T - 1)
                        v.tensor_scalar(z[:, :], z[:, :], mag_b[:, 0:1], None, ALU.add).then_inc(bias_added, 1)
                        dve.wait_ge(norm_made, b + 1)
                        chain(v.tensor_scalar(norm[:, :], norm[:, :], 1e-12, None, ALU.max), 1)
                        dve.wait_ge(ez_made, b + 1)
                        chain(v.tensor_scalar(ez[:, :], ez[:, :], 1.0, None, ALU.add), 2)
                        chain(v.reciprocal(factor[:, :], ez[:, :]), 3)
                        chain(v.reciprocal(norm[:, :], norm[:, :]), 4)
                        chain(v.scalar_tensor_tensor(factor[:, :], factor[:, :], 1.5, norm[:, :], ALU.mult, ALU.mult), 5)
                        dve.wait_ge(rows_stored[p], 16 * pair + 16)
                        for i in range(T):
                            v.tensor_scalar(rows[:, p, i, 0:D], raw[:, i, :], factor[:, i:i + 1], None, ALU.mult)
                        dve.wait_ge(dotted, 1 + (b + 1) * T)
                        v.tensor_tensor(rows[:, p, :, D + 1], dots[:, 0, :], factor[:, :], ALU.mult)
                        v.tensor_tensor(c.dst_score[:, bass.ds(b * T, T)], dots[:, 1, :], factor[:, :], ALU.mult).then_inc(scored, 1)
                        dve.wait_ge(scored, b + 1)

            @block.scalar
            def _(act):
                prime(act, f.xt_made)
                with batches(act) as pair:
                    for p in range(2):
                        b = pair * 2 + p
                        f.scalar(act, nc, c, b, p, projected)
                        for i in range(T):
                            act.wait_ge(raw_made, 1 + b * T + i + 1)
                            nc.scalar.activation(act_junk[:, :], raw[:, i, :], ACT.Square, accum_out=square[:, i:i + 1]).then_inc(squared, 1)
                            act.wait_ge(squared, b * T + i + 1)
                        act.wait_ge(bias_added, b + 1)
                        nc.scalar.activation(ez[:, :], z[:, :], ACT.Exp, scale=-1.0).then_inc(ez_made, 1)
                        nc.scalar.activation(norm[:, :], square[:, :], ACT.Sqrt).then_inc(norm_made, 1)

            @block.tensor
            def _(pe):
                prime(pe, projected)
                pe.wait_ge(w_loaded, 96)
                for a in range(2):
                    for ch in range(2):
                        op = nc.tensor.transpose(c.bank[4][:, ch * D + a * P:ch * D + (a + 1) * P], wg[:, a, ch * P:(ch + 1) * P], c.ident[:, :])
                op.then_inc(w_turned, 1)
                pe.wait_ge(w_ready, 1)

                def mix(b, pair, p):
                    pe.wait_ge(swt_loaded[p], 16 * pair + 16)
                    for i in range(T):
                        pe.wait_ge(x_mixed, 1 + b * T + max(i - 3, 0))
                        for q in range(NBK):
                            op = nc.tensor.matmul(c.bank[4 + i % 4][:, 0:D], swt[:, p, i, q * P:(q + 1) * P], w_comb[:, q, :], start=(q == 0), stop=(q == NBK - 1))
                        op.then_inc(mixed, 1)

                def project(b, p):
                    for i in range(T + 1):
                        if i < T:
                            f.tensor(pe, nc, c, b, p, i)
                        if i >= 1:
                            k = i - 1
                            pe.wait_ge(f.xt_made, 1 + b * T + i)
                            pe.wait_ge(raw_made, 1 + b * T + max(k - 1, 0))
                            for ch in range(2):
                                op = nc.tensor.matmul(c.bank[2 + k % 2][:, 0:D + 1], f.xt[:, k, ch, :], w_ext[:, ch, :], start=(ch == 0), stop=(ch == 1))
                            op.then_inc(projected, 1)

                mix(0, 0, 0)
                with pe.Fori(0, NB // 2 - 1) as pair:
                    for p in range(2):
                        project(pair * 2 + p, p)
                        mix(pair * 2 + p + 1, pair + p, 1 - p)
                project(NB - 2, 0)
                mix(NB - 1, NB // 2 - 1, 1)
                project(NB - 1, 1)


def hyp_finish(nc, c, w, acc):
    MAX_NORM = 0.95
    with ExitStack() as ctx:
        def sb(name, shape, dt=F32):
            return ctx.enter_context(nc.sbuf_tensor(f"hf_{name}", shape, dt))

        def sem(name):
            return nc.alloc_semaphore(f"hf_{name}")

        x = sb("x", [P, 2, T, D])
        h = sb("h", [P, 2, T, B_ROW])
        den = sb("den", [P, T])
        hc = sb("hc", [P, T, D])
        act_junk = sb("act_junk", [P, D])
        square = sb("square", [P, T])
        norm = sb("norm", [P, T])
        clamped = sb("clamped", [P, T])
        th = sb("th", [P, T])
        ball = sb("ball", [P, T])
        over = sb("over", [P, T])
        loaded = [sem("loaded0"), sem("loaded1")]
        stored = [sem("stored0"), sem("stored1")]
        dv, row_made, squared, norm_made, clamped_made, th_made, x_made, passed = (sem(s) for s in (
            "dv", "row_made", "squared", "norm_made", "clamped_made", "th_made", "x_made", "passed"))
        V = 11
        with nc.Block() as block:
            @block.sync
            def _(sp):
                def load(b, p):
                    nc.sync.dma_start(x[:, p, :, :], tiles_of(c.x2, b)).then_inc(loaded[p], 16)
                    nc.sync.dma_start(h[:, p, :, :], tiles_of(c.b_table, b)).then_inc(loaded[p], 16)

                def store(b, p):
                    sp.wait_ge(x_made, 1 + (b + 1) * T)
                    sp.sem_inc(passed, 1)
                    nc.sync.dma_start(tiles_of(c.x3, b), x[:, p, :, :]).then_inc(stored[p], 16)

                for p in range(2):
                    load(p, p)
                with sp.Fori(0, NB // 2 - 1) as pair:
                    for p in range(2):
                        store(pair * 2 + p, p)
                        sp.wait_ge(stored[p], 16 * pair + 16)
                        sp.sem_inc(passed, 1)
                        load(pair * 2 + p + 2, p)
                for p in range(2):
                    store(NB - 2 + p, p)
                for p in range(2):
                    sp.wait_ge(stored[p], 16 * (NB // 2))

            @block.vector
            def _(dve):
                prime(dve, x_made)
                v = nc.vector
                with batches(dve) as pair:
                    for p in range(2):
                        b = pair * 2 + p

                        def chain(op, n):
                            op.then_inc(dv, 1)
                            dve.wait_ge(dv, b * V + n)

                        sums = acc[:, bass.ds(b * T * B_ACC, T * B_ACC)].rearrange("p (t k) -> p t k", t=T)
                        dve.wait_ge(loaded[p], 32 * pair + 32)
                        chain(v.tensor_scalar(den[:, :], sums[:, :, D], 1e-10, None, ALU.add), 1)
                        chain(v.reciprocal(den[:, :], den[:, :]), 2)
                        for i in range(T):
                            v.scalar_tensor_tensor(hc[:, i, :], sums[:, i, 0:D], den[:, i:i + 1], h[:, p, i, 0:D], ALU.mult, ALU.add).then_inc(row_made, 1)
                        dve.wait_ge(norm_made, b + 1)
                        v.tensor_scalar(clamped[:, :], norm[:, :], 1e-15, None, ALU.max).then_inc(clamped_made, 1)
                        dve.wait_ge(clamped_made, b + 1)
                        chain(v.reciprocal(ball[:, :], clamped[:, :]), 3)
                        dve.wait_ge(th_made, b + 1)
                        chain(v.tensor_tensor(ball[:, :], ball[:, :], th[:, :], ALU.mult), 4)
                        chain(v.tensor_tensor(norm[:, :], norm[:, :], ball[:, :], ALU.mult), 5)
                        chain(v.tensor_scalar(over[:, :], norm[:, :], MAX_NORM, None, ALU.is_gt), 6)
                        chain(v.tensor_scalar(norm[:, :], norm[:, :], 1e-8, None, ALU.add), 7)
                        chain(v.reciprocal(norm[:, :], norm[:, :]), 8)
                        chain(v.tensor_scalar(norm[:, :], norm[:, :], MAX_NORM, 1.0, ALU.mult, ALU.subtract), 9)
                        chain(v.tensor_tensor(norm[:, :], norm[:, :], over[:, :], ALU.mult), 10)
                        chain(v.scalar_tensor_tensor(ball[:, :], norm[:, :], 1.0, ball[:, :], ALU.add, ALU.mult), 11)
                        for i in range(T):
                            v.scalar_tensor_tensor(x[:, p, i, :], hc[:, i, :], ball[:, i:i + 1], x[:, p, i, :], ALU.mult, ALU.add).then_inc(x_made, 1)

            @block.scalar
            def _(act):
                with batches(act) as pair:
                    for p in range(2):
                        b = pair * 2 + p
                        for i in range(T):
                            act.wait_ge(row_made, b * T + i + 1)
                            nc.scalar.activation(act_junk[:, :], hc[:, i, :], ACT.Square, accum_out=square[:, i:i + 1]).then_inc(squared, 1)
                            act.wait_ge(squared, b * T + i + 1)
                        act.wait_ge(x_made, 1 + b * T)
                        nc.scalar.activation(norm[:, :], square[:, :], ACT.Sqrt).then_inc(norm_made, 1)
                        act.wait_ge(clamped_made, b + 1)
                        nc.scalar.activation(th[:, :], clamped[:, :], ACT.Tanh).then_inc(th_made, 1)


def route(nc, c, w, up_w, w2):
    with ExitStack() as ctx:
        def sb(name, shape, dt=F32):
            return ctx.enter_context(nc.sbuf_tensor(f"ro_{name}", shape, dt))

        def sem(name):
            return nc.alloc_semaphore(f"ro_{name}")

        f = Front(nc, ctx, "ro", deep=2)
        wgate = sb("wgate", [P, 2, NX])
        bgate = sb("bgate", [P, 2, NX])
        before = sb("before", [P, P])
        lg = sb("lg", [P, T, NX])
        best = sb("best", [P, T, 8])
        best_at = sb("best_at", [P, T, 8], mybir.dt.uint32)
        best_f = sb("best_f", [P, T, 8])
        gap = sb("gap", [P, T])
        share = sb("share", [P, 2, T])
        chosen = sb("chosen", [P, 2, T, NX])
        mask = sb("mask", [P, T, NX])
        base = sb("base", [P, T + 1, NX])
        rank = sb("rank", [P, T, NX])
        placed = sb("placed", [P, 2, T, NX])
        place_f = sb("place_f", [P, 2, T])
        place = sb("place", [P, 2, 2 * T], I32)
        w_loaded, set_up, gated, dv, gap_made, e2_made, mask_made, counted, place_made, scattered0, scattered1, rows_gone, passed_v, experts_loaded = (sem(s) for s in (
            "w_loaded", "set_up", "gated", "dv", "gap_made", "e2_made", "mask_made", "counted", "place_made", "scattered0", "scattered1", "rows_gone", "passed_v", "experts_loaded"))
        scattered = [scattered0, scattered1]
        V = 12 + T
        with nc.Block() as block:
            @block.sync
            def _(sp):
                for ch in range(2):
                    sp.dma_start(wgate[:, ch, :], w["L1_ffn_Wg"].rearrange("(c p) n -> c p n", p=P)[ch]).then_inc(w_loaded, 16)
                sp.dma_start(bgate[:, 0, :], spread_row(w["L1_ffn_bg"], NX)).then_inc(w_loaded, 16)
                sp.dma_start(bgate[:, 1, :], spread_row(w["L1_ffn_bias"], NX)).then_inc(w_loaded, 16)

                def store(b, p):
                    pass

                f.sync(sp, nc, c.x3, store)

            @block.gpsimd
            def _(pool):
                pool.sem_inc(rows_gone, 2)

                def gone(p, rounds):
                    pool.wait_ge(scattered[p], 16 * 2 * T * rounds)
                    pool.sem_inc(rows_gone, 1)

                def scatter(pair, p):
                    for k in range(2):
                        for i in range(T):
                            nc.gpsimd.indirect_dma_start(c.routed, bass.IndirectOffsetOnAxis(ap=place[:, p, k * T + i:k * T + i + 1], axis=0),
                                                         f.xn[:, p, i, 0:D], None).then_inc(scattered[p], 16)

                pool.wait_ge(place_made, 1)
                scatter(0, 0)
                pool.wait_ge(place_made, 2)
                gone(0, 1)
                scatter(0, 1)
                with pool.Fori(1, NB // 2) as pair:
                    for p in range(2):
                        pool.wait_ge(place_made, pair * 2 + p + 1)
                        gone(1 - p, pair + p)
                        scatter(pair, p)
                gone(1, NB // 2)

            @block.vector
            def _(dve):
                v = nc.vector
                v.tensor_scalar(before[:, :], c.ramp_row[:, :], c.ramp_col[:, 0:1], None, ALU.is_gt)
                v.tensor_scalar(base[:, 0, :], c.ramp_row[:, 0:NX], float(REG), None, ALU.mult)
                dve.wait_ge(w_loaded, 64)
                v.tensor_tensor(bgate[:, 0, :], bgate[:, 0, :], bgate[:, 1, :], ALU.add).then_inc(set_up, 1)
                dve.wait_ge(set_up, 1)

                def work(b, pair, p, more):
                    f.scales(dve, nc, b, p)
                    if more:
                        f.moments(dve, nc, b + 1, pair + p, 1 - p)

                    def chain(op, n):
                        op.then_inc(dv, 1)
                        dve.wait_ge(dv, b * V + n)
                        dve.sem_inc(passed_v, 1)

                    dve.wait_ge(gated, 1 + (b + 1) * T)
                    chain(v.tensor_tensor(lg[:, :, :], c.bank[2][:, 0:T * NX].rearrange("p (t e) -> p t e", e=NX),
                                          bgate[:, 0:1, :].broadcast_to([P, T, NX]), ALU.add), 1)
                    for i in range(T):
                        op = v.max(best[:, i, :], lg[:, i, :])
                    chain(op, 2)
                    v.tensor_tensor(gap[:, :], best[:, :, 1], best[:, :, 0], ALU.subtract).then_inc(gap_made, 1)
                    for i in range(T):
                        op = v.max_index(best_at[:, i, :], best[:, i, :], lg[:, i, :])
                    chain(op, 3)
                    chain(v.tensor_copy(best_f[:, :, :], best_at[:, :, :]), 4)
                    ramp = c.ramp_row[:, 0:NX].rearrange("p (o e) -> p o e", o=1).broadcast_to([P, T, NX])
                    for k in range(2):
                        op = v.tensor_tensor(chosen[:, k, :, :], ramp, best_f[:, :, k:k + 1].broadcast_to([P, T, NX]), ALU.is_equal)
                    chain(op, 5)
                    v.tensor_tensor(mask[:, :, :], chosen[:, 0, :, :], chosen[:, 1, :, :], ALU.add).then_inc(mask_made, 1)
                    dve.wait_ge(counted, b + 1)
                    for i in range(T):
                        chain(v.tensor_tensor(base[:, i + 1, :], base[:, i, :], c.bank[3][:, (T + i) * NX:(T + i + 1) * NX], ALU.add), 6 + i)
                    chain(v.tensor_tensor(rank[:, :, :], base[:, 0:T, :], c.bank[3][:, 0:T * NX].rearrange("p (t e) -> p t e", e=NX), ALU.add), 6 + T)
                    v.tensor_copy(base[:, 0, :], base[:, T, :])
                    for k in range(2):
                        op = v.tensor_tensor(placed[:, k, :, :], rank[:, :, :], chosen[:, k, :, :], ALU.mult)
                    chain(op, 7 + T)
                    chain(v.tensor_reduce(place_f[:, :, :].rearrange("p k t -> p (k t)"), placed[:, :, :, :].rearrange("p k t e -> p (k t) e"), AX.X, ALU.add), 8 + T)
                    dve.wait_ge(rows_gone, b + 1)
                    v.tensor_copy(place[:, p, :], place_f[:, :, :].rearrange("p k t -> p (k t)")).then_inc(place_made, 1)
                    chain(v.tensor_copy(c.places_f[:, bass.ds(b * 2 * T, 2 * T)], place_f[:, :, :].rearrange("p k t -> p (k t)")), 9 + T)
                    dve.wait_ge(e2_made, b + 1)
                    chain(v.tensor_scalar(share[:, 0, :], share[:, 1, :], 1.0, None, ALU.add), 10 + T)
                    chain(v.reciprocal(share[:, 0, :], share[:, 0, :]), 11 + T)
                    chain(v.tensor_tensor(share[:, 1, :], share[:, 1, :], share[:, 0, :], ALU.mult), 12 + T)
                    v.tensor_copy(c.shares[:, bass.ds(b * 2 * T, 2 * T)], share[:, :, :].rearrange("p k t -> p (k t)"))

                f.moments(dve, nc, 0, 0, 0)
                with dve.Fori(0, NB // 2 - 1) as pair:
                    for p in range(2):
                        work(pair * 2 + p, pair, p, True)
                for p in range(2):
                    work(NB - 2 + p, NB // 2 - 1, p, p == 0)
                v.tensor_copy(c.next_row[:, :], base[:, 0, :]).then_inc(dv, 1)
                dve.wait_ge(dv, NB * V + 1)

            @block.scalar
            def _(act):
                prime(act, f.xt_made)
                for e in range(NX):
                    nc.scalar.dma_start(up_w[:, e, 0:W1].rearrange("p (c n) -> p c n", n=FF), w["L1_ffn_W1"][e].rearrange("(c p) n -> p c n", p=P)).then_inc(experts_loaded, 16)
                    nc.scalar.dma_start(w2[:, e * FB:(e + 1) * FB, :], w["L1_ffn_W2"][e].rearrange("(k p) n -> p k n", p=P)).then_inc(experts_loaded, 16)
                    nc.scalar.dma_start(up_w[:, e, B1:], spread_row(w["L1_ffn_b2"].rearrange("e d -> (e d)")[e * D:(e + 1) * D], D)).then_inc(experts_loaded, 16)
                    nc.scalar.dma_start(up_w[:, e, W1:B1], w["L1_ffn_b1"].rearrange("e (k p) -> p e k", p=P)[:, e, :], allow_slow_non_contiguous=True).then_inc(experts_loaded, 16)
                with batches(act) as pair:
                    for p in range(2):
                        b = pair * 2 + p

                        def free():
                            act.wait_ge(rows_gone, b + 1)
                            act.sem_inc(passed_v, 1)

                        f.scalar(act, nc, c, b, p, gated, free=free)
                        act.wait_ge(gap_made, b + 1)
                        nc.scalar.activation(share[:, 1, :], gap[:, :], ACT.Exp).then_inc(e2_made, 1)
                act.wait_ge(experts_loaded, 16 * 4 * NX)

            @block.tensor
            def _(pe):
                prime(pe, gated)
                t = nc.tensor
                pe.wait_ge(w_loaded, 64)
                pe.wait_ge(set_up, 1)
                with batches(pe) as pair:
                    for p in range(2):
                        b = pair * 2 + p
                        for i in range(T + 1):
                            if i < T:
                                f.tensor(pe, nc, c, b, p, i)
                            if i >= 1:
                                pe.wait_ge(f.xt_made, 1 + b * T + i)
                                for ch in range(2):
                                    op = t.matmul(c.bank[2][:, (i - 1) * NX:i * NX], f.xt[:, i - 1, ch, :], wgate[:, ch, :], start=(ch == 0), stop=(ch == 1))
                                op.then_inc(gated, 1)
                        pe.wait_ge(mask_made, b + 1)
                        tokens = mask[:, :, :].rearrange("p t e -> p (t e)")
                        t.matmul(c.bank[3][:, 0:T * NX], before[:, :], tokens, start=True, stop=True)
                        t.matmul(c.bank[3][:, T * NX:2 * T * NX], c.ones[:, :], tokens, start=True, stop=True).then_inc(counted, 1)


def plan_tiles(nc, c):
    with ExitStack() as ctx:
        def sb(name, shape, dt=F32):
            return ctx.enter_context(nc.sbuf_tensor(f"pt_{name}", shape, dt))

        def sem(name):
            return nc.alloc_semaphore(f"pt_{name}")

        zeros = sb("zeros", [P, D])
        next_i = sb("next_i", [P, NX], I32)
        count = sb("count", [P, NX])
        tiles_i = sb("tiles_i", [P, NX], I32)
        tiles = sb("tiles", [P, NX])
        ends = sb("ends", [P, NX])
        skip = sb("skip", [P, NX])
        ramp_i = sb("ramp_i", [P, SLOTS], I32)
        slot = sb("slot", [P, SLOTS])
        last = sb("last", [P, 1])
        past = sb("past", [P, NX, SLOTS])
        two = sb("two", [P, 2, SLOTS])
        behind = sb("behind", [P, NX, 2 * NT])
        place = sb("place", [P, 2 * NT])
        dv, ramp_made, padded = sem("dv"), sem("ramp_made"), sem("padded")
        with nc.Block() as block:
            @block.gpsimd
            def _(pool):
                nc.gpsimd.iota(ramp_i[:, :], [[1, SLOTS]], base=0, channel_multiplier=0).then_inc(ramp_made, 1)

            @block.vector
            def _(dve):
                v = nc.vector
                steps = iter(range(1, 1000))

                def chain(op):
                    op.then_inc(dv, 1)
                    dve.wait_ge(dv, next(steps))

                v.memset(zeros[:, :], 0.0)
                chain(v.tensor_copy(next_i[:, :], c.next_row[:, :]))
                dve.wait_ge(ramp_made, 1)
                v.tensor_copy(slot[:, :], ramp_i[:, :])
                v.tensor_scalar(count[:, :], c.ramp_row[:, 0:NX], float(-REG), float(P - 1), ALU.mult, ALU.add).then_inc(dv, 1)
                dve.wait_ge(dv, next(steps))
                chain(v.tensor_tensor(count[:, :], count[:, :], c.next_row[:, :], ALU.add))
                chain(v.tensor_copy(tiles_i[:, :], count[:, :]))
                chain(v.tensor_scalar(tiles_i[:, :], tiles_i[:, :], 7, None, ALU.logical_shift_right))
                chain(v.tensor_copy(tiles[:, :], tiles_i[:, :]))
                chain(v.tensor_scalar(tiles[:, :], tiles[:, :], 1.0, None, ALU.max))
                v.tensor_scalar(skip[:, :], tiles[:, :], float(-P), float(REG), ALU.mult, ALU.add)
                chain(v.tensor_copy(ends[:, 0:1], tiles[:, 0:1]))
                for e in range(1, NX):
                    chain(v.tensor_tensor(ends[:, e:e + 1], ends[:, e - 1:e], tiles[:, e:e + 1], ALU.add))
                chain(v.tensor_scalar(last[:, :], ends[:, NX - 1:NX], -1.0, None, ALU.add))
                chain(v.tensor_scalar(slot[:, :], slot[:, :], last[:, 0:1], None, ALU.min))
                for e in range(NX - 1):
                    op = v.tensor_scalar(past[:, e, :], slot[:, :], ends[:, e:e + 1], None, ALU.is_ge)
                chain(v.tensor_scalar(two[:, 0, :], slot[:, :], float(P), None, ALU.mult))
                chain(v.tensor_copy(two[:, 1, :], past[:, 0, :]))
                for e in range(NX - 1):
                    op = v.scalar_tensor_tensor(two[:, 0, :], past[:, e, :], skip[:, e:e + 1], two[:, 0, :], ALU.mult, ALU.add)
                    if e:
                        op = v.tensor_tensor(two[:, 1, :], two[:, 1, :], past[:, e, :], ALU.add)
                    chain(op)
                v.tensor_copy(c.slot_row[:, :], two[0:1, 0, :])
                for e in range(NX - 1):
                    op = v.tensor_scalar(behind[:, e, :], c.places_f[:, :], float((e + 1) * REG), skip[:, e:e + 1], ALU.is_ge, ALU.mult)
                chain(op)
                for e in range(NX - 1):
                    chain(v.tensor_tensor(place[:, :], place[:, :] if e else c.places_f[:, :], behind[:, e, :], ALU.subtract))
                v.tensor_copy(c.places[:, :], place[:, :])
                chain(v.tensor_copy(c.slot_expert[:, :], two[0:1, 1, :]))

            @block.sync
            def _(sp):
                sp.wait_ge(dv, 1)
                at = nc.values_load_multi_w_load_instructions(next_i[0:1, 0:NX], engines=[mybir.EngineType.SP], min_val=0, max_val=NX * REG - P)[1]
                for e in range(NX):
                    nc.sync.dma_start(c.routed[bass.ds(at[e], P), :], zeros[:, :]).then_inc(padded, 16)
                sp.wait_ge(padded, 16 * NX)


def experts(nc, c, up_w, w2):
    with ExitStack() as ctx:
        def sb(name, shape, dt=F32):
            return ctx.enter_context(nc.sbuf_tensor(f"ex_{name}", shape, dt))

        def sem(name):
            return nc.alloc_semaphore(f"ex_{name}")

        R = 4
        now = sb("now", [P, R, UPW])
        xs = sb("xs", [P, R, D])
        xt = sb("xt", [P, 2, D])
        hid = sb("hid", [P, 2, FF])
        y = sb("y", [P, R, D])
        turned, xt_made, now_made, up, hid_made, down, y_made, passed = (sem(s) for s in (
            "turned", "xt_made", "now_made", "up", "hid_made", "down", "y_made", "passed"))
        loaded, stored = [sem(f"loaded{q}") for q in range(R)], [sem(f"stored{q}") for q in range(R)]
        rounds = SLOTS // R

        def first_rows(first, n):
            return nc.values_load_multi_w_load_instructions(c.slot_row[0:1, bass.ds(first, n)], engines=[mybir.EngineType.SP], min_val=0, max_val=NX * REG - P)[1]

        def experts_of(first, n, engine):
            return nc.values_load_multi_w_load_instructions(c.slot_expert[0:1, bass.ds(first, n)], engines=[engine], min_val=0, max_val=NX - 1)[1]

        with nc.Block() as block:
            @block.sync
            def _(sp):
                def load(row, q):
                    nc.sync.dma_start(xs[:, q, :], c.routed[bass.ds(row, P), :]).then_inc(loaded[q], 16)

                def store(tile, q):
                    sp.wait_ge(y_made, 2 + tile + 1)
                    sp.sem_inc(passed, 1)
                    nc.sync.dma_start(c.y_rows.rearrange("(s p) d -> p s d", p=P)[:, bass.ds(tile, 1), :], y[:, q:q + 1, :]).then_inc(stored[q], 16)

                for q in range(R):
                    sp.sem_inc(stored[q], 16)
                row = first_rows(0, R)
                for q in range(R):
                    load(row[q], q)
                with sp.Fori(0, rounds - 1) as turn:
                    row = first_rows((turn + 1) * R, R)
                    for q in range(R):
                        sp.wait_ge(turned, turn * R + q + 1)
                        sp.sem_inc(passed, 1)
                        load(row[q], q)
                        store(turn * R + q, q)
                for q in range(R):
                    store((rounds - 1) * R + q, q)
                for q in range(R):
                    sp.wait_ge(stored[q], 16 + 16 * rounds)

            @block.tensor
            def _(pe):
                t = nc.tensor

                def turn_tile(tile, q, turn):
                    pe.wait_ge(loaded[q], 16 * turn + 16)
                    if not (isinstance(tile, int) and tile < 2):
                        pe.wait_ge(xt_made, tile - 1)
                        pe.sem_inc(passed, 1)
                    for ch in range(2):
                        op = t.transpose(c.bank[q % 2][:, ch * P:(ch + 1) * P], xs[:, q, ch * P:(ch + 1) * P], c.ident[:, :])
                    op.then_inc(turned, 1)

                def hidden(tile, q):
                    pe.wait_ge(xt_made, tile + 1)
                    pe.wait_ge(now_made, tile + 1)
                    pe.wait_ge(hid_made, 2 + tile - 1)
                    pe.sem_inc(passed, 1)
                    for k in range(FB):
                        for ch in range(2):
                            op = t.matmul(c.bank[2 + q % 2][:, k * P:(k + 1) * P], now[:, q, ch * FF + k * P:ch * FF + (k + 1) * P], xt[:, q % 2, ch * P:(ch + 1) * P],
                                          start=(ch == 0), stop=(ch == 1))
                    op.then_inc(up, 1)

                def out_of(tile, q, expert):
                    pe.wait_ge(hid_made, 2 + tile + 1)
                    pe.wait_ge(y_made, 2 + tile - 1)
                    pe.sem_inc(passed, 1)
                    for k in range(FB):
                        op = t.matmul(c.bank[4 + q % 2][:, 0:D], hid[:, q % 2, k * P:(k + 1) * P], w2[:, bass.ds(expert * FB + k, 1), :].rearrange("p o d -> p (o d)"),
                                      start=(k == 0), stop=(k == FB - 1))
                    op.then_inc(down, 1)

                def work(turn, final):
                    expert = experts_of(turn * R, R, mybir.EngineType.PE)
                    for q in range(R):
                        tile = turn * R + q
                        if not (final and q >= R - 2):
                            turn_tile(tile + 2, (q + 2) % R, turn + (q + 2) // R)
                        if not (final and q == R - 1):
                            hidden(tile + 1, (q + 1) % R)
                        out_of(tile, q, expert[q])

                turn_tile(0, 0, 0)
                turn_tile(1, 1, 0)
                hidden(0, 0)
                with pe.Fori(0, rounds - 1) as turn:
                    work(turn, False)
                work(rounds - 1, True)

            @block.vector
            def _(dve):
                dve.sem_inc(y_made, 2)
                v = nc.vector

                def prepare(tile, q, expert):
                    dve.wait_ge(turned, tile + 1)
                    v.tensor_copy(xt[:, q % 2, :], c.bank[q % 2][:, 0:D]).then_inc(xt_made, 1)
                    if not (isinstance(tile, int) and tile < 2):
                        dve.wait_ge(y_made, 2 + tile - 4 + 1)
                        dve.sem_inc(passed, 1)
                    v.tensor_copy(now[:, q, :], up_w[:, bass.ds(expert, 1), :].rearrange("p o n -> p (o n)")).then_inc(now_made, 1)

                def finish(turn, q):
                    tile = turn * R + q
                    dve.wait_ge(stored[q], 16 + 16 * turn)
                    dve.wait_ge(down, tile + 1)
                    v.tensor_tensor(y[:, q, :], c.bank[4 + q % 2][:, 0:D], now[:, q, B1:], ALU.add).then_inc(y_made, 1)

                def work(turn, final):
                    expert = experts_of(turn * R + 2, R - 2 if final else R, mybir.EngineType.DVE)
                    for q in range(R):
                        if not (final and q >= R - 2):
                            prepare(turn * R + q + 2, (q + 2) % R, expert[q])
                        finish(turn, q)

                expert = experts_of(0, 2, mybir.EngineType.DVE)
                for q in range(2):
                    prepare(q, q, expert[q])
                with dve.Fori(0, rounds - 1) as turn:
                    work(turn, False)
                work(rounds - 1, True)

            @block.scalar
            def _(act):
                act.sem_inc(hid_made, 2)
                with act.Fori(0, rounds) as turn:
                    for q in range(R):
                        act.wait_ge(up, turn * R + q + 1)
                        for k in range(FB):
                            op = nc.scalar.activation(hid[:, q % 2, k * P:(k + 1) * P], c.bank[2 + q % 2][:, k * P:(k + 1) * P], ACT.Relu, bias=now[:, q, W1 + k:W1 + k + 1])
                        op.then_inc(hid_made, 1)


def combine(nc, c, out):
    with ExitStack() as ctx:
        def sb(name, shape, dt=F32):
            return ctx.enter_context(nc.sbuf_tensor(f"co_{name}", shape, dt))

        def sem(name):
            return nc.alloc_semaphore(f"co_{name}")

        x = sb("x", [P, 2, T, D])
        y = sb("y", [P, 2, 2 * T, D])
        place = sb("place", [P, 2, 2 * T], I32)
        loaded, gathered, stored = ([sem(f"{s}{p}") for p in range(2)] for s in ("loaded", "gathered", "stored"))
        place_ready, best_added, made, passed = sem("place_ready"), sem("best_added"), sem("made"), sem("passed")
        with nc.Block() as block:
            @block.sync
            def _(sp):
                def load(b, p):
                    nc.sync.dma_start(x[:, p, :, :], tiles_of(c.x3, b)).then_inc(loaded[p], 16)

                def store(b, p):
                    sp.wait_ge(made, b + 1)
                    sp.sem_inc(passed, 1)
                    nc.sync.dma_start(tiles_of(out, b), x[:, p, :, :]).then_inc(stored[p], 16)

                for p in range(2):
                    load(p, p)
                with sp.Fori(0, NB // 2 - 1) as pair:
                    for p in range(2):
                        store(pair * 2 + p, p)
                        sp.wait_ge(stored[p], 16 * pair + 16)
                        sp.sem_inc(passed, 1)
                        load(pair * 2 + p + 2, p)
                for p in range(2):
                    store(NB - 2 + p, p)
                for p in range(2):
                    sp.wait_ge(stored[p], 16 * (NB // 2))

            @block.gpsimd
            def _(pool):
                with batches(pool) as pair:
                    for p in range(2):
                        pool.wait_ge(place_ready, pair * 2 + p + 1)
                        pool.sem_inc(passed, 1)
                        for i in range(2 * T):
                            nc.gpsimd.indirect_dma_start(y[:, p, i, :], None, c.y_rows,
                                                         bass.IndirectOffsetOnAxis(ap=place[:, p, i:i + 1], axis=0)).then_inc(gathered[p], 16)

            @block.vector
            def _(dve):
                v = nc.vector

                def places(b, p):
                    v.tensor_copy(place[:, p, :], c.places[:, bass.ds(b * 2 * T, 2 * T)]).then_inc(place_ready, 1)

                def work(pair, p):
                    b = pair * 2 + p
                    share = c.shares[:, bass.ds(b * 2 * T, 2 * T)]
                    v.tensor_copy(share_now[:, p, :], share).then_inc(share_made, 1)
                    dve.wait_ge(share_made, b + 1)
                    dve.wait_ge(loaded[p], 16 * pair + 16)
                    dve.wait_ge(gathered[p], 16 * 2 * T * (pair + 1))
                    dve.sem_inc(passed, 1)
                    for k in range(2):
                        for i in range(T):
                            op = v.scalar_tensor_tensor(x[:, p, i, :], y[:, p, k * T + i, :], share_now[:, p, k * T + i:k * T + i + 1], x[:, p, i, :], ALU.mult, ALU.add)
                        if k == 0:
                            op.then_inc(best_added, 1)
                            dve.wait_ge(best_added, b + 1)
                            dve.sem_inc(passed, 1)
                    op.then_inc(made, 1)

                share_now = sb("share_now", [P, 2, 2 * T])
                share_made = sem("share_made")
                for p in range(2):
                    places(p, p)
                with dve.Fori(0, NB // 2 - 1) as pair:
                    for p in range(2):
                        work(pair, p)
                        places(pair * 2 + p + 2, p)
                for p in range(2):
                    work(NB // 2 - 1, p)


def program(nc, w, out):
    def dram(name, shape, dt=F32):
        return nc.dram_tensor(name, shape, dt).ap()

    with ExitStack() as ctx:
        def sb(name, shape, dt=F32):
            return ctx.enter_context(nc.sbuf_tensor(name, shape, dt))

        def sem(name):
            return nc.alloc_semaphore(name)

        c = Core()
        c.bank = [ctx.enter_context(nc.psum_tensor(f"bank{b}", [P, 512], F32)) for b in range(8)]
        c.x_in, c.x1, c.x2, c.x3 = w["x"], dram("x1", [NPAD, D]), dram("x2", [NPAD, D]), dram("x3", [NPAD, D])
        c.a_table, c.b_table = dram("a_table", [NPAD, A_ROW]), dram("b_table", [NPAD, B_ROW])
        c.swt = dram("swt", [NT, P, INNER])
        make_constants(nc, c, sb, sem)
        c.dst_score = sb("dst_score", [P, NT * HEADS])
        with nc.cleanup_on_exit():
            make_schedule(nc, c, w["src"], w["dst"], dram)
        with nc.cleanup_on_exit():
            gat_project(nc, c, w)
        with nc.sbuf_tensor("a_sums", [P, NT * A_ACC], F32) as sums:
            with nc.cleanup_on_exit():
                edge_stage(nc, c, "ea", HEADS, 0.2, c.a_table, A_ROW, A_ACC, HEADS * HC, None, sums)
            with nc.cleanup_on_exit():
                gat_finish(nc, c, w, sums)
        with nc.sbuf_tensor("w_comb", [P, INNER // P, D], F32) as w_comb:
            with nc.sbuf_tensor("pooled", [P, INNER // P, D + 1], F32) as pooled:
                with nc.cleanup_on_exit():
                    slice_tokens(nc, c, w, pooled)
                with nc.cleanup_on_exit():
                    token_attention(nc, c, w, pooled, w_comb)
            with nc.cleanup_on_exit():
                hyp_project(nc, c, w, w_comb)
        with nc.sbuf_tensor("b_sums", [P, NT * B_ACC], F32) as sums:
            with nc.cleanup_on_exit():
                edge_stage(nc, c, "eb", 1, None, c.b_table, B_ROW, B_ACC, D + 1, -1e9, sums)
            with nc.cleanup_on_exit():
                hyp_finish(nc, c, w, sums)
        up_w, w2 = sb("up_w", [P, NX, UPW]), sb("w2", [P, NX * FB, D])
        c.places = sb("places", [P, NT * 2], I32)
        c.places_f, c.shares = sb("places_f", [P, NT * 2]), sb("shares", [P, NT * 2])
        c.next_row = sb("next_row", [P, NX])
        c.slot_row, c.slot_expert = (sb(name, [1, SLOTS], I32) for name in ("slot_row", "slot_expert"))
        c.routed, c.y_rows = dram("routed", [NX * REG, D]), dram("y_rows", [SLOTS * P, D])
        with nc.cleanup_on_exit():
            route(nc, c, w, up_w, w2)
        with nc.cleanup_on_exit():
            plan_tiles(nc, c)
        with nc.cleanup_on_exit():
            experts(nc, c, up_w, w2)
        with nc.cleanup_on_exit():
            combine(nc, c, out)


_WEIGHTS = ["L0_gnn_W", "L0_gnn_att_src", "L0_gnn_att_dst", "L0_gnn_bias", "L0_gnn_Wp", "L0_gnn_bp",
            "L0_ffn_W_fx", "L0_ffn_b_fx", "L0_ffn_W_x", "L0_ffn_b_x", "L0_ffn_W_slice", "L0_ffn_b_slice",
            "L0_ffn_W_q", "L0_ffn_W_k", "L0_ffn_W_v", "L0_ffn_W_out", "L0_ffn_b_out", "L0_ffn_temperature",
            "L1_gnn_W", "L1_gnn_b", "L1_gnn_mag_w", "L1_gnn_mag_b", "L1_gnn_attn_w",
            "L1_ffn_Wg", "L1_ffn_bg", "L1_ffn_bias", "L1_ffn_W1", "L1_ffn_b1", "L1_ffn_W2", "L1_ffn_b2"]


def kernel(**inputs):
    import numpy as _np
    import concourse.bacc as _bacc
    from concourse import mybir as _mybir
    from concourse.bass_utils import run_bass_kernel_spmd as _run

    def padded(a, shape, fill):
        a = _np.asarray(a)
        out = _np.full(shape, fill, a.dtype)
        out.reshape(-1)[:a.size] = a.reshape(-1)
        return out

    arrays = {
        "x": padded(inputs["x"], (NPAD, D), 0),
        "src": padded(inputs["src"], (K, P), 0),
        "dst": padded(inputs["dst"], (K, P), NPAD - 1),
    }
    for name in _WEIGHTS:
        arrays[name] = _np.ascontiguousarray(inputs[name])
    nc = _bacc.Bacc("TRN2", target_bir_lowering=False, num_devices=1)
    w = {name: nc.dram_tensor(name, a.shape, _mybir.dt.from_np(a.dtype), kind="ExternalInput").ap() for name, a in arrays.items()}
    out = nc.dram_tensor("out", (NPAD, D), F32, kind="ExternalOutput").ap()
    program(nc, w, out)
    r = _run(nc, [arrays], core_ids=[0])
    return r.results[0]["out"][:N]
```
